# Optimizing a Trainium2 kernel written in Bass

```python
import numpy as np
import jax
import jax.numpy as jnp

def _softmax(x, axis=-1):
    return jax.nn.softmax(x, axis=axis)

def _gelu(x):
    return jax.nn.gelu(x, approximate=True)

def _silu(x):
    return jax.nn.silu(x)

def _sigmoid(x):
    return jax.nn.sigmoid(x)

def _layernorm(x, axis=-1, eps=1e-05):
    m = jnp.mean(x, axis=axis, keepdims=True)
    v = jnp.var(x, axis=axis, keepdims=True)
    return (x - m) / jnp.sqrt(v + eps)

def _scatter_add(tgt, idx, src, axis=0):
    return tgt.at[idx].add(src)

def _segment_sum(src, seg, n):
    return jax.ops.segment_sum(src, seg, n)
kernel_name = 'mk_flamingo_gated_d4_seqx_r4_87e1f9'

def setup_inputs(seed: int=0):
    np.random.seed(seed)
    _w = jnp.asarray

    def _rec_inputs():
        import jax
        import jax.numpy as jnp
        _rk = jax.random.key(seed)
        x = -0.0002928 + 1 * jax.random.normal(jax.random.fold_in(_rk, 1), (2, 1024, 256), jnp.float32)
        _lenS = 1024 - jax.random.randint(jax.random.fold_in(_rk, 7), (2,), 0, max(1, 1024 // 4) + 1, jnp.int32)
        _lenS2 = 77 - jax.random.randint(jax.random.fold_in(_rk, 8), (2,), 0, max(1, 77 // 4) + 1, jnp.int32)
        _ctx_1024P = jax.random.normal(jax.random.fold_in(_rk, 11), (2, 16, 256), jnp.float32)
        _ctx_1024c = jax.random.dirichlet(jax.random.fold_in(_rk, 511), 0.3 * jnp.ones((16,), jnp.float32), (2, 77))
        _ctx_1024t = jnp.einsum('bsk,bkd->bsd', _ctx_1024c, _ctx_1024P)
        _ctx_1024t = _ctx_1024t * jax.lax.rsqrt(jnp.mean(jnp.square(_ctx_1024t)) + 1e-12) * 0.953939
        ctx_1024 = -1.39393e-06 + 0.999914 * (_ctx_1024t + 0.3 * jax.random.normal(jax.random.fold_in(_rk, 611), (2, 77, 256), jnp.float32))
        _validS = jnp.arange(1024)[None, :] < _lenS[:, None]
        _validS2 = jnp.arange(77)[None, :] < _lenS2[:, None]
        _causal = jnp.tril(jnp.ones((1024, 1024), dtype=bool))
        mask_1x1xSxS2_ik0 = jnp.where(jnp.broadcast_to(_validS2[0:1, None, None, :], (1, 1, 1024, 77)), 0, 1).astype(jnp.int32)
        _g = jax.random.normal(jax.random.fold_in(_rk, 9001), (2, 4), jnp.float32)
        _g = jnp.sign(_g) * jnp.maximum(jnp.abs(_g), 1.0) + (_g == 0) * 1.0
        g_xattn = _g[0]
        g_ffn = _g[1]
        return (x, ctx_1024, mask_1x1xSxS2_ik0, g_xattn, g_ffn)
    x, ctx_1024, mask_1x1xSxS2_ik0, g_xattn, g_ffn = _rec_inputs()

    def _L0_xattn_setup():
        import jax, jax.numpy as jnp
        import numpy as np
        B, N, DIM, H = (2, 512, 256, 16)
        HD = DIM // H
        SCALE = HD ** (-0.5)

        def _split_heads(x):
            b, n, _ = x.shape
            return x.reshape(b, n, H, HD).transpose(0, 2, 1, 3)
        key = jax.random.key(seed)
        ks = jax.random.split(key, 11)
        std = DIM ** (-0.5)
        inp = {'q': jax.random.normal(ks[0], (B, N, DIM), jnp.float32), 'k': jax.random.normal(ks[1], (B, N, DIM), jnp.float32), 'v': jax.random.normal(ks[2], (B, N, DIM), jnp.float32), 'mask': jnp.tril(jnp.ones((N, N), jnp.int32))[None, None], 'Wq': jax.random.normal(ks[3], (DIM, DIM), jnp.float32) * std, 'bq': jnp.zeros((DIM,), jnp.float32), 'Wk': jax.random.normal(ks[4], (DIM, DIM), jnp.float32) * std, 'bk': jnp.zeros((DIM,), jnp.float32), 'Wv': jax.random.normal(ks[5], (DIM, DIM), jnp.float32) * std, 'bv': jnp.zeros((DIM,), jnp.float32), 'Wo': jax.random.normal(ks[6], (DIM, DIM), jnp.float32) * std, 'bo': jnp.zeros((DIM,), jnp.float32)}
        return inp
    _L0_xattn_all = _L0_xattn_setup()
    _L0_xattn_in = {k: v for k, v in _L0_xattn_all.items() if k in ('Wq', 'bq', 'Wk', 'bk', 'Wv', 'bv', 'Wo', 'bo')}
    del _L0_xattn_all

    def _L0_ffn_setup():
        import jax, jax.numpy as jnp
        import numpy as np
        B, S, D = (4, 1024, 256)
        E, F_EXP = (16, 512)
        F_C = 2.0
        F_SH = 512
        key = jax.random.key(seed)
        ks = jax.random.split(key, 8)
        s = 0.02
        return {'hidden_states': jax.random.normal(ks[0], (B, S, D), jnp.float32), 'gate_w': jax.random.normal(ks[1], (E, D), jnp.float32) * s, 'Wg': jax.random.normal(ks[2], (E, F_EXP, D), jnp.float32) * s, 'Wu': jax.random.normal(ks[3], (E, F_EXP, D), jnp.float32) * s, 'Wd': jax.random.normal(ks[4], (E, D, F_EXP), jnp.float32) * s, 'Ws_g': jax.random.normal(ks[5], (F_SH, D), jnp.float32) * s, 'Ws_u': jax.random.normal(ks[6], (F_SH, D), jnp.float32) * s, 'Ws_d': jax.random.normal(ks[7], (D, F_SH), jnp.float32) * s}
    _L0_ffn_all = _L0_ffn_setup()
    _L0_ffn_in = {k: v for k, v in _L0_ffn_all.items() if k in ('gate_w', 'Wg', 'Wu', 'Wd', 'Ws_g', 'Ws_u', 'Ws_d')}
    del _L0_ffn_all

    def _L1_xattn_setup():
        import jax, jax.numpy as jnp
        import numpy as np
        DIM = 256
        SCALE_DIM = 4
        QK_DIM = DIM // SCALE_DIM
        B, S = (4, 1024)
        key = jax.random.key(seed)
        ks = jax.random.split(key, 8)
        std = 1.0 / np.sqrt(DIM)
        return {'q': jax.random.normal(ks[0], (B, S, DIM), jnp.float32), 'k': jax.random.normal(ks[1], (B, S, DIM), jnp.float32), 'v': jax.random.normal(ks[2], (B, S, DIM), jnp.float32), 'Wq': jax.random.normal(ks[3], (QK_DIM, DIM), jnp.float32) * std, 'bq': jnp.zeros((QK_DIM,), jnp.float32), 'Wk': jax.random.normal(ks[4], (QK_DIM, DIM), jnp.float32) * std, 'bk': jnp.zeros((QK_DIM,), jnp.float32), 'Wv': jax.random.normal(ks[5], (DIM, DIM), jnp.float32) * std, 'bv': jnp.zeros((DIM,), jnp.float32)}
    _L1_xattn_all = _L1_xattn_setup()
    _L1_xattn_in = {k: v for k, v in _L1_xattn_all.items() if k in ('Wq', 'bq', 'Wk', 'bk', 'Wv', 'bv')}
    del _L1_xattn_all

    def _L1_ffn_setup():
        import jax, jax.numpy as jnp
        import numpy as np
        B, S, D_MODEL, D_HIDDEN = (4, 512, 256, 1024)

        def act_quant(x):
            scale = 127.0 / jnp.clip(jnp.max(jnp.abs(x), axis=-1, keepdims=True), 1e-05)
            return jnp.clip(jnp.round(x * scale), -128, 127) / scale

        def weight_quant(w):
            scale = 1.0 / jnp.clip(jnp.mean(jnp.abs(w)), 1e-05)
            return jnp.clip(jnp.round(w * scale), -1, 1) / scale

        def bit_linear(x, w):
            xq = x + jax.lax.stop_gradient(act_quant(x) - x)
            wq = w + jax.lax.stop_gradient(weight_quant(w) - w)
            return jnp.einsum('bsd,hd->bsh', xq, wq)

        def depthwise_conv1d(x_bcl, w, b):
            y = jax.lax.conv_general_dilated(x_bcl, w, window_strides=(1,), padding=[(1, 1)], dimension_numbers=('NCH', 'OIH', 'NCH'), feature_group_count=x_bcl.shape[1])
            return y + b[None, :, None]
        key = jax.random.key(seed)
        ks = jax.random.split(key, 5)
        lim1 = 1.0 / np.sqrt(D_MODEL)
        lim2 = 1.0 / np.sqrt(D_HIDDEN)
        limc = 1.0 / np.sqrt(3.0)
        return {'x': jax.random.normal(ks[0], (B, S, D_MODEL), dtype=jnp.float32), 'w1': jax.random.uniform(ks[1], (D_HIDDEN, D_MODEL), jnp.float32, -lim1, lim1), 'conv_w': jax.random.uniform(ks[2], (D_HIDDEN, 1, 3), jnp.float32, -limc, limc), 'conv_b': jax.random.uniform(ks[3], (D_HIDDEN,), jnp.float32, -limc, limc), 'w2': jax.random.uniform(ks[4], (D_MODEL, D_HIDDEN), jnp.float32, -lim2, lim2)}
    _L1_ffn_all = _L1_ffn_setup()
    _L1_ffn_in = {k: v for k, v in _L1_ffn_all.items() if k in ('w1', 'conv_w', 'conv_b', 'w2')}
    del _L1_ffn_all

    def _L2_xattn_setup():
        import jax, jax.numpy as jnp
        import numpy as np
        key = jax.random.key(seed)
        k1, k2, k3, k4 = jax.random.split(key, 4)
        B, L1, L2, D = (32, 128, 128, 256)
        ix = jax.random.normal(k1, (B, L1, D), dtype=jnp.float32)
        iother = jax.random.normal(k2, (B, L2, D), dtype=jnp.float32)
        scale = 1.0 / np.sqrt(D)
        W = jax.random.uniform(k3, (D, D), dtype=jnp.float32, minval=-scale, maxval=scale)
        b = jax.random.uniform(k4, (D,), dtype=jnp.float32, minval=-scale, maxval=scale)
        return {'ix': ix, 'iother': iother, 'W': W, 'b': b}
    _L2_xattn_all = _L2_xattn_setup()
    _L2_xattn_in = {k: v for k, v in _L2_xattn_all.items() if k in ('W', 'b')}
    del _L2_xattn_all

    def _L2_ffn_setup():
        import jax, jax.numpy as jnp
        import numpy as np
        EPS = 1e-08

        def _ternary_linear(x, w):
            alpha = jnp.mean(jnp.abs(w))
            w_t = jnp.sign(w) * (jnp.abs(w) > 0.5 * alpha).astype(w.dtype)
            w_q = w + jax.lax.stop_gradient(w_t - w)
            d = x.shape[-1]
            rms = jnp.sqrt(jnp.sum(x * x, axis=-1, keepdims=True)) / jnp.sqrt(jnp.asarray(d, x.dtype))
            x_norm = x / (rms + EPS)
            return jnp.einsum('bsd,fd->bsf', x_norm, w_q)
        key = jax.random.key(seed)
        k1, k2, k3 = jax.random.split(key, 3)
        d_model, d_ff = (256, 1024)
        B, S = (4, 1024)
        x = jax.random.normal(k1, (B, S, d_model), dtype=jnp.float32)
        w_up = jax.random.normal(k2, (d_ff, d_model), dtype=jnp.float32) * 0.02
        w_down = jax.random.normal(k3, (d_model, d_ff), dtype=jnp.float32) * 0.02
        return {'x': x, 'w_up': w_up, 'w_down': w_down}
    _L2_ffn_all = _L2_ffn_setup()
    _L2_ffn_in = {k: v for k, v in _L2_ffn_all.items() if k in ('w_up', 'w_down')}
    del _L2_ffn_all

    def _L3_xattn_setup():
        import jax, jax.numpy as jnp
        import numpy as np
        D_MODEL = 256
        H = 16
        D_K = D_MODEL // H
        key = jax.random.key(seed)
        ks = jax.random.split(key, 7)
        B, S = (4, 512)
        q = jax.random.normal(ks[0], (B, S, D_MODEL), dtype=jnp.float32)
        k = jax.random.normal(ks[1], (B, S, D_MODEL), dtype=jnp.float32)
        v = jax.random.normal(ks[2], (B, S, D_MODEL), dtype=jnp.float32)
        scale = 1.0 / np.sqrt(D_MODEL)
        w_q = jax.random.normal(ks[3], (D_MODEL, D_MODEL), dtype=jnp.float32) * scale
        w_k = jax.random.normal(ks[4], (D_MODEL, D_MODEL), dtype=jnp.float32) * scale
        w_v = jax.random.normal(ks[5], (D_MODEL, D_MODEL), dtype=jnp.float32) * scale
        w_o = jax.random.normal(ks[6], (D_MODEL, D_MODEL), dtype=jnp.float32) * scale
        return {'q': q, 'k': k, 'v': v, 'w_q': w_q, 'w_k': w_k, 'w_v': w_v, 'w_o': w_o}
    _L3_xattn_all = _L3_xattn_setup()
    _L3_xattn_in = {k: v for k, v in _L3_xattn_all.items() if k in ('w_q', 'w_k', 'w_v', 'w_o')}
    del _L3_xattn_all

    def _L3_ffn_setup():
        import jax, jax.numpy as jnp
        import numpy as np
        TOP_K = 2
        key = jax.random.key(seed)
        k0, k1, k2, k3, k4 = jax.random.split(key, 5)
        B, S, H, I, E = (1, 1024, 256, 512, 8)
        hidden_states = jax.random.normal(k0, (B, S, H), dtype=jnp.float32)
        wg = jax.random.normal(k1, (E, H), dtype=jnp.float32) * 0.02
        w1 = jax.random.normal(k2, (E, I, H), dtype=jnp.float32) * 0.02
        w3 = jax.random.normal(k3, (E, I, H), dtype=jnp.float32) * 0.02
        w2 = jax.random.normal(k4, (E, H, I), dtype=jnp.float32) * 0.02
        return {'hidden_states': hidden_states, 'wg': wg, 'w1': w1, 'w3': w3, 'w2': w2}
    _L3_ffn_all = _L3_ffn_setup()
    _L3_ffn_in = {k: v for k, v in _L3_ffn_all.items() if k in ('wg', 'w1', 'w3', 'w2')}
    del _L3_ffn_all
    return {'x': x, 'ctx_1024': ctx_1024, 'mask_1x1xSxS2_ik0': mask_1x1xSxS2_ik0, 'g_xattn': g_xattn, 'g_ffn': g_ffn, 'L0_xattn_Wq': _L0_xattn_in['Wq'], 'L0_xattn_bq': _L0_xattn_in['bq'], 'L0_xattn_Wk': _L0_xattn_in['Wk'], 'L0_xattn_bk': _L0_xattn_in['bk'], 'L0_xattn_Wv': _L0_xattn_in['Wv'], 'L0_xattn_bv': _L0_xattn_in['bv'], 'L0_xattn_Wo': _L0_xattn_in['Wo'], 'L0_xattn_bo': _L0_xattn_in['bo'], 'L0_ffn_gate_w': _L0_ffn_in['gate_w'], 'L0_ffn_Wg': _L0_ffn_in['Wg'], 'L0_ffn_Wu': _L0_ffn_in['Wu'], 'L0_ffn_Wd': _L0_ffn_in['Wd'], 'L0_ffn_Ws_g': _L0_ffn_in['Ws_g'], 'L0_ffn_Ws_u': _L0_ffn_in['Ws_u'], 'L0_ffn_Ws_d': _L0_ffn_in['Ws_d'], 'L1_xattn_Wq': _L1_xattn_in['Wq'], 'L1_xattn_bq': _L1_xattn_in['bq'], 'L1_xattn_Wk': _L1_xattn_in['Wk'], 'L1_xattn_bk': _L1_xattn_in['bk'], 'L1_xattn_Wv': _L1_xattn_in['Wv'], 'L1_xattn_bv': _L1_xattn_in['bv'], 'L1_ffn_w1': _L1_ffn_in['w1'], 'L1_ffn_conv_w': _L1_ffn_in['conv_w'], 'L1_ffn_conv_b': _L1_ffn_in['conv_b'], 'L1_ffn_w2': _L1_ffn_in['w2'], 'L2_xattn_W': _L2_xattn_in['W'], 'L2_xattn_b': _L2_xattn_in['b'], 'L2_ffn_w_up': _L2_ffn_in['w_up'], 'L2_ffn_w_down': _L2_ffn_in['w_down'], 'L3_xattn_w_q': _L3_xattn_in['w_q'], 'L3_xattn_w_k': _L3_xattn_in['w_k'], 'L3_xattn_w_v': _L3_xattn_in['w_v'], 'L3_xattn_w_o': _L3_xattn_in['w_o'], 'L3_ffn_wg': _L3_ffn_in['wg'], 'L3_ffn_w1': _L3_ffn_in['w1'], 'L3_ffn_w3': _L3_ffn_in['w3'], 'L3_ffn_w2': _L3_ffn_in['w2']}

def reference(x, ctx_1024, mask_1x1xSxS2_ik0, g_xattn, g_ffn, L0_xattn_Wq, L0_xattn_bq, L0_xattn_Wk, L0_xattn_bk, L0_xattn_Wv, L0_xattn_bv, L0_xattn_Wo, L0_xattn_bo, L0_ffn_gate_w, L0_ffn_Wg, L0_ffn_Wu, L0_ffn_Wd, L0_ffn_Ws_g, L0_ffn_Ws_u, L0_ffn_Ws_d, L1_xattn_Wq, L1_xattn_bq, L1_xattn_Wk, L1_xattn_bk, L1_xattn_Wv, L1_xattn_bv, L1_ffn_w1, L1_ffn_conv_w, L1_ffn_conv_b, L1_ffn_w2, L2_xattn_W, L2_xattn_b, L2_ffn_w_up, L2_ffn_w_down, L3_xattn_w_q, L3_xattn_w_k, L3_xattn_w_v, L3_xattn_w_o, L3_ffn_wg, L3_ffn_w1, L3_ffn_w3, L3_ffn_w2):
    import jax
    import jax.numpy as jnp

    def _L0_xattn_ref(q, k, v, mask, Wq, bq, Wk, bk, Wv, bv, Wo, bo):
        import jax, jax.numpy as jnp
        import numpy as np
        B, N, DIM, H = (2, 512, 256, 16)
        HD = DIM // H
        SCALE = HD ** (-0.5)

        def _split_heads(x):
            b, n, _ = x.shape
            return x.reshape(b, n, H, HD).transpose(0, 2, 1, 3)
        qh = _split_heads(q @ Wq.T + bq)
        kh = _split_heads(k @ Wk.T + bk)
        vh = _split_heads(v @ Wv.T + bv)
        attn = jnp.einsum('bhqc,bhkc->bhqk', qh, kh) * SCALE
        attn = jnp.where(mask == 0, -jnp.inf, attn)
        attn = jax.nn.softmax(attn, axis=-1)
        out = jnp.einsum('bhqk,bhkc->bhqc', attn, vh)
        b, h, n, c = out.shape
        out = out.transpose(0, 2, 1, 3).reshape(b, n, h * c)
        return out @ Wo.T + bo

    def _L0_ffn_ref(hidden_states, gate_w, Wg, Wu, Wd, Ws_g, Ws_u, Ws_d):
        import jax, jax.numpy as jnp
        import numpy as np
        B, S, D = (4, 1024, 256)
        E, F_EXP = (16, 512)
        F_C = 2.0
        F_SH = 512
        b, s, d = hidden_states.shape
        e = gate_w.shape[0]
        cap = int(s * F_C / e)
        logits = jnp.einsum('bsd,ed->bse', hidden_states, gate_w)
        scores = jax.nn.softmax(logits, axis=-1).transpose(0, 2, 1)
        topk_w, topk_idx = jax.lax.top_k(scores, cap)
        x_tok = jnp.take_along_axis(hidden_states[:, None, :, :], topk_idx[..., None], axis=2)
        g = jnp.einsum('becd,efd->becf', x_tok, Wg)
        u = jnp.einsum('becd,efd->becf', x_tok, Wu)
        h = jax.nn.gelu(g, approximate=False) * u
        eo = jnp.einsum('becf,edf->becd', h, Wd) * topk_w[..., None]
        offs = (jnp.arange(b) * s)[:, None, None]
        flat_idx = (topk_idx + offs).reshape(-1)
        flat = jnp.zeros((b * s, d), hidden_states.dtype)
        flat = flat.at[flat_idx].add(eo.reshape(-1, d))
        out = flat.reshape(b, s, d)
        gs = jnp.einsum('bsd,fd->bsf', hidden_states, Ws_g)
        us = jnp.einsum('bsd,fd->bsf', hidden_states, Ws_u)
        shared = jnp.einsum('bsf,df->bsd', jax.nn.gelu(gs, approximate=False) * us, Ws_d)
        return out + shared

    def _L1_xattn_ref(q, k, v, Wq, bq, Wk, bk, Wv, bv):
        import jax, jax.numpy as jnp
        import numpy as np
        DIM = 256
        SCALE_DIM = 4
        QK_DIM = DIM // SCALE_DIM
        B, S = (4, 1024)
        scale = jnp.asarray(np.sqrt(QK_DIM), q.dtype)
        qp = jnp.einsum('bsd,ed->bse', q, Wq) + bq
        kp = jnp.einsum('bsd,ed->bse', k, Wk) + bk
        vp = jnp.einsum('bsd,ed->bse', v, Wv) + bv
        z = jnp.einsum('bqe,bke->bqk', qp, kp)
        z = jax.nn.sigmoid(z / scale)
        return jnp.einsum('bqk,bkd->bqd', z, vp)

    def _L1_ffn_ref(x, w1, conv_w, conv_b, w2):
        import jax, jax.numpy as jnp
        import numpy as np
        B, S, D_MODEL, D_HIDDEN = (4, 512, 256, 1024)

        def act_quant(x):
            scale = 127.0 / jnp.clip(jnp.max(jnp.abs(x), axis=-1, keepdims=True), 1e-05)
            return jnp.clip(jnp.round(x * scale), -128, 127) / scale

        def weight_quant(w):
            scale = 1.0 / jnp.clip(jnp.mean(jnp.abs(w)), 1e-05)
            return jnp.clip(jnp.round(w * scale), -1, 1) / scale

        def bit_linear(x, w):
            xq = x + jax.lax.stop_gradient(act_quant(x) - x)
            wq = w + jax.lax.stop_gradient(weight_quant(w) - w)
            return jnp.einsum('bsd,hd->bsh', xq, wq)

        def depthwise_conv1d(x_bcl, w, b):
            y = jax.lax.conv_general_dilated(x_bcl, w, window_strides=(1,), padding=[(1, 1)], dimension_numbers=('NCH', 'OIH', 'NCH'), feature_group_count=x_bcl.shape[1])
            return y + b[None, :, None]
        h = bit_linear(x, w1)
        h = depthwise_conv1d(h.transpose(0, 2, 1), conv_w, conv_b)
        h = h.transpose(0, 2, 1)
        h = jax.nn.silu(h)
        return bit_linear(h, w2)

    def _L2_xattn_ref(ix, iother, W, b):
        import jax, jax.numpy as jnp
        import numpy as np
        ex = jnp.einsum('bld,ed->ble', ix, W) + b
        eother = jnp.einsum('bld,ed->ble', iother, W) + b
        scores = jnp.einsum('bld,bmd->blm', ex, eother)
        attn = jax.nn.softmax(scores, axis=-1)
        aligned = jnp.einsum('blm,bmd->bld', attn, iother)
        return aligned

    def _L2_ffn_ref(x, w_up, w_down):
        import jax, jax.numpy as jnp
        import numpy as np
        EPS = 1e-08

        def _ternary_linear(x, w):
            alpha = jnp.mean(jnp.abs(w))
            w_t = jnp.sign(w) * (jnp.abs(w) > 0.5 * alpha).astype(w.dtype)
            w_q = w + jax.lax.stop_gradient(w_t - w)
            d = x.shape[-1]
            rms = jnp.sqrt(jnp.sum(x * x, axis=-1, keepdims=True)) / jnp.sqrt(jnp.asarray(d, x.dtype))
            x_norm = x / (rms + EPS)
            return jnp.einsum('bsd,fd->bsf', x_norm, w_q)
        h = jax.nn.gelu(_ternary_linear(x, w_up), approximate=False)
        return _ternary_linear(h, w_down)

    def _L3_xattn_ref(q, k, v, w_q, w_k, w_v, w_o):
        import jax, jax.numpy as jnp
        import numpy as np
        D_MODEL = 256
        H = 16
        D_K = D_MODEL // H
        B, S, _ = q.shape

        def proj(x, w):
            y = jnp.einsum('bsd,ed->bse', x, w)
            return y.reshape(B, -1, H, D_K).transpose(0, 2, 1, 3)
        query = proj(q, w_q)
        key_ = proj(k, w_k)
        value = proj(v, w_v)
        scores = jnp.einsum('bhqd,bhkd->bhqk', query, key_) / jnp.sqrt(jnp.float32(D_K))
        attn = jax.nn.softmax(scores, axis=-1)
        x = jnp.einsum('bhqk,bhkd->bhqd', attn, value)
        x = x.transpose(0, 2, 1, 3).reshape(B, S, H * D_K)
        return jnp.einsum('bsd,ed->bse', x, w_o)

    def _L3_ffn_ref(hidden_states, wg, w1, w3, w2):
        import jax, jax.numpy as jnp
        import numpy as np
        TOP_K = 2
        orig_shape = hidden_states.shape
        H = orig_shape[-1]
        E = wg.shape[0]
        x = hidden_states.reshape(-1, H)
        router_logits = x @ wg.T
        probs = jax.nn.softmax(router_logits, axis=-1)
        topk_w, topk_idx = jax.lax.top_k(probs, TOP_K)
        topk_w = topk_w / jnp.sum(topk_w, axis=-1, keepdims=True)
        expert_w = jnp.sum(jax.nn.one_hot(topk_idx, E, dtype=x.dtype) * topk_w[..., None], axis=1)
        h1 = jnp.einsum('th,eih->tei', x, w1)
        h3 = jnp.einsum('th,eih->tei', x, w3)
        y = jnp.einsum('tei,ehi->teh', jax.nn.silu(h1) * h3, w2)
        out = jnp.einsum('te,teh->th', expert_w, y)
        return out.reshape(orig_shape)
    x = x + jnp.tanh(g_xattn[0]) * _L0_xattn_ref(_layernorm(x, axis=-1), ctx_1024, ctx_1024, mask_1x1xSxS2_ik0, L0_xattn_Wq, L0_xattn_bq, L0_xattn_Wk, L0_xattn_bk, L0_xattn_Wv, L0_xattn_bv, L0_xattn_Wo, L0_xattn_bo)
    x = x + jnp.tanh(g_ffn[0]) * _L0_ffn_ref(_layernorm(x, axis=-1), L0_ffn_gate_w, L0_ffn_Wg, L0_ffn_Wu, L0_ffn_Wd, L0_ffn_Ws_g, L0_ffn_Ws_u, L0_ffn_Ws_d)
    x = x + jnp.tanh(g_xattn[1]) * _L1_xattn_ref(_layernorm(x, axis=-1), ctx_1024, ctx_1024, L1_xattn_Wq, L1_xattn_bq, L1_xattn_Wk, L1_xattn_bk, L1_xattn_Wv, L1_xattn_bv)
    x = x + jnp.tanh(g_ffn[1]) * _L1_ffn_ref(_layernorm(x, axis=-1), L1_ffn_w1, L1_ffn_conv_w, L1_ffn_conv_b, L1_ffn_w2)
    x = x + jnp.tanh(g_xattn[2]) * _L2_xattn_ref(_layernorm(x, axis=-1), ctx_1024, L2_xattn_W, L2_xattn_b)
    x = x + jnp.tanh(g_ffn[2]) * _L2_ffn_ref(_layernorm(x, axis=-1), L2_ffn_w_up, L2_ffn_w_down)
    x = x + jnp.tanh(g_xattn[3]) * _L3_xattn_ref(_layernorm(x, axis=-1), ctx_1024, ctx_1024, L3_xattn_w_q, L3_xattn_w_k, L3_xattn_w_v, L3_xattn_w_o)
    x = x + jnp.tanh(g_ffn[3]) * _L3_ffn_ref(_layernorm(x, axis=-1), L3_ffn_wg, L3_ffn_w1, L3_ffn_w3, L3_ffn_w2)
    return x

_drawn_inputs = setup_inputs


def setup_inputs(seed=0):
    import zlib

    import numpy as np

    out = dict(_drawn_inputs(seed))
    spreads = {'L0_xattn_bq': (0.0, 0.8),
     'L0_xattn_bk': (0.0, 2.0),
     'L0_xattn_bv': (0.0, 0.535),
     'L0_xattn_bo': (0.0, 0.631),
     'L1_xattn_bq': (0.0, 0.527),
     'L1_xattn_bk': (0.0, 0.1),
     'L1_xattn_bv': (0.0, 0.1)}
    factors = {'g_ffn': 8.0,
     'L0_ffn_gate_w': 8.0,
     'L0_ffn_Wg': 8.0,
     'L0_ffn_Wu': 8.0,
     'L0_ffn_Wd': 8.0,
     'L0_ffn_Ws_g': 8.0,
     'L0_ffn_Ws_u': 8.0,
     'L0_ffn_Ws_d': 8.0,
     'L1_ffn_w1': 8.0,
     'L1_ffn_conv_w': 8.0,
     'L1_ffn_conv_b': 8.0,
     'L1_ffn_w2': 8.0,
     'L2_xattn_b': 99.403,
     'L3_xattn_w_q': 8.0,
     'L3_xattn_w_k': 8.0,
     'L3_xattn_w_v': 3.837,
     'L3_xattn_w_o': 3.923,
     'L3_ffn_wg': 8.0,
     'L3_ffn_w1': 8.0,
     'L3_ffn_w3': 8.0,
     'L3_ffn_w2': 8.0,
     'L2_xattn_W': 2.741}
    for name, (base, spread) in spreads.items():
        noise = np.random.default_rng([zlib.crc32(name.encode()), seed]).standard_normal(out[name].shape)
        drawn = base * np.exp(spread * noise) if base else spread * noise
        out[name] = jnp.asarray(drawn.astype(out[name].dtype))
    for name, factor in factors.items():
        out[name] = (out[name] * factor).astype(out[name].dtype)
    return out
```

```python
from contextlib import ExitStack

import numpy as np

import concourse.bass as bass
from concourse import mybir

F32 = mybir.dt.float32
F32R = mybir.dt.float32r
BF16 = mybir.dt.bfloat16
I32 = mybir.dt.int32
U32 = mybir.dt.uint32
ALU = mybir.AluOpType
ACT = mybir.ActivationFunctionType
AX = mybir.AxisListType

P = 128
B, S, D = 2, 1024, 256
NT = B * S // P
TB = S // P
KT = D // P
L = 77
H, HD = 16, 16
LN_EPS = 1e-5
MAGIC = 1.5 * 2.0 ** 23

_STAGES = tuple(range(8))


_used = {}
_made = []


class Steps:

    def __init__(self, sem, base=0):
        self.sem, self.base, self.n = sem, base, 0

    def did(self, ins):
        self.n += 1
        return ins.then_inc(self.sem, 1)

    def last(self):
        return self.base + self.n


class Core:
    pass


def sbuf(nc, ctx, name, shape, dt=F32):
    _used[name] = _used.get(name, 0) + 1
    name = f"{name}_{_used[name]}"
    return ctx.enter_context(nc.sbuf_tensor(name, shape, dt))


def semaphores(nc, ctx, prefix, names):
    made = [ctx.enter_context(nc.semaphore(prefix + n)) for n in names.split()]
    _made.extend(made)
    return made


def software_dma_semaphores(nc, ctx, prefix, names):
    return [ctx.enter_context(nc.semaphore(prefix + n)) for n in names.split()]


def clear_semaphores(nc):
    with nc.Block() as block:
        @block.gpsimd
        def _(pool):
            for sem in _made:
                pool.sem_clear(sem)
    _made.clear()


def load_and_constants(nc, ctx, K, ins):
    K.ps = ctx.enter_context(nc.psum_tensor("ps", [P, 8, 512], F32))
    K.x = sbuf(nc, ctx, "x_sb", [P, NT, D])
    K.xn = sbuf(nc, ctx, "xn_sb", [P, NT, D])
    K.ident = sbuf(nc, ctx, "ident", [P, P])
    K.identb = sbuf(nc, ctx, "identb", [P, P], BF16)
    K.zeros = sbuf(nc, ctx, "zeros", [P, D])
    K.ones = sbuf(nc, ctx, "ones", [P, P])
    K.shift = sbuf(nc, ctx, "shift", [P, 336])
    K.headmask = sbuf(nc, ctx, "headmask", [P, 8])
    K.npow = sbuf(nc, ctx, "npow", [P, NT])
    K.hpow = sbuf(nc, ctx, "hpow", [P, NT])
    K.gate = sbuf(nc, ctx, "gates", [P, 2, 4])
    K.ctx_nat = sbuf(nc, ctx, "ctx_nat", [L, B, D])
    K.ctxT = sbuf(nc, ctx, "ctxT", [P, KT, B * L])
    K.st = sbuf(nc, ctx, "bn_st", [P, NT, 6])
    K.nv = sbuf(nc, ctx, "norm_vec", [P, 10, NT])
    K.rg = [sbuf(nc, ctx, f"row_gather{i}", [P, 2, 1], I32) for i in range(2)]
    s_const, s_ctx, s_tr, s_dve = semaphores(nc, ctx, "load_", "const ctx tr dve")
    with nc.Block() as block:
        @block.sync
        def _(sp):
            sp.dma_start(K.ctx_nat[:, :, :], ins["ctx_1024"].rearrange("b k d -> k b d")).then_inc(s_ctx, 16)
            sp.dma_start(K.gate[:, :, :], ins["gates"].partition_broadcast(P)).then_inc(s_ctx, 16)
            sp.dma_start(K.x[:, :, :], ins["x"].rearrange("b (t p) d -> p (b t) d", p=P)).then_inc(s_ctx, 16)
            sp.wait_ge(s_ctx, 48)

        @block.gpsimd
        def _(pool):
            pool.memset(K.ident[:, :], 0.0).then_inc(s_const, 1)
            pool.memset(K.shift[:, :], 0.0).then_inc(s_const, 1)
            pool.memset(K.headmask[:, :], HD ** -0.5).then_inc(s_const, 1)
            pool.memset(K.ones[:, :], 1.0).then_inc(s_const, 1)
            pool.memset(K.npow[:, :], -0.5).then_inc(s_const, 1)
            pool.memset(K.hpow[:, :], 0.5).then_inc(s_const, 1)
            pool.memset(K.zeros[:, :], 0.0).then_inc(s_const, 1)
            pool.wait_ge(s_const, 7)
            pool.affine_select(out=K.ident[:, :], in_=K.ident[:, :], compare_op=ALU.not_equal, fill=1.0, base=0,
                               pattern=[[-1, P]], channel_multiplier=1).then_inc(s_const, 1)
            pool.affine_select(out=K.shift[:, :], in_=K.shift[:, :], compare_op=ALU.not_equal, fill=1.0, base=P,
                               pattern=[[-1, 336]], channel_multiplier=1).then_inc(s_const, 1)
            pool.affine_select(out=K.headmask[:, :], in_=K.headmask[:, :], compare_op=ALU.is_ge, fill=0.0, base=0,
                               pattern=[[-HD, 8]], channel_multiplier=1).then_inc(s_const, 1)
            pool.wait_ge(s_const, 10)
            pool.affine_select(out=K.headmask[:, :], in_=K.headmask[:, :], compare_op=ALU.is_ge, fill=0.0,
                               base=HD - 1, pattern=[[HD, 8]], channel_multiplier=-1).then_inc(s_const, 1)

        @block.tensor
        def _(pe):
            pe.wait_ge(s_const, 8)
            pe.wait_ge(s_ctx, 48)
            for b in range(B):
                for k in range(KT):
                    m = pe.transpose(K.ps[:, 0, (k * B + b) * L:(k * B + b + 1) * L],
                                     K.ctx_nat[:, b, k * P:(k + 1) * P], K.ident[0:L, 0:L])
            m.then_inc(s_tr, 1)

        @block.scalar
        def _(act):
            act.wait_ge(s_ctx, 48)
            act.activation(K.gate[:, :, :], K.gate[:, :, :], ACT.Tanh).then_inc(s_dve, 1)

        @block.vector
        def _(dve):
            dve.wait_ge(s_const, 8)
            dve.tensor_copy(K.identb[:, :], K.ident[:, :]).then_inc(s_dve, 1)
            dve.wait_ge(s_tr, 1)
            dve.tensor_copy(K.ctxT[:, :, :].rearrange("p k c -> p (k c)"), K.ps[:, 0, 0:KT * B * L]).then_inc(s_dve, 1)


class Weights:

    def __init__(self, nc, ctx, ins):
        self.nc, self.ctx, self.ins, self.loads = nc, ctx, ins, []

    def add(self, name, shape, src):
        t = sbuf(self.nc, self.ctx, "w_" + name, shape)
        self.loads.append((t[tuple([slice(None)] * len(shape))], src))
        return t

    def rows(self, name):
        src = self.ins[name].rearrange("(k p) o -> p k o", p=P)
        return self.add(name, list(src.shape), src)

    def experts(self, name):
        src = self.ins[name].rearrange("e (k p) o -> p e k o", p=P)
        t = sbuf(self.nc, self.ctx, "w_" + name, list(src.shape))
        for e in range(src.shape[1]):
            self.loads.append((t[:, e, :, :], src[:, e, :, :]))
        return t

    def same(self, name):
        return self.add(name, list(self.ins[name].shape), self.ins[name])

    def repeated(self, name, n=P):
        return self.add(name, [n, self.ins[name].shape[0]], self.ins[name].partition_broadcast(n))


def norm_block(nc, ctx, K, tag, loads, ternary=False, transposed=True, to_dram=None):
    with ExitStack() as c:
        s_stat, s_vec, s_pow, s_xn, s_tr, s_out = semaphores(nc, ctx, tag, "stat vec pow xn tr out")
        (s_w,) = semaphores(nc, c, tag, "weights")
        nv = K.nv
        with nc.Block() as block:
            @block.vector
            def _(dve):
                with dve.Fori(0, NT) as t:
                    dve.bn_stats(K.st[:, t, :], K.x[:, t, :]).then_inc(s_stat, 1)
                dve.wait_ge(s_stat, NT)
                v = Steps(s_vec)
                st = K.st
                v.did(dve.tensor_tensor(nv[:, 0, :], st[:, :, 1], st[:, :, 4], ALU.add))
                v.did(dve.tensor_tensor(nv[:, 1, :], st[:, :, 1], st[:, :, 4], ALU.subtract))
                v.did(dve.tensor_tensor(nv[:, 2, :], st[:, :, 2], st[:, :, 5], ALU.add))
                dve.wait_ge(s_vec, v.last())
                v.did(dve.tensor_scalar(nv[:, 3, :], nv[:, 0, :], 0.5, None, ALU.mult))
                v.did(dve.tensor_tensor(nv[:, 4, :], nv[:, 1, :], nv[:, 1, :], ALU.mult))
                dve.wait_ge(s_vec, v.last())
                v.did(dve.scalar_tensor_tensor(nv[:, 5, :], nv[:, 4, :], D / 4.0, nv[:, 2, :], ALU.mult, ALU.add))
                dve.wait_ge(s_vec, v.last())
                v.did(dve.tensor_scalar(nv[:, 6, :], nv[:, 5, :], 1.0 / D, LN_EPS, ALU.mult, ALU.add))
                dve.wait_ge(s_pow, 1)
                scale = nv[:, 7, :]
                if ternary:
                    v.did(dve.tensor_scalar(nv[:, 8, :], nv[:, 5, :], 1.0 / D, None, ALU.mult))
                    v.did(dve.tensor_tensor(nv[:, 0, :], nv[:, 7, :], nv[:, 7, :], ALU.mult))
                    dve.wait_ge(s_vec, v.last())
                    v.did(dve.tensor_tensor(nv[:, 8, :], nv[:, 8, :], nv[:, 0, :], ALU.mult))
                    dve.wait_ge(s_pow, 2)
                    v.did(dve.tensor_scalar(nv[:, 0, :], nv[:, 9, :], 1e-8, None, ALU.add))
                    dve.wait_ge(s_vec, v.last())
                    v.did(dve.reciprocal(nv[:, 1, :], nv[:, 0, :]))
                    dve.wait_ge(s_vec, v.last())
                    v.did(dve.tensor_tensor(nv[:, 8, :], nv[:, 1, :], nv[:, 7, :], ALU.mult))
                    dve.wait_ge(s_vec, v.last())
                    scale = nv[:, 8, :]
                with dve.Fori(0, NT) as t:
                    dve.tensor_scalar(K.xn[:, t, :], K.x[:, t, :], nv[:, 3, bass.ds(t, 1)], scale[:, bass.ds(t, 1)],
                                      ALU.subtract, ALU.mult).then_inc(s_xn, 1)

            @block.gpsimd
            def _(pool):
                pool.wait_ge(s_vec, 7)
                pool.tensor_tensor(nv[:, 7, :], nv[:, 6, :], K.npow[:, :], ALU.pow).then_inc(s_pow, 1)
                if ternary:
                    pool.wait_ge(s_vec, 10)
                    pool.tensor_tensor(nv[:, 9, :], nv[:, 8, :], K.hpow[:, :], ALU.pow).then_inc(s_pow, 1)

            @block.sync
            def _(sp):
                for dst, src in loads:
                    sp.dma_start(dst, src).then_inc(s_w, 16)
                if to_dram is not None:
                    for q in range(4):
                        sp.wait_ge(s_xn, 4 * (q + 1))
                        sp.dma_start(to_dram[q * 512:(q + 1) * 512, :].rearrange("(t p) d -> p t d", p=P),
                                     K.xn[:, 4 * q:4 * q + 4, :]).then_inc(s_out, 16)
                    sp.wait_ge(s_out, 64)
                sp.wait_ge(s_w, 16 * len(loads))

            if transposed:
                @block.tensor
                def _(pe):
                    for t in range(NT):
                        pe.wait_ge(s_xn, t + 1)
                        for k in range(KT):
                            m = pe.transpose(K.ps[:, t // 2, (2 * k + t % 2) * P:(2 * k + t % 2 + 1) * P],
                                             K.xn[:, t, k * P:(k + 1) * P], K.ident[:, :])
                        if t % 2:
                            m.then_inc(s_tr, 1)

                @block.scalar
                def _(act):
                    for u in range(NT // 2):
                        act.wait_ge(s_tr, u + 1)
                        act.activation(K.xnT[:, :, 2 * u * P:(2 * u + 2) * P],
                                       K.ps[:, u, :].rearrange("p (k c) -> p k c", k=KT), ACT.Copy)


def multihead(nc, ctx, K, tag, layer, wq, wk, wv, wo, bq=None, bk=None, bv=None, bo=None, mask=None):
    NC = -(-H * L // P)
    HV = HD + 1
    heads = [sorted({r // L for r in range(c * P, min((c + 1) * P, H * L))}) for c in range(NC)]
    rows = [min(P, H * L - c * P) for c in range(NC)]
    G4 = 4 * L
    rounds = [(0, 4), (4, 8), (8, NC)]
    ps = K.ps
    with ExitStack() as c:
        kT = sbuf(nc, c, tag + "kT", [P, KT, B * L])
        kblk = sbuf(nc, c, tag + "kblk", [P, B, KT, 8 * L])
        vaug = sbuf(nc, c, tag + "vaug", [L, B, H, HV])
        vblk = sbuf(nc, c, tag + "vblk", [P, B, NC * 3 * HV])
        qT = sbuf(nc, c, tag + "qT", [P, KT, S])
        sm = sbuf(nc, c, tag + "sm", [P, 2, H * L])
        pr = sbuf(nc, c, tag + "pr", [P, 2, H * L])
        pT = sbuf(nc, c, tag + "pT", [P, 2, NC, P])
        mx = sbuf(nc, c, tag + "mx", [P, 2, H])
        rden = sbuf(nc, c, tag + "rden", [P, 2, H])
        on = sbuf(nc, c, tag + "on", [P, 2, D])
        oT = sbuf(nc, c, tag + "oT", [P, D])
        gbo = sbuf(nc, c, tag + "gbo", [P, D])
        if mask is not None:
            mi = sbuf(nc, c, tag + "mi", [P, TB, L], I32)
            mf = sbuf(nc, c, tag + "mf", [P, TB, L])
        (s_mask, s_kv, s_set, s_vb, s_vc, q_ps, q_sb, s_ready, s_used, sh_step, mx_ready, p_in, p_ready, pt_ps, pt_sb,
         o_ready, n_step, o_used, on_ready, oT_ps, oT_sb, y_ready, x_done) = semaphores(
            nc, ctx, tag, "mask kv set vb vc q_ps q_sb s_ready s_used sh_step mx_ready p_in p_ready pt_ps pt_sb "
            "o_ready n_step o_used on_ready oT_ps oT_sb y_ready x_done")
        gate = K.gate[:, 0, layer:layer + 1]
        with nc.Block() as block:
            if mask is not None:
                @block.sync
                def _(sp):
                    sp.dma_start(mi[:, :, :], mask.rearrange("(t p) k -> p t k", p=P)).then_inc(s_mask, 16)

            @block.tensor
            def _(pe):
                for ct in range(KT):
                    for k in range(KT):
                        pe.matmul(ps[:, 0, ct * 256:ct * 256 + B * L], wk[:, k, ct * P:(ct + 1) * P],
                                  K.ctxT[:, k, :], start=(k == 0), stop=(k == KT - 1))
                for b in range(B):
                    for k in range(KT):
                        m = pe.matmul(ps[0:L, 1, b * D:(b + 1) * D], K.ctxT[:, k, b * L:(b + 1) * L],
                                      wv[:, k, :], start=(k == 0), stop=(k == KT - 1))
                m.then_inc(s_kv, 1)
                pe.wait_ge(s_vb, 3)
                for b in range(B):
                    for part in range(NC):
                        for j, h in enumerate(heads[part]):
                            down = h * L - part * P
                            m = pe.matmul(ps[:, 2 + b, (3 * part + j) * HV:(3 * part + j + 1) * HV],
                                          K.shift[0:L, P - down:2 * P - down], vaug[:, b, h, :],
                                          start=True, stop=True)
                m.then_inc(s_vc, 1)

                def scores(b, i):
                    pe.wait_ge(s_used, b * TB + i + 1)
                    for g in range(4):
                        m = pe.matmul(ps[:, g, 0:G4], qT[:, g // 2, i * P:(i + 1) * P],
                                      kblk[:, b, g // 2, (g % 2) * G4:(g % 2 + 1) * G4], start=True, stop=True)
                    m.then_inc(s_ready, 1)

                def turn(b, i):
                    pe.wait_ge(p_ready, b * TB + i + 1)
                    for r, (lo, hi) in enumerate(rounds):
                        if r != 1:
                            pe.wait_ge(pt_sb, b * 3 * TB + 3 * i + (r == 2) + 1)
                        for part in range(lo, hi):
                            n = rows[part]
                            m = pe.transpose(ps[0:n, 4 + r % 2, (part - lo) * P:(part - lo + 1) * P],
                                             pr[:, i % 2, part * P:part * P + n], K.ident[:, :])
                        m.then_inc(pt_ps, 1)

                def values(b, i):
                    pe.wait_ge(o_used, b * TB + i + 1)
                    for r, (lo, hi) in enumerate(rounds):
                        pe.wait_ge(pt_sb, b * 3 * TB + 3 * i + r + 2)
                        for part in range(lo, hi):
                            n, hs = rows[part], heads[part]
                            m = pe.matmul(ps[:, 6, hs[0] * HV:(hs[-1] + 1) * HV], pT[0:n, i % 2, part, :],
                                          vblk[0:n, b, 3 * part * HV:(3 * part + len(hs)) * HV],
                                          start=(part == 0), stop=(part == NC - 1), skip_group_check=True)
                    m.then_inc(o_ready, 1)

                def project(b, i):
                    pe.wait_ge(on_ready, b * TB + i + 1)
                    pe.wait_ge(x_done, b * TB + i + 1)
                    for k in range(KT):
                        m = pe.transpose(ps[:, 7, k * P:(k + 1) * P], on[:, i % 2, k * P:(k + 1) * P], K.ident[:, :])
                    m.then_inc(oT_ps, 1)
                    pe.wait_ge(oT_sb, b * TB + i + 1)
                    for k in range(KT):
                        m = pe.matmul(ps[:, 7, D:2 * D], oT[:, k * P:(k + 1) * P], wo[:, k, :],
                                      start=(k == 0), stop=(k == KT - 1))
                    m.then_inc(y_ready, 1)

                pe.wait_ge(s_set, 9)
                with pe.Fori(0, B) as b:
                    pe.wait_ge(x_done, b * TB + 1)
                    for n in range(4):
                        for k in range(KT):
                            m = pe.matmul(ps[:, n, :], wq[:, k, (n // 2) * P:(n // 2 + 1) * P],
                                          K.xnT[:, k, bass.ds(b * S + (n % 2) * 512, 512)],
                                          start=(k == 0), stop=(k == KT - 1))
                        m.then_inc(q_ps, 1)
                    pe.wait_ge(q_sb, b * 4 + 4)
                    scores(b, 0)
                    for i in range(TB):
                        if i + 1 < TB:
                            scores(b, i + 1)
                        turn(b, i)
                        values(b, i)
                        if i:
                            project(b, i - 1)
                    project(b, TB - 1)

            @block.scalar
            def _(act):
                act.sem_inc(pt_sb, 1)

                def exps(b, i):
                    act.wait_ge(p_in, b * TB + i + 1)
                    if i >= 2:
                        act.wait_ge(pt_ps, b * 3 * TB + 3 * (i - 1))
                    act.activation(pr[:, i % 2, :], sm[:, i % 2, :], ACT.Exp).then_inc(p_ready, 1)

                with act.Fori(0, B) as b:
                    act.wait_ge(x_done, b * TB + 1)
                    for n in range(4):
                        act.wait_ge(q_ps, b * 4 + n + 1)
                        dst = qT[:, n // 2, (n % 2) * 512:(n % 2 + 1) * 512]
                        if bq is None:
                            act.activation(dst, ps[:, n, :], ACT.Copy).then_inc(q_sb, 1)
                        else:
                            act.activation(dst, ps[:, n, :], ACT.Identity,
                                           bias=bq[:, n // 2:n // 2 + 1]).then_inc(q_sb, 1)
                    exps(b, 0)
                    for i in range(TB):
                        for r, (lo, hi) in enumerate(rounds):
                            act.wait_ge(pt_ps, b * 3 * TB + 3 * i + r + 1)
                            if i >= 2 and r == 0:
                                act.wait_ge(o_ready, b * TB + i - 1)
                            if r < 2:
                                act.activation(pT[:, i % 2, lo:hi, :].rearrange("p a b -> p (a b)"),
                                               ps[:, 4 + r, :], ACT.Copy).then_inc(pt_sb, 1)
                            else:
                                act.activation(pT[:, i % 2, lo, :], ps[:, 4, 0:P], ACT.Copy)
                                act.activation(pT[0:rows[-1], i % 2, lo + 1, :], ps[0:rows[-1], 4, P:2 * P],
                                               ACT.Copy).then_inc(pt_sb, 1)
                        if i:
                            act.wait_ge(oT_ps, b * TB + i)
                            act.activation(oT[:, :], ps[:, 7, 0:D], ACT.Copy).then_inc(oT_sb, 1)
                        if i + 1 < TB:
                            exps(b, i + 1)
                    act.wait_ge(oT_ps, b * TB + TB)
                    act.activation(oT[:, :], ps[:, 7, 0:D], ACT.Copy).then_inc(oT_sb, 1)

            @block.gpsimd
            def _(pool):
                if bo is not None:
                    pool.tensor_tensor(gbo[:, :], bo[:, :], gate.broadcast_to([P, D]), ALU.mult).then_inc(s_vb, 1)
                    pool.wait_ge(s_vb, 1)
                    pool.tensor_tensor(K.x[:, :, :], K.x[:, :, :],
                                       gbo[:, :].unsqueeze(1).broadcast_to([P, NT, D]), ALU.add).then_inc(s_vb, 1)
                else:
                    pool.memset(gbo[:, 0:1], 0.0).then_inc(s_vb, 2)

            @block.vector
            def _(dve):
                s = Steps(s_set)
                s.did(dve.memset(vaug[:, :, :, :], 1.0))
                dve.wait_ge(s_set, 1)
                dve.wait_ge(s_kv, 1)
                for ct in range(KT):
                    if bk is None:
                        s.did(dve.tensor_copy(kT[:, ct, :], ps[:, 0, ct * 256:ct * 256 + B * L]))
                    else:
                        s.did(dve.tensor_scalar(kT[:, ct, :], ps[:, 0, ct * 256:ct * 256 + B * L],
                                                bk[:, ct:ct + 1], None, ALU.add))
                for b in range(B):
                    v = ps[0:L, 1, b * D:(b + 1) * D].rearrange("p (h c) -> p h c", h=H)
                    if bv is None:
                        m = dve.tensor_copy(vaug[:, b, :, 0:HD], v)
                    else:
                        m = dve.tensor_tensor(vaug[:, b, :, 0:HD], v, bv[:, :].rearrange("p (h c) -> p h c", h=H), ALU.add)
                    m.then_inc(n_step, 1)
                dve.wait_ge(n_step, 2)
                dve.wait_ge(s_vb, 2)
                dve.sem_inc(s_vb, 1)
                dve.wait_ge(s_set, 3)
                for b in range(B):
                    for ct in range(KT):
                        s.did(dve.tensor_tensor(
                            kblk[:, b, ct, :].rearrange("p (h k) -> p h k", h=8),
                            kT[:, ct, b * L:(b + 1) * L].unsqueeze(1).broadcast_to([P, 8, L]),
                            K.headmask[:, :].unsqueeze(2).broadcast_to([P, 8, L]), ALU.mult))
                if mask is not None:
                    dve.wait_ge(s_mask, 16)
                    dve.tensor_scalar(mf[:, :, :], mi[:, :, :], 0, -3e38, ALU.is_equal, ALU.mult).then_inc(n_step, 1)
                    dve.wait_ge(n_step, 3)
                dve.wait_ge(s_vc, 1)
                W = NC * 3 * HV
                used = [3 * part * HV + n for part in range(NC) for n in range(len(heads[part]) * HV)]
                full = used == list(range(len(used)))
                for b in range(B):
                    if full:
                        s.did(dve.tensor_copy(vblk[:, b, 0:len(used)], ps[:, 2 + b, 0:len(used)]))
                    else:
                        for part in range(NC):
                            lo, n = 3 * part * HV, len(heads[part]) * HV
                            m = dve.tensor_copy(vblk[:, b, lo:lo + n], ps[:, 2 + b, lo:lo + n])
                            if part == NC - 1:
                                s.did(m)
                dve.wait_ge(s_set, s.last())
                assert s.last() == 9

                for free in (s_used, o_used, x_done):
                    dve.sem_inc(free, 1)

                def front(b, i):
                    dve.wait_ge(s_ready, b * TB + i + 1)
                    if i >= 2:
                        dve.wait_ge(p_ready, b * TB + i - 1)
                    sc = ps[:, 0:4, 0:G4].rearrange("p g (h k) -> p g h k", h=4)
                    smt = sm[:, i % 2, :].rearrange("p (g h k) -> p g h k", g=4, h=4)
                    sm2 = sm[:, i % 2, :].rearrange("p (h k) -> p h k", h=H)
                    mxt = mx[:, i % 2, :]
                    if mask is not None:
                        dve.tensor_tensor(sm[:, i % 2, :].rearrange("p (g c) -> p g c", g=4).rearrange("p g (h k) -> p g h k", h=4),
                                          sc, mf[:, i, :].unsqueeze(1).unsqueeze(1).broadcast_to([P, 4, 4, L]),
                                          ALU.add).then_inc(s_used, 1)
                        dve.wait_ge(s_used, b * TB + i + 2)
                        dve.tensor_reduce(mxt, sm2, AX.X, ALU.max).then_inc(sh_step, 1)
                        dve.wait_ge(sh_step, b * TB + i + 1)
                        dve.tensor_tensor(sm2, sm2, mxt.unsqueeze(2).broadcast_to([P, H, L]),
                                          ALU.subtract).then_inc(p_in, 1)
                    else:
                        dve.tensor_reduce(mxt.rearrange("p (g h) -> p g h", g=4), sc, AX.X, ALU.max).then_inc(sh_step, 1)
                        dve.wait_ge(sh_step, b * TB + i + 1)
                        m = dve.tensor_tensor(smt, sc, mxt.rearrange("p (g h) -> p g h", g=4).unsqueeze(3)
                                              .broadcast_to([P, 4, 4, L]), ALU.subtract)
                        m.then_inc(p_in, 1)
                        dve.wait_ge(p_in, b * TB + i + 1)
                        dve.sem_inc(s_used, 1)

                def normalise(b, i):
                    o = ps[:, 6, 0:H * HV].rearrange("p (h c) -> p h c", h=H)
                    dve.wait_ge(o_ready, b * TB + i + 1)
                    dve.reciprocal(rden[:, i % 2, :], o[:, :, HD]).then_inc(mx_ready, 1)
                    dve.wait_ge(mx_ready, b * TB + i + 1)
                    if i >= 2:
                        dve.wait_ge(oT_ps, b * TB + i - 1)
                    dve.tensor_tensor(on[:, i % 2, :].rearrange("p (h c) -> p h c", h=H), o[:, :, 0:HD],
                                      rden[:, i % 2, :].unsqueeze(2).broadcast_to([P, H, HD]),
                                      ALU.mult).then_inc(on_ready, 1)
                    dve.wait_ge(on_ready, b * TB + i + 1)
                    dve.sem_inc(o_used, 1)

                def residual(b, i):
                    dve.wait_ge(y_ready, b * TB + i + 1)
                    xt = K.x[:, b * TB + i, :]
                    dve.scalar_tensor_tensor(xt, ps[:, 7, D:2 * D], gate, xt, ALU.mult, ALU.add).then_inc(x_done, 1)

                with dve.Fori(0, B) as b:
                    dve.wait_ge(x_done, b * TB + 1)
                    front(b, 0)
                    for i in range(TB):
                        if i + 1 < TB:
                            front(b, i + 1)
                        normalise(b, i)
                        if i:
                            residual(b, i - 1)
                    residual(b, TB - 1)


def sigmoid_attention(nc, ctx, K, tag, layer, wqn, wk, wv, bq, bk, bv):
    QK = 64
    ps = K.ps
    with ExitStack() as c:
        kp = sbuf(nc, c, tag + "kp", [QK, B * L])
        v = sbuf(nc, c, tag + "v", [L, B, D])
        a = sbuf(nc, c, tag + "a", [P, KT, B * L])
        cb = sbuf(nc, c, tag + "cb", [L, B])
        zT = sbuf(nc, c, tag + "zT", [L, 2, 512])
        s_kv, s_kvb, s_a, s_ab, s_ps, s_z, s_y, s_x = semaphores(nc, c, tag, "kv kvb a ab s_ps z y x")
        gate = K.gate[:, 0, layer:layer + 1]
        groups = B * S // 512
        with nc.Block() as block:
            @block.tensor
            def _(pe):
                for k in range(KT):
                    pe.matmul(ps[0:QK, 0, 0:B * L], wk[:, k, :], K.ctxT[:, k, :], start=(k == 0), stop=(k == KT - 1))
                for b in range(B):
                    for k in range(KT):
                        m = pe.matmul(ps[0:L, 1, b * D:(b + 1) * D], K.ctxT[:, k, b * L:(b + 1) * L],
                                      wv[:, k, :], start=(k == 0), stop=(k == KT - 1))
                m.then_inc(s_kv, 1)
                pe.wait_ge(s_kvb, 2)
                for k in range(KT):
                    pe.matmul(ps[:, 2, k * 256:k * 256 + B * L], wqn[:, k * P:(k + 1) * P], kp[:, :],
                              start=True, stop=True)
                for b in range(B):
                    m = pe.matmul(ps[0:L, 3, b:b + 1], kp[:, b * L:(b + 1) * L], bq[:, 0:1], start=True, stop=True)
                m.then_inc(s_a, 1)
                pe.wait_ge(s_ab, 2)

                def scores(g):
                    b = g * 512 // S
                    if g >= 2:
                        pe.wait_ge(s_z, g - 1)
                    for k in range(KT):
                        m = pe.matmul(ps[0:L, 4 + g % 2, :], a[:, k, b * L:(b + 1) * L],
                                      K.xnT[:, k, g * 512:(g + 1) * 512], start=(k == 0), stop=(k == KT - 1))
                    m.then_inc(s_ps, 1)

                scores(0)
                for g in range(groups):
                    b = g * 512 // S
                    if g + 1 < groups:
                        scores(g + 1)
                    pe.wait_ge(s_z, g + 1)
                    for u in range(2):
                        n = 2 * g + u
                        if n >= 2:
                            pe.wait_ge(s_x, n - 1)
                        for j in range(2):
                            m = pe.matmul(ps[:, 6 + n % 2, j * D:(j + 1) * D],
                                          zT[:, g % 2, (2 * u + j) * P:(2 * u + j + 1) * P], v[:, b, :],
                                          start=True, stop=True)
                        m.then_inc(s_y, 1)

            @block.scalar
            def _(act):
                act.wait_ge(s_a, 1)
                act.activation(cb[:, :], ps[0:L, 3, 0:B], ACT.Copy, scale=QK ** -0.5).then_inc(s_ab, 1)
                act.wait_ge(s_ab, 2)
                for g in range(groups):
                    b = g * 512 // S
                    act.wait_ge(s_ps, g + 1)
                    if g >= 2:
                        act.wait_ge(s_y, 2 * (g - 1))
                    act.activation(zT[:, g % 2, :], ps[0:L, 4 + g % 2, :], ACT.Sigmoid, bias=cb[:, b:b + 1],
                                   scale=QK ** -0.5).then_inc(s_z, 1)

            @block.vector
            def _(dve):
                dve.wait_ge(s_kv, 1)
                dve.tensor_scalar(kp[:, :], ps[0:QK, 0, 0:B * L], bk[:, 0:1], None, ALU.add).then_inc(s_kvb, 1)
                dve.tensor_tensor(v[:, :, :], ps[0:L, 1, :].rearrange("p (b d) -> p b d", b=B),
                                  bv[:, :].unsqueeze(1).broadcast_to([L, B, D]), ALU.add).then_inc(s_kvb, 1)
                dve.wait_ge(s_a, 1)
                dve.tensor_copy(a[:, :, :], ps[:, 2, :].rearrange("p (k c) -> p k c", k=KT)[:, :, 0:B * L]).then_inc(s_ab, 1)
                for n in range(2 * groups):
                    dve.wait_ge(s_y, n + 1)
                    xt = K.x[:, 2 * n:2 * n + 2, :].rearrange("p t d -> p (t d)")
                    dve.scalar_tensor_tensor(xt, ps[:, 6 + n % 2, :], gate, xt, ALU.mult, ALU.add).then_inc(s_x, 1)


def align_attention(nc, ctx, K, tag, layer, wT, wn, bc):
    ps = K.ps
    with ExitStack() as c:
        eo = sbuf(nc, c, tag + "eo", [P, KT, B * L])
        a = sbuf(nc, c, tag + "a", [P, KT, B * L])
        cr = sbuf(nc, c, tag + "cr", [1, B * L])
        sm = sbuf(nc, c, tag + "sm", [P, 2, 4, L])
        pr = sbuf(nc, c, tag + "pr", [P, 2, 4, L])
        pT = sbuf(nc, c, tag + "pT", [L, 2, 512])
        vec = sbuf(nc, c, tag + "vec", [P, 2, 4, 4])
        s_e, s_eb, s_a, s_ab, s_ps, s_mx, s_sh, s_p, s_sum, s_tp, s_tb, s_y, s_x = semaphores(
            nc, c, tag, "e eb a ab s_ps mx sh p sum tp tb y x")
        gate = K.gate[:, 0, layer:layer + 1]
        groups = B * S // 512
        with nc.Block() as block:
            @block.tensor
            def _(pe):
                for e in range(KT):
                    for k in range(KT):
                        m = pe.matmul(ps[:, 0, e * 256:e * 256 + B * L], wT[:, k, e * P:(e + 1) * P], K.ctxT[:, k, :],
                                      start=(k == 0), stop=(k == KT - 1))
                m.then_inc(s_e, 1)
                pe.wait_ge(s_eb, 2)
                for d in range(KT):
                    for e in range(KT):
                        pe.matmul(ps[:, 1, d * 256:d * 256 + B * L], wn[:, e, d * P:(d + 1) * P], eo[:, e, :],
                                  start=(e == 0), stop=(e == KT - 1))
                for e in range(KT):
                    m = pe.matmul(ps[0:1, 2, 0:B * L], bc[:, e:e + 1], eo[:, e, :], start=(e == 0), stop=(e == KT - 1))
                m.then_inc(s_a, 1)
                pe.wait_ge(s_ab, 2)

                def scores(g):
                    b = g * 512 // S
                    if g >= 2:
                        pe.wait_ge(s_sh, g - 1)
                    for i in range(4):
                        t = 4 * g + i
                        o = ps[:, g % 2, i * L:(i + 1) * L]
                        for k in range(KT):
                            pe.matmul(o, K.xnT[:, k, t * P:(t + 1) * P], a[:, k, b * L:(b + 1) * L],
                                      start=(k == 0), stop=False)
                        m = pe.matmul(o, K.ones[0:1, :], cr[:, b * L:(b + 1) * L], start=False, stop=True)
                    m.then_inc(s_ps, 1)

                scores(0)
                for g in range(groups):
                    b = g * 512 // S
                    if g + 1 < groups:
                        scores(g + 1)
                    pe.wait_ge(s_p, g + 1)
                    for i in range(4):
                        m = pe.transpose(ps[0:L, 2 + g % 2, i * P:(i + 1) * P], pr[:, g % 2, i, :], K.ident[:, :])
                    m.then_inc(s_tp, 1)
                    pe.wait_ge(s_tb, g + 1)
                    for u in range(2):
                        n = 2 * g + u
                        if n >= 4:
                            pe.wait_ge(s_x, n - 3)
                        for j in range(2):
                            m = pe.matmul(ps[:, 4 + n % 4, j * D:(j + 1) * D],
                                          pT[:, g % 2, (2 * u + j) * P:(2 * u + j + 1) * P], K.ctx_nat[:, b, :],
                                          start=True, stop=True)
                        m.then_inc(s_y, 1)

            @block.scalar
            def _(act):
                act.wait_ge(s_a, 1)
                act.activation(cr[:, :], ps[0:1, 2, 0:B * L], ACT.Copy).then_inc(s_ab, 1)
                for g in range(groups):
                    act.wait_ge(s_sh, g + 1)
                    if g >= 2:
                        act.wait_ge(s_tp, g - 1)
                        act.wait_ge(s_sum, g - 1)
                    act.activation(pr[:, g % 2, :, :], sm[:, g % 2, :, :], ACT.Exp).then_inc(s_p, 1)
                    act.wait_ge(s_tp, g + 1)
                    if g >= 2:
                        act.wait_ge(s_y, 2 * (g - 1))
                    act.activation(pT[:, g % 2, :], ps[0:L, 2 + g % 2, :], ACT.Copy).then_inc(s_tb, 1)

            @block.vector
            def _(dve):
                dve.wait_ge(s_e, 1)
                for e in range(KT):
                    dve.tensor_scalar(eo[:, e, :], ps[:, 0, e * 256:e * 256 + B * L], bc[:, e:e + 1], None,
                                      ALU.add).then_inc(s_eb, 1)
                dve.wait_ge(s_a, 1)
                dve.tensor_copy(a[:, :, :], ps[:, 1, :].rearrange("p (k c) -> p k c", k=KT)[:, :, 0:B * L]).then_inc(s_ab, 1)

                def front(g):
                    dve.wait_ge(s_ps, g + 1)
                    sc = ps[:, g % 2, 0:4 * L].rearrange("p (i k) -> p i k", i=4)
                    dve.tensor_reduce(vec[:, g % 2, 0, :], sc, AX.X, ALU.max).then_inc(s_mx, 1)
                    dve.wait_ge(s_mx, g + 1)
                    if g >= 2:
                        dve.wait_ge(s_p, g - 1)
                    dve.tensor_tensor(sm[:, g % 2, :, :], sc, vec[:, g % 2, 0, :].unsqueeze(2).broadcast_to([P, 4, L]),
                                      ALU.subtract).then_inc(s_sh, 1)

                front(0)
                s_c = s_eb
                st = Steps(s_c, 2)
                for g in range(groups):
                    if g + 1 < groups:
                        front(g + 1)
                    dve.wait_ge(s_p, g + 1)
                    vg = vec[:, g % 2, :, :]
                    dve.tensor_reduce(vg[:, 1, :], pr[:, g % 2, :, :], AX.X, ALU.add).then_inc(s_sum, 1)
                    dve.wait_ge(s_sum, g + 1)
                    st.did(dve.reciprocal(vg[:, 2, :], vg[:, 1, :]))
                    dve.wait_ge(s_c, st.last())
                    st.did(dve.tensor_scalar(vg[:, 3, :], vg[:, 2, :], gate, None, ALU.mult))
                    dve.wait_ge(s_c, st.last())
                    for u in range(2):
                        dve.wait_ge(s_y, 2 * g + u + 1)
                        for j in range(2):
                            i = 2 * u + j
                            xt = K.x[:, 4 * g + i, :]
                            m = dve.scalar_tensor_tensor(xt, ps[:, 4 + (2 * g + u) % 4, j * D:(j + 1) * D],
                                                         vg[:, 3, i:i + 1], xt, ALU.mult, ALU.add)
                        m.then_inc(s_x, 1)


def sum_magnitudes(dve, s_part, weights, part, out, steps):
    for n, w in enumerate(weights):
        dve.tensor_reduce(part[:, n, :], w[:, :, :].rearrange("p k f -> p (k f)").rearrange("p (a c) -> p a c", c=64),
                          AX.X, ALU.add, apply_absolute_value=True).then_inc(s_part, 1)
    dve.wait_ge(s_part, 2)
    for n in range(2):
        steps.did(dve.tensor_reduce(out[:, n:n + 1], part[:, n, :], AX.X, ALU.add))


def bitnet_ffn(nc, ctx, K, tag, layer, w1, w2, cw, cbias):
    F = 1024
    FT = F // P
    ps = K.ps
    psb = [ps[:, k, :].bitcast(BF16) for k in range(8)]
    with ExitStack() as c:
        q1 = sbuf(nc, c, tag + "q1", [P, KT, F], BF16)
        q2 = sbuf(nc, c, tag + "q2", [P, FT, D], BF16)
        wt = sbuf(nc, c, tag + "wt", [P, 2, 2048])
        xq = sbuf(nc, c, tag + "xq", [P, NT, D], BF16)
        xqT = sbuf(nc, c, tag + "xqT", [P, KT, B * S], BF16)
        dqb = sbuf(nc, c, tag + "dqb", [P, B * S])
        diag = sbuf(nc, c, tag + "diag", [P, 4, P])
        vec = sbuf(nc, c, tag + "vec", [P, 8, NT])
        wv = sbuf(nc, c, tag + "wv", [P, 4, 2])
        magic = sbuf(nc, c, tag + "magic", [P, 1])
        hb = sbuf(nc, c, tag + "hb", [P, 2, S + 2])
        yb = sbuf(nc, c, tag + "yb", [P, 2, S])
        act_s = sbuf(nc, c, tag + "act", [P, FT, S])
        tv = sbuf(nc, c, tag + "tv", [P, 6, TB])
        qf = sbuf(nc, c, tag + "qf", [P, 2, F])
        qb = sbuf(nc, c, tag + "qb", [P, 2, F], BF16)
        qT = sbuf(nc, c, tag + "qT", [P, 2, F], BF16)
        part = sbuf(nc, c, tag + "part", [P, 2, 32])
        (s_part,) = semaphores(nc, c, tag, "part")
        (s_set, s_sum, s_xq, s_xt, s_xe, s_dg, s_db, s_de, h_ps, h_sb, y0, tap, y_sb, a_sb, t_ps, t_step, sc_ready,
         qf_sb, qb_sb, u_ps, u_sb, y_ps, x_done) = semaphores(
            nc, c, tag, "set sum xq xt xe dg db de h_ps h_sb y0 tap y_sb a_sb t_ps t_step sc qf qb u_ps u_sb y_ps xd")
        gate = K.gate[:, 1, layer:layer + 1]
        with nc.Block() as block:
            @block.tensor
            def _(pe):
                pe.wait_ge(s_set, 2)
                pe.matmul(ps[:, 7, 0:2], K.ones[:, :], wv[:, 0, :], start=True, stop=True).then_inc(s_sum, 1)
                for q in range(4):
                    pe.wait_ge(s_xq, 1)
                    for k in range(KT):
                        for i in range(4):
                            t = 4 * q + i
                            m = pe.transpose(psb[q][:, (4 * k + i) * P:(4 * k + i + 1) * P],
                                             xq[:, t, k * P:(k + 1) * P], K.identb[:, :])
                    m.then_inc(s_xt, 1)
                for t in range(NT):
                    pe.wait_ge(s_dg, t + 1)
                    if t % 4 == 0:
                        pe.wait_ge(s_xe, 4)
                        if t >= 8:
                            pe.wait_ge(s_de, t // 4 - 1)
                    m = pe.matmul(ps[:, 4 + (t // 4) % 2, (t % 4) * P:(t % 4 + 1) * P], K.ones[:, :], diag[:, t % 4, :],
                                  start=True, stop=True)
                    m.then_inc(s_db, 1)
                pe.wait_ge(s_de, 4)
                with pe.Fori(0, B) as b:
                    pe.wait_ge(x_done, b * TB + 1)
                    for f in range(FT):
                        if f >= 2:
                            pe.wait_ge(h_sb, b * FT + f - 1)
                        for hf in range(2):
                            for k in range(KT):
                                m = pe.matmul(ps[:, 2 * (f % 2) + hf, :], q1[:, k, f * P:(f + 1) * P],
                                              xqT[:, k, bass.ds(b * S + hf * 512, 512)],
                                              start=(k == 0), stop=(k == KT - 1))
                        m.then_inc(h_ps, 1)
                    pe.wait_ge(a_sb, b * FT + FT)

                    def turn(i):
                        if i:
                            pe.wait_ge(qf_sb, b * TB + i)
                        for f in range(FT):
                            m = pe.transpose(ps[:, 4 + f // 4, (f % 4) * P:(f % 4 + 1) * P],
                                             act_s[:, f, i * P:(i + 1) * P], K.ident[:, :])
                        m.then_inc(t_ps, 1)

                    turn(0)
                    for i in range(TB):
                        if i + 1 < TB:
                            turn(i + 1)
                        pe.wait_ge(qb_sb, b * TB + i + 1)
                        if i:
                            pe.wait_ge(u_sb, b * TB + i)
                        for f in range(FT):
                            m = pe.transpose(psb[6][:, f * P:(f + 1) * P], qb[:, i % 2, f * P:(f + 1) * P],
                                             K.identb[:, :])
                        m.then_inc(u_ps, 1)
                        pe.wait_ge(u_sb, b * TB + i + 1)
                        if i:
                            pe.wait_ge(x_done, b * TB + i + 1)
                        for f in range(FT):
                            m = pe.matmul(ps[:, 7, 0:D], qT[:, i % 2, f * P:(f + 1) * P], q2[:, f, :],
                                          start=(f == 0), stop=(f == FT - 1))
                        m.then_inc(y_ps, 1)

            @block.scalar
            def _(act):
                for q in range(4):
                    act.wait_ge(s_xt, q + 1)
                    act.activation(xqT[:, :, q * 512:(q + 1) * 512], psb[q].rearrange("p (k c) -> p k c", k=KT),
                                   ACT.Copy).then_inc(s_xe, 1)
                for q in range(4):
                    act.wait_ge(s_db, 4 * q + 4)
                    act.activation(dqb[:, q * 512:(q + 1) * 512], ps[:, 4 + q % 2, :], ACT.Copy).then_inc(s_de, 1)
                with act.Fori(0, B) as b:
                    def centre(f):
                        act.wait_ge(h_sb, b * FT + f + 1)
                        if f >= 2:
                            act.wait_ge(a_sb, b * FT + f - 1)
                        act.activation(yb[:, f % 2, :], hb[:, f % 2, 1:S + 1], ACT.Identity, bias=cbias[:, f:f + 1],
                                       scale=cw[:, f, 1:2]).then_inc(y0, 1)

                    centre(0)
                    for f in range(FT):
                        if f + 1 < FT:
                            centre(f + 1)
                        act.wait_ge(y_sb, b * FT + f + 1)
                        act.activation(act_s[:, f, :], yb[:, f % 2, :], ACT.Silu).then_inc(a_sb, 1)

                    def scaled(i):
                        act.wait_ge(sc_ready, b * TB + i + 1)
                        if i >= 2:
                            act.wait_ge(qb_sb, b * TB + i - 1)
                        act.activation(qf[:, i % 2, :], ps[:, 4:6, :].rearrange("p a c -> p (a c)"), ACT.Identity,
                                       bias=magic[:, 0:1], scale=tv[:, 3, i:i + 1]).then_inc(qf_sb, 1)

                    scaled(0)
                    for i in range(TB):
                        if i + 1 < TB:
                            scaled(i + 1)
                        act.wait_ge(u_ps, b * TB + i + 1)
                        if i >= 2:
                            act.wait_ge(y_ps, b * TB + i - 1)
                        act.activation(qT[:, i % 2, :], psb[6], ACT.Copy).then_inc(u_sb, 1)

            @block.vector
            def _(dve):
                s = Steps(s_set)

                def then(ins):
                    s.did(ins)
                    dve.wait_ge(s_set, s.last())

                sum_magnitudes(dve, s_part, (w1, w2), part, wv[:, 0, :], s)
                dve.memset(hb[:, :, :], 0.0).then_inc(tap, 1)
                dve.memset(magic[:, :], MAGIC).then_inc(tap, 1)
                dve.wait_ge(tap, 2)
                then(dve.tensor_reduce(vec[:, 0, :], K.xn[:, :, :], AX.X, ALU.max, apply_absolute_value=True))
                then(dve.tensor_scalar(vec[:, 1, :], vec[:, 0, :], 1e-5, None, ALU.max))
                then(dve.reciprocal(vec[:, 2, :], vec[:, 1, :]))
                then(dve.tensor_scalar(vec[:, 3, :], vec[:, 2, :], 127.0, None, ALU.mult))
                then(dve.tensor_tensor(K.xn[:, :, :], K.xn[:, :, :],
                                       vec[:, 3, :].unsqueeze(2).broadcast_to([P, NT, D]), ALU.mult))
                dve.tensor_scalar(xq[:, :, :], K.xn[:, :, :], MAGIC, MAGIC, ALU.add, ALU.subtract).then_inc(s_xq, 1)
                dve.wait_ge(s_sum, 1)
                then(dve.tensor_scalar(wv[:, 1, :], ps[:, 7, 0:2], 1.0 / (F * D), 1e-5, ALU.mult, ALU.max))
                then(dve.reciprocal(wv[:, 2, :], wv[:, 1, :]))
                for n, (w, q) in enumerate(((w1, q1), (w2, q2))):
                    flat, qflat = (z[:, :, :].rearrange("p k f -> p (k f)") for z in (w, q))
                    then(dve.tensor_scalar(wt[:, 0, :], flat, wv[:, 2, n:n + 1], MAGIC, ALU.mult, ALU.add))
                    then(dve.tensor_scalar(wt[:, 1, :], wt[:, 0, :], MAGIC, 1.0, ALU.subtract, ALU.min))
                    then(dve.tensor_scalar(qflat, wt[:, 1, :], -1.0, None, ALU.max))
                then(dve.tensor_scalar(vec[:, 4, :], vec[:, 1, :], wv[:, 1, 0:1], 1.0 / 127, ALU.mult, ALU.mult))
                then(dve.tensor_scalar(wv[:, 3, 1:2], wv[:, 1, 1:2], gate, 1.0 / 127, ALU.mult, ALU.mult))
                for t in range(NT):
                    if t >= 4:
                        dve.wait_ge(s_db, t - 3)
                    dve.tensor_scalar(diag[:, t % 4, :], K.ident[:, :], vec[:, 4, t:t + 1], None,
                                      ALU.mult).then_inc(s_dg, 1)
                dve.wait_ge(s_de, 4)
                dve.sem_inc(x_done, 1)
                TS = 4
                with dve.Fori(0, B) as b:
                    def dequant(f):
                        dve.wait_ge(h_ps, b * FT + f + 1)
                        if f >= 2:
                            dve.wait_ge(y_sb, b * FT + f - 1)
                        dve.tensor_tensor(hb[:, f % 2, 1:S + 1], ps[:, 2 * (f % 2):2 * (f % 2) + 2, :].rearrange("p a c -> p (a c)"),
                                          dqb[:, bass.ds(b * S, S)], ALU.mult).then_inc(h_sb, 1)

                    dequant(0)
                    for f in range(FT):
                        if f + 1 < FT:
                            dequant(f + 1)
                        dve.wait_ge(y0, b * FT + f + 1)
                        y = yb[:, f % 2, :]
                        dve.scalar_tensor_tensor(y, hb[:, f % 2, 0:S], cw[:, f, 0:1], y, ALU.mult, ALU.add).then_inc(tap, 1)
                        dve.wait_ge(tap, b * FT + f + 3)
                        dve.scalar_tensor_tensor(y, hb[:, f % 2, 2:S + 2], cw[:, f, 2:3], y, ALU.mult,
                                                 ALU.add).then_inc(y_sb, 1)

                    def scale(i):
                        dve.wait_ge(t_ps, b * TB + i + 1)
                        t = Steps(t_step, b * TS * TB + TS * i)
                        t.did(dve.tensor_reduce(tv[:, 0, i:i + 1], ps[:, 4:6, :].rearrange("p a c -> p (a c)"), AX.X, ALU.max,
                                                apply_absolute_value=True))
                        dve.wait_ge(t_step, t.last())
                        t.did(dve.tensor_scalar(tv[:, 1, i:i + 1], tv[:, 0, i:i + 1], 1e-5, None, ALU.max))
                        dve.wait_ge(t_step, t.last())
                        t.did(dve.reciprocal(tv[:, 2, i:i + 1], tv[:, 1, i:i + 1]))
                        t.did(dve.tensor_scalar(tv[:, 4, i:i + 1], tv[:, 1, i:i + 1], wv[:, 3, 1:2], None, ALU.mult))
                        dve.wait_ge(t_step, t.last())
                        dve.tensor_scalar(tv[:, 3, i:i + 1], tv[:, 2, i:i + 1], 127.0, None, ALU.mult).then_inc(sc_ready, 1)

                    def residual(i):
                        dve.wait_ge(y_ps, b * TB + i + 1)
                        xt = K.x[:, b * TB + i, :]
                        dve.scalar_tensor_tensor(xt, ps[:, 7, 0:D], tv[:, 4, i:i + 1], xt, ALU.mult,
                                                 ALU.add).then_inc(x_done, 1)

                    scale(0)
                    for i in range(TB):
                        dve.wait_ge(qf_sb, b * TB + i + 1)
                        if i >= 2:
                            dve.wait_ge(u_ps, b * TB + i - 1)
                        dve.tensor_scalar(qb[:, i % 2, :], qf[:, i % 2, :], MAGIC, None, ALU.subtract).then_inc(qb_sb, 1)
                        if i + 1 < TB:
                            scale(i + 1)
                        if i:
                            residual(i - 1)
                    residual(TB - 1)


def ternary_ffn(nc, ctx, K, tag, layer, wu, wd):
    F = 1024
    FT = F // P
    W = 512
    NH = S // W
    ps = K.ps
    with ExitStack() as c:
        tu = sbuf(nc, c, tag + "tu", [P, KT, F], F32R)
        td = sbuf(nc, c, tag + "td", [P, FT, D], F32R)
        wneg = sbuf(nc, c, tag + "wneg", [P, 2048])
        wv = sbuf(nc, c, tag + "wv", [P, 4, 2])
        xh = sbuf(nc, c, tag + "xh", [P, 2, KT, W], F32R)
        xl = sbuf(nc, c, tag + "xl", [P, 2, KT, W], F32R)
        h = sbuf(nc, c, tag + "h", [P, 4, W])
        hh = sbuf(nc, c, tag + "hh", [P, FT, W], F32R)
        hl = sbuf(nc, c, tag + "hl", [P, FT, W], F32R)
        sq = sbuf(nc, c, tag + "sq", [P, FT, W])
        vec = sbuf(nc, c, tag + "vec", [P, 5, 4])
        part = sbuf(nc, c, tag + "part", [P, 2, 32])
        (s_part,) = semaphores(nc, c, tag, "part")
        s_set, s_sum, x_hi, x_lo, u_ps, h_sb, h_hi, h_lo, h_sq, q_ps, vstep, rms, y_ps, x_done = semaphores(
            nc, c, tag, "set sum x_hi x_lo u_ps h_sb h_hi h_lo h_sq q_ps vstep rms y_ps xd")
        gate = K.gate[:, 1, layer:layer + 1]
        with nc.Block() as block:
            @block.tensor
            def _(pe):
                pe.wait_ge(s_set, 2)
                pe.matmul(ps[:, 7, 0:2], K.ones[:, :], wv[:, 0, :], start=True, stop=True).then_inc(s_sum, 1)
                pe.wait_ge(s_set, 8)
                with pe.Fori(0, B) as b:
                    for g in range(NH):
                        pe.wait_ge(x_done, (b * NH + g) * 4 + 1)
                        pe.wait_ge(x_lo, b * NH + g + 1)
                        for f in range(FT):
                            if f >= 4:
                                pe.wait_ge(h_sb, (b * NH + g) * FT + f - 3)
                            for k in range(KT):
                                for n, xs in enumerate((xh, xl)):
                                    m = pe.matmul(ps[:, f % 4, :], tu[:, k, f * P:(f + 1) * P], xs[:, g, k, :],
                                                  start=(k == 0 and n == 0), stop=(k == KT - 1 and n == 1))
                            m.then_inc(u_ps, 1)
                        pe.wait_ge(h_lo, (b * NH + g) * FT + FT)
                        for i in range(4):
                            if i >= 2:
                                pe.wait_ge(x_done, (b * NH + g) * 4 + i)
                            for f in range(FT):
                                for n, hs in enumerate((hh, hl)):
                                    m = pe.matmul(ps[:, 4 + i % 2, 0:D], hs[:, f, i * P:(i + 1) * P], td[:, f, :],
                                                  start=(f == 0 and n == 0), stop=(f == FT - 1 and n == 1))
                            m.then_inc(y_ps, 1)
                            if i == 0:
                                pe.wait_ge(h_sq, (b * NH + g) * FT + FT)
                                for j in range(4):
                                    for f in range(FT):
                                        m = pe.matmul(ps[:, 6, j:j + 1], sq[:, f, j * P:(j + 1) * P], K.ones[:, 0:1],
                                                      start=(f == 0), stop=(f == FT - 1))
                                m.then_inc(q_ps, 1)

            @block.scalar
            def _(act):
                with act.Fori(0, B) as b:
                    for g in range(NH):
                        for f in range(FT):
                            act.wait_ge(u_ps, (b * NH + g) * FT + f + 1)
                            if f >= 4:
                                act.wait_ge(h_lo, (b * NH + g) * FT + f - 3)
                                act.wait_ge(h_sq, (b * NH + g) * FT + f - 3)
                            act.activation(h[:, f % 4, :], ps[:, f % 4, :], ACT.Gelu).then_inc(h_sb, 1)

            @block.gpsimd
            def _(pool):
                with pool.Fori(0, B) as b:
                    for g in range(NH):
                        for f in range(FT):
                            pool.wait_ge(h_sb, (b * NH + g) * FT + f + 1)
                            pool.tensor_tensor(sq[:, f, :], h[:, f % 4, :], h[:, f % 4, :], ALU.mult).then_inc(h_sq, 1)
                        pool.wait_ge(vstep, (b * NH + g) * 3 + 1)
                        pool.tensor_tensor(vec[:, 1, :], vec[:, 0, :], K.hpow[:, 0:4], ALU.pow).then_inc(rms, 1)

            @block.vector
            def _(dve):
                s = Steps(s_set)

                def then(ins):
                    s.did(ins)
                    dve.wait_ge(s_set, s.last())

                flats = [z[:, :, :].rearrange("p k f -> p (k f)") for z in (wu, wd)]
                sum_magnitudes(dve, s_part, (wu, wd), part, wv[:, 0, :], s)
                dve.wait_ge(s_sum, 1)
                s.did(dve.tensor_scalar(wv[:, 1, :], ps[:, 7, 0:2], 0.5 / (F * D), None, ALU.mult))
                then(dve.tensor_scalar(wv[:, 2, :], ps[:, 7, 0:2], -0.5 / (F * D), None, ALU.mult))
                for n, q in enumerate((tu, td)):
                    then(dve.tensor_scalar(wneg[:, :], flats[n], wv[:, 2, n:n + 1], None, ALU.is_lt))
                    then(dve.scalar_tensor_tensor(q[:, :, :].rearrange("p k f -> p (k f)"), flats[n],
                                                  wv[:, 1, n:n + 1], wneg[:, :], ALU.is_gt, ALU.subtract))
                dve.sem_inc(x_done, 1)
                with dve.Fori(0, B) as b:
                    for g in range(NH):
                        xs = K.xnT[:, :, bass.ds(b * S + g * W, W)]
                        dve.tensor_copy(xh[:, g, :, :], xs).then_inc(x_hi, 1)
                        dve.wait_ge(x_hi, b * NH + g + 1)
                        dve.tensor_tensor(xl[:, g, :, :], xs, xh[:, g, :, :].bitcast(F32), ALU.subtract).then_inc(x_lo, 1)
                        for f in range(FT):
                            n = (b * NH + g) * FT + f + 1
                            dve.wait_ge(h_sb, n)
                            if f == 0:
                                dve.wait_ge(x_done, (b * NH + g) * 4 + 1)
                            dve.tensor_copy(hh[:, f, :], h[:, f % 4, :]).then_inc(h_hi, 1)
                            dve.wait_ge(h_hi, n)
                            dve.tensor_tensor(hl[:, f, :], h[:, f % 4, :], hh[:, f, :].bitcast(F32),
                                              ALU.subtract).then_inc(h_lo, 1)
                        dve.wait_ge(q_ps, b * NH + g + 1)
                        v = (b * NH + g) * 3
                        dve.tensor_scalar(vec[:, 0, :], ps[:, 6, 0:4], 1.0 / F, None, ALU.mult).then_inc(vstep, 1)
                        dve.wait_ge(rms, b * NH + g + 1)
                        dve.tensor_scalar(vec[:, 2, :], vec[:, 1, :], 1e-8, None, ALU.add).then_inc(vstep, 1)
                        dve.wait_ge(vstep, v + 2)
                        dve.reciprocal(vec[:, 3, :], vec[:, 2, :]).then_inc(vstep, 1)
                        dve.wait_ge(vstep, v + 3)
                        dve.tensor_scalar(vec[:, 4, :], vec[:, 3, :], gate, None, ALU.mult).then_inc(s_sum, 1)
                        dve.wait_ge(s_sum, b * NH + g + 2)
                        for i in range(4):
                            dve.wait_ge(y_ps, (b * NH + g) * 4 + i + 1)
                            xt = K.x[:, b * TB + 4 * g + i, :]
                            dve.scalar_tensor_tensor(xt, ps[:, 4 + i % 2, 0:D], vec[:, 4, i:i + 1], xt, ALU.mult,
                                                     ALU.add).then_inc(x_done, 1)


def expert_choice_ffn(nc, ctx, K, tag, layer, gw, sg, su, sd, wg_d, wu_d, wd_d, xn_dram, acc_dram):
    E, F = 16, 512
    CAP = S * 2 // E
    FT = F // P
    NS = B * S // 256
    W = 2 * P
    ps = K.ps
    ROUNDS = CAP // 8
    per_unit = [3, 3, 3, 3, 2, 2]
    assert sum(per_unit) == ROUNDS
    with ExitStack() as c:
        lg = sbuf(nc, c, tag + "lg", [P, NT, E])
        sc = sbuf(nc, c, tag + "sc", [P, TB, B, E])
        vec = sbuf(nc, c, tag + "vec", [P, 3, NT])
        va = [sbuf(nc, c, tag + f"va{i}", [B * E, S]) for i in range(2)]
        tw = sbuf(nc, c, tag + "tw", [B * E, CAP])
        ti = sbuf(nc, c, tag + "ti", [B * E, CAP], U32)
        tf = sbuf(nc, c, tag + "tf", [B * E, CAP])
        boff = sbuf(nc, c, tag + "boff", [B * E, 1])
        wcol = sbuf(nc, c, tag + "wcol", [P, B * E])
        idx = sbuf(nc, c, tag + "idx", [P, B * E], U32)
        wg = [sbuf(nc, c, tag + f"wg{i}", [P, KT, F]) for i in range(2)]
        wu = [sbuf(nc, c, tag + f"wu{i}", [P, KT, F]) for i in range(2)]
        wd = [sbuf(nc, c, tag + f"wd{i}", [P, FT, D]) for i in range(2)]
        xg = [sbuf(nc, c, tag + f"xg{i}", [P, B, D]) for i in range(2)]
        xgT = [sbuf(nc, c, tag + f"xgT{i}", [P, KT, W]) for i in range(2)]
        ge = [sbuf(nc, c, tag + f"ge{i}", [P, FT * W]) for i in range(2)]
        hT = [sbuf(nc, c, tag + f"hT{i}", [P, FT, W]) for i in range(2)]
        eo = [sbuf(nc, c, tag + f"eo{i}", [P, B, D]) for i in range(2)]
        acc = [sbuf(nc, c, tag + f"acc{i}", [P, 4, D]) for i in range(2)]
        (l_ps, smx, exp_in, exp_done, sc_rdy, v_ps, rnd, off, t_rdy, t_ps, i_rdy, xt_ps, xt_sb,
         g_ps, u_ps, ge_sb, h_sb, y_ps, y_sb, x_done, added) = semaphores(
            nc, c, tag, "l_ps smx exp_in exp_done sc_rdy v_ps rnd off t_rdy t_ps i_rdy xt_ps xt_sb "
            "g_ps u_ps ge_sb h_sb y_ps y_sb x_done added")
        w_in, d_in, out_dma, acc_in = (semaphores(nc, c, tag, f"{n}0 {n}1") for n in
                                       ("w_in", "d_in", "out_dma", "acc_in"))
        gat, scat = K.row_gathered, K.row_scattered
        gate = K.gate[:, 1, layer:layer + 1]
        with nc.Block() as block:
            @block.sync
            def _(sp):
                def store_shared(u, p):
                    sp.wait_ge(y_sb, u + 3)
                    for j in range(2):
                        sp.dma_start(acc_dram[bass.ds(u * W + j * P, P), :], eo[p][:, j, :]).then_inc(out_dma[p], 16)

                with sp.Fori(0, NS // 2) as pair:
                    u = 2 * pair
                    for p in range(2):
                        store_shared(u + p, p)
                with sp.Fori(0, E // 2) as pair:
                    e = 2 * pair
                    for p in range(2):
                        sp.wait_ge(u_ps, e + p + NS - 1)
                        sp.dma_start(wg[p][:, :, :], wg_d[e + p].rearrange("(k q) f -> q k f", q=P)).then_inc(w_in[p], 16)
                        sp.dma_start(wu[p][:, :, :], wu_d[e + p].rearrange("(k q) f -> q k f", q=P)).then_inc(w_in[p], 16)
                        sp.wait_ge(y_ps, e + p + NS + 1)
                        sp.dma_start(wd[p][:, :, :], wd_d[e + p].rearrange("(k q) f -> q k f", q=P)).then_inc(d_in[p], 16)
                sp.wait_ge(added, E + 2)
                for q in range(4):
                    if q >= 2:
                        sp.wait_ge(x_done, q - 1)
                    sp.dma_start(acc[q % 2][:, :, :],
                                 acc_dram[q * 512:(q + 1) * 512, :].rearrange("(t p) d -> p t d", p=P)).then_inc(acc_in[q % 2], 16)

            @block.gpsimd
            def _(pool):
                pool.memset(boff[:, :], float(S)).then_inc(off, 1)
                pool.wait_ge(off, 1)
                pool.affine_select(out=boff[:, :], in_=boff[:, :], compare_op=ALU.is_ge, fill=0.0, base=-E,
                                   pattern=[[0, 1]], channel_multiplier=1).then_inc(off, 1)

                def gather(e):
                    if e >= 2:
                        pool.wait_ge(xt_ps, e - 1)
                    for b in range(B):
                        n = b * E + e
                        pool.indirect_dma_start(xg[e % 2][:, b, :], None, xn_dram[:, :],
                                                bass.IndirectOffsetOnAxis(ap=idx[:, n:n + 1], axis=0)).then_inc(gat[e % 2], 16)

                pool.sem_inc(added, 2)
                pool.wait_ge(i_rdy, 2)
                gather(0)
                gather(1)
                for e in range(E):
                    if e == 0:
                        for q in range(2):
                            pool.wait_ge(out_dma[q], 32 + 32 * NS // 2)
                    else:
                        pool.wait_ge(scat[(e - 1) % 2], 32 * ((e - 1) // 2 + 1))
                        pool.sem_inc(added, 1)
                    pool.wait_ge(y_sb, NS + e + 3)
                    for b in range(B):
                        n = b * E + e
                        pool.indirect_dma_start(acc_dram[:, :], bass.IndirectOffsetOnAxis(ap=idx[:, n:n + 1], axis=0),
                                                eo[e % 2][:, b, :], None, compute_op=ALU.add).then_inc(scat[e % 2], 16)
                    if e + 2 < E:
                        gather(e + 2)
                pool.wait_ge(scat[(E - 1) % 2], 32 * (E // 2))
                pool.sem_inc(added, 1)

            def up(pe, n, p, g, u, rhs):
                pe.wait_ge(ge_sb, n + 1)
                for f in range(FT):
                    for k in range(KT):
                        m = pe.matmul(ps[:, f // 2, (f % 2) * W:(f % 2 + 1) * W], g[:, k, f * P:(f + 1) * P], rhs[k],
                                      start=(k == 0), stop=(k == KT - 1))
                m.then_inc(g_ps, 1)
                pe.wait_ge(h_sb, n + 2)
                for f in range(FT):
                    for k in range(KT):
                        m = pe.matmul(ps[:, 2 + f // 2, (f % 2) * W:(f % 2 + 1) * W], u[:, k, f * P:(f + 1) * P], rhs[k],
                                      start=(k == 0), stop=(k == KT - 1))
                m.then_inc(u_ps, 1)

            def down(pe, n, p, w):
                pe.wait_ge(h_sb, n + 3)
                pe.wait_ge(y_sb, n + 1)
                for j in range(2):
                    for f in range(FT):
                        m = pe.matmul(ps[:, 4 + p, j * D:(j + 1) * D], hT[p][:, f, j * P:(j + 1) * P], w[:, f, :],
                                      start=(f == 0), stop=(f == FT - 1))
                m.then_inc(y_ps, 1)

            @block.tensor
            def _(pe):
                for t in range(NT):
                    for k in range(KT):
                        m = pe.matmul(ps[:, 7, t * E:(t + 1) * E], K.xnT[:, k, t * P:(t + 1) * P], gw[:, k, :],
                                      start=(k == 0), stop=(k == KT - 1))
                m.then_inc(l_ps, 1)
                pe.sem_inc(y_ps, 2)
                pe.wait_ge(sc_rdy, 1)
                for i in range(TB):
                    m = pe.transpose(ps[0:B * E, 6 + i // 4, (i % 4) * P:(i % 4 + 1) * P],
                                     sc[:, i, :, :].rearrange("p b e -> p (b e)"), K.ident[:, :])
                m.then_inc(v_ps, 1)

                def shared_pair(u):
                    for p in range(2):
                        rhs = [K.xnT[:, k, bass.ds((u + p) * W, W)] for k in range(KT)]
                        up(pe, u + p, p, sg, su, rhs)
                    for p in range(2):
                        down(pe, u + p, p, sd)

                with pe.Fori(0, (NS - 2) // 2) as pair:
                    u = 2 * pair
                    shared_pair(u)
                pe.wait_ge(t_rdy, 1)
                pe.transpose(ps[:, 6, 0:B * E], tf[:, :], K.ident[0:B * E, 0:B * E])
                pe.transpose(ps[:, 6, 128:128 + B * E], tw[:, :], K.ident[0:B * E, 0:B * E]).then_inc(t_ps, 1)
                shared_pair(NS - 2)
                pe.wait_ge(i_rdy, 2)
                with pe.Fori(0, E // 2) as pair:
                    e = 2 * pair
                    for p in range(2):
                        pe.wait_ge(gat[p], 32 * pair + 32)
                        pe.wait_ge(xt_sb, e + p + 1)
                        for k in range(KT):
                            for b in range(B):
                                m = pe.transpose(ps[:, 6 + p, (k * B + b) * P:(k * B + b + 1) * P],
                                                 xg[p][:, b, k * P:(k + 1) * P], K.ident[:, :])
                        m.then_inc(xt_ps, 1)
                    for p in range(2):
                        pe.wait_ge(xt_sb, e + p + 3)
                        pe.wait_ge(w_in[p], 32 * pair + 32)
                        up(pe, e + p + NS, p, wg[p], wu[p], [xgT[p][:, k, :] for k in range(KT)])
                    for p in range(2):
                        pe.wait_ge(d_in[p], 16 * pair + 16)
                        down(pe, e + p + NS, p, wd[p])

            @block.scalar
            def _(act):
                def gelu(n, p):
                    act.wait_ge(g_ps, n + 1)
                    act.wait_ge(h_sb, n + 1)
                    act.activation(ge[p][:, :], ps[:, 0:2, :].rearrange("p a c -> p (a c)"), ACT.Gelu).then_inc(ge_sb, 1)

                act.sem_inc(ge_sb, 1)
                act.sem_inc(y_sb, 2)
                act.sem_inc(xt_sb, 2)
                act.wait_ge(exp_in, 1)
                act.activation(lg[:, :, :], lg[:, :, :], ACT.Exp).then_inc(exp_done, 1)
                with act.Fori(0, NS // 2) as pair:
                    u = 2 * pair
                    for p in range(2):
                        gelu(u + p, p)
                    for p in range(2):
                        act.wait_ge(y_ps, u + p + 3)
                        act.wait_ge(out_dma[p], 32 * pair + 32)
                        act.activation(eo[p][:, :, :].rearrange("p a c -> p (a c)"), ps[:, 4 + p, :],
                                       ACT.Copy).then_inc(y_sb, 1)
                with act.Fori(0, E // 2) as pair:
                    e = 2 * pair
                    for p in range(2):
                        act.wait_ge(xt_ps, e + p + 1)
                        act.wait_ge(u_ps, e + p + NS - 1)
                        act.activation(xgT[p][:, :, :].rearrange("p a c -> p (a c)"), ps[:, 6 + p, :],
                                       ACT.Copy).then_inc(xt_sb, 1)
                    for p in range(2):
                        gelu(e + p + NS, p)

            @block.vector
            def _(dve):
                dve.sem_inc(h_sb, 2)
                for p in range(2):
                    dve.sem_inc(out_dma[p], 32)
                s = Steps(smx)

                def then(ins):
                    s.did(ins)
                    dve.wait_ge(smx, s.last())

                dve.wait_ge(l_ps, 1)
                logits = ps[:, 7, 0:NT * E].rearrange("p (t e) -> p t e", t=NT)
                then(dve.tensor_reduce(vec[:, 0, :], logits, AX.X, ALU.max))
                dve.tensor_tensor(lg[:, :, :], logits, vec[:, 0, :].unsqueeze(2).broadcast_to([P, NT, E]),
                                  ALU.subtract).then_inc(exp_in, 1)
                dve.wait_ge(exp_done, 1)
                then(dve.tensor_reduce(vec[:, 1, :], lg[:, :, :], AX.X, ALU.add))
                then(dve.reciprocal(vec[:, 2, :], vec[:, 1, :]))
                dve.tensor_tensor(sc[:, :, :, :].rearrange("p i b e -> p b i e"),
                                  lg[:, :, :].rearrange("p (b i) e -> p b i e", b=B),
                                  vec[:, 2, :].rearrange("p (b i) -> p b i", b=B).unsqueeze(3).broadcast_to([P, B, TB, E]),
                                  ALU.mult).then_inc(sc_rdy, 1)
                dve.wait_ge(v_ps, 1)
                then(dve.tensor_copy(va[0][:, :], ps[0:B * E, 6:8, :].rearrange("p a c -> p (a c)")))

                def pick(r):
                    best = tw[:, 8 * r:8 * r + 8]
                    then(dve.max(best, va[r % 2][:, :]))
                    dve.max_index(ti[:, 8 * r:8 * r + 8], best, va[r % 2][:, :]).then_inc(rnd, 1)
                    then(dve.match_replace(va[1 - r % 2][:, :], best, va[r % 2][:, :], -1.0))

                def hidden(n, p):
                    dve.wait_ge(ge_sb, n + 2)
                    dve.wait_ge(u_ps, n + 1)
                    dve.wait_ge(y_ps, n + 1)
                    dve.tensor_tensor(hT[p][:, :, :].rearrange("p a c -> p (a c)"), ge[p][:, :],
                                      ps[:, 2:4, :].rearrange("p a c -> p (a c)"), ALU.mult).then_inc(h_sb, 1)

                r = 0
                for u in range(NS):
                    if u < len(per_unit):
                        for _ in range(per_unit[u]):
                            pick(r)
                            r += 1
                    hidden(u, u % 2)
                    if r == ROUNDS and u == len(per_unit) - 1:
                        dve.wait_ge(rnd, ROUNDS)
                        dve.wait_ge(off, 2)
                        dve.tensor_scalar(tf[:, :], ti[:, :], boff[:, 0:1], None, ALU.add).then_inc(t_rdy, 1)
                        dve.wait_ge(t_ps, 1)
                        dve.tensor_copy(idx[:, :], ps[:, 6, 0:B * E]).then_inc(i_rdy, 1)
                        dve.tensor_copy(wcol[:, :], ps[:, 6, 128:128 + B * E]).then_inc(i_rdy, 1)
                dve.wait_ge(i_rdy, 2)
                for p in range(2):
                    dve.wait_ge(out_dma[p], 32 + 32 * NS // 2)
                with dve.Fori(0, E // 2) as pair:
                    e = 2 * pair
                    for p in range(2):
                        hidden(e + p + NS, p)
                    for p in range(2):
                        dve.wait_ge(y_ps, e + p + NS + 3)
                        dve.wait_ge(added, e + p + 1)
                        for b in range(B):
                            m = dve.tensor_scalar(eo[p][:, b, :], ps[:, 4 + p, b * D:(b + 1) * D],
                                                  wcol[:, bass.ds(e + p + b * E, 1)], None, ALU.mult)
                        m.then_inc(y_sb, 1)
                for q in range(4):
                    dve.wait_ge(acc_in[q % 2], 16 * (q // 2 + 1))
                    xt = K.x[:, 4 * q:4 * q + 4, :]
                    dve.scalar_tensor_tensor(xt, acc[q % 2][:, :, :], gate, xt, ALU.mult, ALU.add).then_inc(x_done, 1)


def top2_ffn(nc, ctx, K, tag, layer, gw, w1, w3, w2, xs_dram, ys_dram, out):
    E, F, TOP = 8, 512, 2
    FT = F // P
    ps = K.ps
    NTILE = (TOP * B * S + E * (P - 1)) // P
    NTILE += NTILE % 2
    assert xs_dram.shape[0] == NTILE * P
    gate = K.gate[:, 1, layer:layer + 1]
    with ExitStack() as c:
        slot = sbuf(nc, c, tag + "slot", [P, TOP, NT], U32)
        gwt = sbuf(nc, c, tag + "gwt", [P, TOP, NT])
        te = sbuf(nc, c, tag + "te", [1, NTILE], I32)

        with ExitStack() as r:
            pr = sbuf(nc, r, tag + "pr", [P, NT, E])
            oh = sbuf(nc, r, tag + "oh", [P, TOP, NT, E])
            both = sbuf(nc, r, tag + "both", [P, NT, E])
            tmp = sbuf(nc, r, tag + "tmp", [P, 3, NT, E])
            vec = sbuf(nc, r, tag + "vec", [P, 8, NT])
            ev = sbuf(nc, r, tag + "ev", [P, 6, E])
            slf = sbuf(nc, r, tag + "slf", [P, TOP, NT])
            tri = sbuf(nc, r, tag + "tri", [P, P])
            rev_i = sbuf(nc, r, tag + "rev_i", [P, E], I32)
            rev = sbuf(nc, r, tag + "rev", [P, E])
            jrow_i = sbuf(nc, r, tag + "jrow_i", [1, NTILE], I32)
            jrow = sbuf(nc, r, tag + "jrow", [1, NTILE])
            cmp = sbuf(nc, r, tag + "cmp", [1, NTILE, E])
            cnt = sbuf(nc, r, tag + "cnt", [1, 2, NTILE])
            l_ps, step, exp_in, exp_done, const, oh_rdy, rank_ps, slot_rdy = semaphores(
                nc, r, tag, "l_ps step exp_in exp_done const oh_rdy rank_ps slot_rdy")
            sent = K.rows_sent
            with nc.Block() as block:
                @block.tensor
                def _(pe):
                    for t in range(NT):
                        for k in range(KT):
                            m = pe.matmul(ps[:, 0, t * E:(t + 1) * E], K.xnT[:, k, t * P:(t + 1) * P], gw[:, k, :],
                                          start=(k == 0), stop=(k == KT - 1))
                    m.then_inc(l_ps, 1)
                    pe.wait_ge(oh_rdy, 1)
                    pe.wait_ge(const, 3)
                    flat = both[:, :, :].rearrange("p t e -> p (t e)")
                    pe.matmul(ps[:, 1, 0:NT * E], tri[:, :], flat, start=True, stop=False, skip_group_check=True)
                    for n in range(1, NT):
                        pe.matmul(ps[:, 1, n * E:NT * E], K.ones[:, :], flat[:, 0:(NT - n) * E], start=False,
                                  stop=(n == NT - 1), skip_group_check=True)
                    pe.matmul(ps[:, 2, 0:NT * E], K.ones[:, :], flat, start=True, stop=True).then_inc(rank_ps, 1)

                @block.scalar
                def _(act):
                    act.wait_ge(exp_in, 1)
                    act.activation(pr[:, :, :], pr[:, :, :], ACT.Exp).then_inc(exp_done, 1)

                @block.gpsimd
                def _(pool):
                    pool.iota(rev_i[:, :], [[-1, E]], base=E, channel_multiplier=0).then_inc(const, 1)
                    pool.iota(jrow_i[:, :], [[1, NTILE]], base=0, channel_multiplier=0).then_inc(const, 1)
                    pool.affine_select(out=tri[:, :], in_=K.ones[:, :], compare_op=ALU.is_ge, fill=0.0, base=-1,
                                       pattern=[[1, P]], channel_multiplier=-1).then_inc(const, 1)
                    pool.wait_ge(slot_rdy, 1)
                    for t in range(NT):
                        for n in range(TOP):
                            pool.indirect_dma_start(xs_dram[:, :], bass.IndirectOffsetOnAxis(ap=slot[:, n, t:t + 1], axis=0),
                                                    K.xn[:, t, :], None).then_inc(sent, 16)
                    pool.wait_ge(sent, 16 * TOP * NT)

                @block.vector
                def _(dve):
                    s = Steps(step)

                    def then(ins):
                        s.did(ins)
                        dve.wait_ge(step, s.last())

                    def wide(v):
                        return v.unsqueeze(2).broadcast_to([P, NT, E])

                    def per_expert(v):
                        return v.unsqueeze(1).broadcast_to([P, NT, E])

                    dve.wait_ge(const, 2)
                    then(dve.tensor_copy(rev[:, :], rev_i[:, :]))
                    then(dve.tensor_copy(jrow[:, :], jrow_i[:, :]))
                    dve.wait_ge(l_ps, 1)
                    logits = ps[:, 0, 0:NT * E].rearrange("p (t e) -> p t e", t=NT)
                    then(dve.tensor_reduce(vec[:, 0, :], logits, AX.X, ALU.max))
                    dve.tensor_tensor(pr[:, :, :], logits, wide(vec[:, 0, :]), ALU.subtract).then_inc(exp_in, 1)
                    dve.wait_ge(exp_done, 1)
                    then(dve.tensor_reduce(vec[:, 1, :], pr[:, :, :], AX.X, ALU.add))
                    then(dve.reciprocal(vec[:, 2, :], vec[:, 1, :]))
                    then(dve.tensor_tensor(pr[:, :, :], pr[:, :, :], wide(vec[:, 2, :]), ALU.mult))
                    src = pr
                    for n in range(TOP):
                        best = vec[:, 3 + n, :]
                        then(dve.tensor_reduce(best, src[:, :, :], AX.X, ALU.max))
                        then(dve.tensor_tensor(tmp[:, 0, :, :], src[:, :, :], wide(best), ALU.is_equal))
                        then(dve.tensor_tensor(tmp[:, 1, :, :], tmp[:, 0, :, :], per_expert(rev[:, :]), ALU.mult))
                        then(dve.tensor_reduce(vec[:, 5, :], tmp[:, 1, :, :], AX.X, ALU.max))
                        then(dve.tensor_tensor(oh[:, n, :, :], tmp[:, 1, :, :], wide(vec[:, 5, :]), ALU.is_equal))
                        if n == 0:
                            then(dve.scalar_tensor_tensor(tmp[:, 2, :, :], oh[:, 0, :, :], -2.0, pr[:, :, :],
                                                          ALU.mult, ALU.add))
                            src = tmp[:, 2, :, :]
                    dve.tensor_tensor(both[:, :, :], oh[:, 0, :, :], oh[:, 1, :, :], ALU.add).then_inc(oh_rdy, 1)
                    then(dve.tensor_tensor(vec[:, 6, :], vec[:, 3, :], vec[:, 4, :], ALU.add))
                    then(dve.reciprocal(vec[:, 7, :], vec[:, 6, :]))
                    then(dve.tensor_scalar(vec[:, 7, :], vec[:, 7, :], gate, None, ALU.mult))
                    for n in range(TOP):
                        s.did(dve.tensor_tensor(gwt[:, n, :], vec[:, 3 + n, :], vec[:, 7, :], ALU.mult))
                    dve.wait_ge(rank_ps, 1)
                    then(dve.tensor_reduce(ev[:, 0, :], ps[:, 2, 0:NT * E].rearrange("p (t e) -> p e t", t=NT), AX.X, ALU.add))
                    then(dve.tensor_scalar(ev[:, 1, :], ev[:, 0, :], 1.0 / P, (P - 1.0) / (2 * P), ALU.mult, ALU.add))
                    then(dve.tensor_scalar(ev[:, 2, :], ev[:, 1, :], MAGIC, MAGIC, ALU.add, ALU.subtract))
                    then(dve.tensor_tensor_scan(ev[:, 3, :], K.ones[:, 0:E], ev[:, 2, :], 0.0, ALU.mult, ALU.add))
                    then(dve.tensor_tensor(ev[:, 4, :], ev[:, 3, :], ev[:, 2, :], ALU.subtract))
                    then(dve.scalar_tensor_tensor(tmp[:, 0, :, :], per_expert(ev[:, 4, :]), float(P),
                                                  ps[:, 1, 0:NT * E].rearrange("p (t e) -> p t e", t=NT),
                                                  ALU.mult, ALU.add))
                    for n in range(TOP):
                        then(dve.tensor_tensor(tmp[:, 1, :, :], oh[:, n, :, :], tmp[:, 0, :, :], ALU.mult))
                        then(dve.tensor_reduce(slf[:, n, :], tmp[:, 1, :, :], AX.X, ALU.add))
                    dve.tensor_copy(slot[:, :, :], slf[:, :, :]).then_inc(slot_rdy, 1)
                    then(dve.tensor_tensor(cmp[:, :, :], ev[0:1, 3, :].unsqueeze(1).broadcast_to([1, NTILE, E]),
                                           jrow[:, :].unsqueeze(2).broadcast_to([1, NTILE, E]), ALU.is_le))
                    then(dve.tensor_reduce(cnt[:, 0, :], cmp[:, :, :], AX.X, ALU.add))
                    then(dve.tensor_scalar(te[:, :], cnt[:, 0, :], E - 1.0, None, ALU.min))

        with ExitStack() as r:
            xs = [sbuf(nc, r, tag + f"xs{i}", [P, D]) for i in range(2)]
            xsT = [sbuf(nc, r, tag + f"xsT{i}", [P, KT * P]) for i in range(2)]
            s1 = [sbuf(nc, r, tag + f"s1{i}", [P, F]) for i in range(2)]
            hid = [sbuf(nc, r, tag + f"hid{i}", [P, F]) for i in range(2)]
            hT = [sbuf(nc, r, tag + f"hT{i}", [P, F]) for i in range(2)]
            yo = [sbuf(nc, r, tag + f"yo{i}", [P, D]) for i in range(2)]
            xt_ps, xt_sb, h1_ps, up_ps, silu, h_sb, ht_ps, ht_sb, y_ps, y_sb = semaphores(
                nc, r, tag, "xt_ps xt_sb h1_ps up_ps silu h_sb ht_ps ht_sb y_ps y_sb")
            x_in = semaphores(nc, r, tag, "x_in0 x_in1")
            y_out = semaphores(nc, r, tag, "y_out0 y_out1")
            with nc.Block() as block:
                @block.sync
                def _(sp):
                    for p in range(2):
                        sp.sem_inc(y_out[p], 16)

                    def load(j, p):
                        sp.wait_ge(xt_ps, j + 1)
                        sp.dma_start(xs[p][:, :], xs_dram[bass.ds(j * P, P), :]).then_inc(x_in[p], 16)

                    def store(j, p):
                        sp.wait_ge(y_sb, j + 2)
                        sp.dma_start(ys_dram[bass.ds(j * P, P), :], yo[p][:, :]).then_inc(y_out[p], 16)

                    for p in range(2):
                        load(p, p)
                    with sp.Fori(0, NTILE // 2 - 1) as pair:
                        for p in range(2):
                            load(2 * pair + p + 2, p)
                        for p in range(2):
                            store(2 * pair + p, p)
                    for p in range(2):
                        store(NTILE - 2 + p, p)
                    for p in range(2):
                        sp.wait_ge(y_out[p], 16 * (NTILE // 2) + 16)

                @block.tensor
                def _(pe):
                    for sem in (xt_ps, up_ps, ht_ps, y_ps):
                        pe.sem_inc(sem, 2)
                    with pe.Fori(0, NTILE // 2) as pair:
                        for p in range(2):
                            j = 2 * pair + p
                            pe.wait_ge(x_in[p], 16 * pair + 16)
                            pe.wait_ge(xt_sb, j + 1)
                            for k in range(KT):
                                m = pe.transpose(ps[:, 6 + p, k * P:(k + 1) * P], xs[p][:, k * P:(k + 1) * P], K.ident[:, :])
                            m.then_inc(xt_ps, 1)
                        expert = []
                        for p in range(2):
                            j = 2 * pair + p
                            e = pe.value_load(te[0:1, bass.ds(j, 1)], min_val=0, max_val=E - 1)
                            expert.append(e)
                            pe.wait_ge(xt_sb, j + 3)
                            pe.wait_ge(h_sb, j + 1)
                            for n, w in enumerate((w1, w3)):
                                for k in range(KT):
                                    m = pe.matmul(ps[:, 2 * p + n, :], xsT[p][:, k * P:(k + 1) * P], w[:, e, k, :],
                                                  start=(k == 0), stop=(k == KT - 1))
                                m.then_inc((h1_ps, up_ps)[n], 1)
                        for p in range(2):
                            j = 2 * pair + p
                            pe.wait_ge(h_sb, j + 3)
                            pe.wait_ge(ht_sb, j + 1)
                            for f in range(FT):
                                m = pe.transpose(ps[:, 4, f * P:(f + 1) * P], hid[p][:, f * P:(f + 1) * P], K.ident[:, :])
                            m.then_inc(ht_ps, 1)
                            pe.wait_ge(ht_sb, j + 2)
                            pe.wait_ge(y_sb, j + 1)
                            for f in range(FT):
                                m = pe.matmul(ps[:, 5, 0:D], hT[p][:, f * P:(f + 1) * P], w2[:, expert[p], f, :],
                                              start=(f == 0), stop=(f == FT - 1))
                            m.then_inc(y_ps, 1)

                @block.scalar
                def _(act):
                    act.sem_inc(xt_sb, 2)
                    with act.Fori(0, NTILE // 2) as pair:
                        for p in range(2):
                            j = 2 * pair + p
                            act.wait_ge(xt_ps, j + 3)
                            act.wait_ge(up_ps, j + 1)
                            act.activation(xsT[p][:, :], ps[:, 6 + p, 0:KT * P], ACT.Copy).then_inc(xt_sb, 1)
                        for p in range(2):
                            j = 2 * pair + p
                            act.wait_ge(h1_ps, j + 1)
                            act.wait_ge(h_sb, j + 1)
                            act.activation(s1[p][:, :], ps[:, 2 * p, :], ACT.Silu).then_inc(silu, 1)

                @block.vector
                def _(dve):
                    dve.sem_inc(h_sb, 2)
                    dve.sem_inc(ht_sb, 1)
                    dve.sem_inc(y_sb, 1)
                    with dve.Fori(0, NTILE // 2) as pair:
                        for p in range(2):
                            j = 2 * pair + p
                            dve.wait_ge(silu, j + 1)
                            dve.wait_ge(up_ps, j + 3)
                            dve.wait_ge(ht_ps, j + 1)
                            dve.tensor_tensor(hid[p][:, :], s1[p][:, :], ps[:, 2 * p + 1, :], ALU.mult).then_inc(h_sb, 1)
                        for p in range(2):
                            j = 2 * pair + p
                            dve.wait_ge(ht_ps, j + 3)
                            dve.wait_ge(y_ps, j + 1)
                            dve.tensor_copy(hT[p][:, :], ps[:, 4, :]).then_inc(ht_sb, 1)
                            dve.wait_ge(y_ps, j + 3)
                            dve.wait_ge(y_out[p], 16 * pair + 16)
                            dve.tensor_copy(yo[p][:, :], ps[:, 5, 0:D]).then_inc(y_sb, 1)

        with ExitStack() as r:
            RING = 4
            yg = [[sbuf(nc, r, tag + f"yg{i}{n}", [P, D]) for n in range(TOP)] for i in range(RING)]
            got = K.rows_back
            x_mid, x_done, stored = semaphores(nc, r, tag, "x_mid x_fin stored")
            with nc.Block() as block:
                @block.gpsimd
                def _(pool):
                    for t in range(NT):
                        if t >= RING:
                            pool.wait_ge(x_done, t - RING + 1)
                        for n in range(TOP):
                            pool.indirect_dma_start(yg[t % RING][n][:, :], None, ys_dram[:, :],
                                                    bass.IndirectOffsetOnAxis(ap=slot[:, n, t:t + 1], axis=0)).then_inc(got[t % RING], 16)

                @block.vector
                def _(dve):
                    for t in range(NT):
                        dve.wait_ge(got[t % RING], 32 * (t // RING + 1))
                        xt = K.x[:, t, :]
                        dve.scalar_tensor_tensor(xt, yg[t % RING][0][:, :], gwt[:, 0, t:t + 1], xt, ALU.mult,
                                                 ALU.add).then_inc(x_mid, 1)
                        dve.wait_ge(x_mid, t + 1)
                        dve.scalar_tensor_tensor(xt, yg[t % RING][1][:, :], gwt[:, 1, t:t + 1], xt, ALU.mult,
                                                 ALU.add).then_inc(x_done, 1)

                @block.sync
                def _(sp):
                    rows = out.rearrange("b (t p) d -> p (b t) d", p=P)
                    for q in range(4):
                        sp.wait_ge(x_done, 4 * q + 4)
                        sp.dma_start(rows[:, 4 * q:4 * q + 4, :], K.x[:, 4 * q:4 * q + 4, :]).then_inc(stored, 16)
                    sp.wait_ge(stored, 64)


def store_result(nc, ctx, K, out):
    (s_st,) = semaphores(nc, ctx, "store_", "dma")
    with nc.Block() as block:
        @block.sync
        def _(sp):
            sp.dma_start(out.rearrange("b (t p) d -> p (b t) d", p=P), K.x[:, :, :]).then_inc(s_st, 16)
            sp.wait_ge(s_st, 16)


def flamingo(nc, ins, out):
    K = Core()
    with ExitStack() as ctx:
        load_and_constants(nc, ctx, K, ins)
        K.row_gathered = software_dma_semaphores(nc, ctx, "row_gathered", "0 1")
        K.row_scattered = software_dma_semaphores(nc, ctx, "row_scattered", "0 1")
        (K.rows_sent,) = software_dma_semaphores(nc, ctx, "rows_", "sent")
        K.rows_back = software_dma_semaphores(nc, ctx, "rows_back", "0 1 2 3")

        def stage(n):
            sub = ExitStack()
            return sub, Weights(nc, sub, ins)

        def transposed_rows(sub):
            K.xnT = sbuf(nc, sub, "xnT_sb", [P, KT, B * S])

        if 0 in _STAGES:
            sub, w = stage(0)
            with sub:
                transposed_rows(sub)
                wq, wk, wv, wo = (w.rows("L0_xattn_W" + n) for n in "qkvo")
                bq, bk = w.same("L0_xattn_bq"), w.same("L0_xattn_bk")
                bv, bo = w.repeated("L0_xattn_bv", L), w.repeated("L0_xattn_bo")
                norm_block(nc, sub, K, "n0_", w.loads)
                multihead(nc, sub, K, "a0_", 0, wq, wk, wv, wo, bq, bk, bv, bo, mask=ins["mask_1x1xSxS2_ik0"])
        if 1 in _STAGES:
            sub, w = stage(1)
            with sub:
                transposed_rows(sub)
                gw, sg, su, sd = (w.rows("L0_ffn_" + n) for n in ("gate_w", "Ws_g", "Ws_u", "Ws_d"))
                xn_dram = nc.dram_tensor("xn_rows_1", (B * S, D), F32, kind="Internal").ap()
                acc_dram = nc.dram_tensor("acc_rows_1", (B * S, D), F32, kind="Internal").ap()
                norm_block(nc, sub, K, "n1_", w.loads, to_dram=xn_dram)
                expert_choice_ffn(nc, sub, K, "f1_", 0, gw, sg, su, sd, ins["L0_ffn_Wg"], ins["L0_ffn_Wu"],
                                  ins["L0_ffn_Wd"], xn_dram, acc_dram)
        if 2 in _STAGES:
            sub, w = stage(2)
            with sub:
                transposed_rows(sub)
                wq, wk, wv = w.same("L1_xattn_Wq"), w.rows("L1_xattn_Wk"), w.rows("L1_xattn_Wv")
                bq, bk, bv = w.same("L1_xattn_bq"), w.same("L1_xattn_bk"), w.repeated("L1_xattn_bv", L)
                norm_block(nc, sub, K, "n2_", w.loads)
                sigmoid_attention(nc, sub, K, "a2_", 1, wq, wk, wv, bq, bk, bv)
        if 3 in _STAGES:
            sub, w = stage(3)
            with sub:
                w1, w2 = w.rows("L1_ffn_w1"), w.rows("L1_ffn_w2")
                cw, cb = w.same("L1_ffn_conv_w"), w.same("L1_ffn_conv_b")
                norm_block(nc, sub, K, "n3_", w.loads, transposed=False)
                bitnet_ffn(nc, sub, K, "f3_", 1, w1, w2, cw, cb)
        clear_semaphores(nc)
        if 4 in _STAGES:
            sub, w = stage(4)
            with sub:
                transposed_rows(sub)
                wT, wn, bc = w.rows("L2_xattn_W"), w.rows("L2_xattn_Wn"), w.same("L2_xattn_b")
                norm_block(nc, sub, K, "n4_", w.loads)
                align_attention(nc, sub, K, "a4_", 2, wT, wn, bc)
        if 5 in _STAGES:
            sub, w = stage(5)
            with sub:
                transposed_rows(sub)
                wu, wd = w.rows("L2_ffn_w_up"), w.rows("L2_ffn_w_down")
                norm_block(nc, sub, K, "n5_", w.loads, ternary=True)
                ternary_ffn(nc, sub, K, "f5_", 2, wu, wd)
        if 6 in _STAGES:
            sub, w = stage(6)
            with sub:
                transposed_rows(sub)
                wq, wk, wv, wo = (w.rows("L3_xattn_w_" + n) for n in "qkvo")
                norm_block(nc, sub, K, "n6_", w.loads)
                multihead(nc, sub, K, "a6_", 3, wq, wk, wv, wo)
        if 7 in _STAGES:
            sub, w = stage(7)
            with sub:
                transposed_rows(sub)
                NS_ROWS = 40 * P
                gw = w.rows("L3_ffn_wg")
                w1, w3, w2 = (w.experts("L3_ffn_" + n) for n in ("w1", "w3", "w2"))
                xs_dram = nc.dram_tensor("xs_rows_7", (NS_ROWS, D), F32, kind="Internal").ap()
                ys_dram = nc.dram_tensor("ys_rows_7", (NS_ROWS, D), F32, kind="Internal").ap()
                for n in range(NS_ROWS // 512):
                    w.loads.append((xs_dram[n * 512:(n + 1) * 512, :].rearrange("(a p) d -> p a d", p=P),
                                    K.zeros[:, :].unsqueeze(1).broadcast_to([P, 4, D])))
                norm_block(nc, sub, K, "n7_", w.loads)
                top2_ffn(nc, sub, K, "f7_", 3, gw, w1, w3, w2, xs_dram, ys_dram, out)
        else:
            store_result(nc, ctx, K, out)


def kernel(**inputs):
    import concourse.bacc as _bacc
    from concourse.bass_utils import run_bass_kernel_spmd as _run

    nc = _bacc.Bacc("TRN2", target_bir_lowering=False, num_devices=1)

    def laid(name):
        a = np.asarray(inputs[name])
        if name in _FLIP:
            a = np.swapaxes(a, -1, -2)
        if name == "L1_ffn_conv_w":
            a = a.reshape(8, P, 3).transpose(1, 0, 2)
        if name in ("L1_xattn_bq", "L1_xattn_bk"):
            a = a.reshape(64, 1)
        if name in _COLUMNS:
            a = a.reshape(-1, P).T
        if name == "mask_1x1xSxS2_ik0":
            a = a.reshape(S, L)
        return np.ascontiguousarray(a)

    arrays = {n: laid(n) for n in _NAMES}
    arrays["L2_xattn_Wn"] = np.ascontiguousarray(np.asarray(inputs["L2_xattn_W"]))
    arrays["gates"] = np.stack([np.asarray(inputs["g_xattn"]), np.asarray(inputs["g_ffn"])])
    aps = {n: nc.dram_tensor("in_" + n, a.shape, mybir.dt.from_np(a.dtype), kind="ExternalInput").ap()
           for n, a in arrays.items()}
    out = nc.dram_tensor("out_x", (B, S, D), F32, kind="ExternalOutput").ap()
    flamingo(nc, aps, out)
    r = _run(nc, [{"in_" + n: a for n, a in arrays.items()}], core_ids=[0])
    return r.results[0]["out_x"]


_COLUMNS = ("L0_xattn_bq", "L0_xattn_bk", "L1_ffn_conv_b", "L2_xattn_b")
_FLIP = ("L3_ffn_wg", "L3_ffn_w1", "L3_ffn_w3", "L3_ffn_w2", "L0_ffn_gate_w", "L0_ffn_Ws_g", "L0_ffn_Ws_u", "L0_ffn_Ws_d", "L0_ffn_Wg", "L0_ffn_Wu", "L0_ffn_Wd",
         "L0_xattn_Wq", "L0_xattn_Wk", "L0_xattn_Wv", "L0_xattn_Wo", "L1_xattn_Wk", "L1_xattn_Wv",
         "L1_ffn_w1", "L1_ffn_w2", "L2_xattn_W", "L2_ffn_w_up", "L2_ffn_w_down",
         "L3_xattn_w_q", "L3_xattn_w_k", "L3_xattn_w_v", "L3_xattn_w_o")
_NAMES = ("x", "ctx_1024", "mask_1x1xSxS2_ik0", "L0_xattn_bv", "L0_xattn_bo", "L1_xattn_Wq",
          "L1_xattn_bq", "L1_xattn_bk", "L1_xattn_bv", "L1_ffn_conv_w") + _COLUMNS + _FLIP
```

```python
from contextlib import ExitStack

import numpy as np

import concourse.bass as bass
from concourse import mybir

F32 = mybir.dt.float32
F32R = mybir.dt.float32r
BF16 = mybir.dt.bfloat16
I32 = mybir.dt.int32
U32 = mybir.dt.uint32
ALU = mybir.AluOpType
ACT = mybir.ActivationFunctionType
AX = mybir.AxisListType

P = 128
B, S, D = 2, 1024, 256
NT = B * S // P
TB = S // P
KT = D // P
L = 77
H, HD = 16, 16
LN_EPS = 1e-5
MAGIC = 1.5 * 2.0 ** 23

_STAGES = tuple(range(8))


_used = {}
_made = []


class Steps:

    def __init__(self, sem, base=0):
        self.sem, self.base, self.n = sem, base, 0

    def did(self, ins):
        self.n += 1
        return ins.then_inc(self.sem, 1)

    def last(self):
        return self.base + self.n


class Core:
    pass


def sbuf(nc, ctx, name, shape, dt=F32):
    _used[name] = _used.get(name, 0) + 1
    name = f"{name}_{_used[name]}"
    return ctx.enter_context(nc.sbuf_tensor(name, shape, dt))


def semaphores(nc, ctx, prefix, names):
    made = [ctx.enter_context(nc.semaphore(prefix + n)) for n in names.split()]
    _made.extend(made)
    return made


def software_dma_semaphores(nc, ctx, prefix, names):
    return [ctx.enter_context(nc.semaphore(prefix + n)) for n in names.split()]


def clear_semaphores(nc):
    with nc.Block() as block:
        @block.gpsimd
        def _(pool):
            for sem in _made:
                pool.sem_clear(sem)
    _made.clear()


def load_and_constants(nc, ctx, K, ins):
    K.ps = ctx.enter_context(nc.psum_tensor("ps", [P, 8, 512], F32))
    K.x = sbuf(nc, ctx, "x_sb", [P, NT, D])
    K.xn = sbuf(nc, ctx, "xn_sb", [P, NT, D])
    K.ident = sbuf(nc, ctx, "ident", [P, P])
    K.identb = sbuf(nc, ctx, "identb", [P, P], BF16)
    K.zeros = sbuf(nc, ctx, "zeros", [P, D])
    K.ones = sbuf(nc, ctx, "ones", [P, P])
    K.shift = sbuf(nc, ctx, "shift", [P, 336])
    K.headmask = sbuf(nc, ctx, "headmask", [P, 8])
    K.npow = sbuf(nc, ctx, "npow", [P, NT])
    K.hpow = sbuf(nc, ctx, "hpow", [P, NT])
    K.gate = sbuf(nc, ctx, "gates", [P, 2, 4])
    K.ctx_nat = sbuf(nc, ctx, "ctx_nat", [L, B, D])
    K.ctxT = sbuf(nc, ctx, "ctxT", [P, KT, B * L])
    K.st = sbuf(nc, ctx, "bn_st", [P, NT, 6])
    K.nv = sbuf(nc, ctx, "norm_vec", [P, 10, NT])
    K.rg = [sbuf(nc, ctx, f"row_gather{i}", [P, 2, 1], I32) for i in range(2)]
    s_const, s_ctx, s_tr, s_dve = semaphores(nc, ctx, "load_", "const ctx tr dve")
    with nc.Block() as block:
        @block.sync
        def _(sp):
            sp.dma_start(K.ctx_nat[:, :, :], ins["ctx_1024"].rearrange("b k d -> k b d")).then_inc(s_ctx, 16)
            sp.dma_start(K.gate[:, :, :], ins["gates"].partition_broadcast(P)).then_inc(s_ctx, 16)
            sp.dma_start(K.x[:, :, :], ins["x"].rearrange("b (t p) d -> p (b t) d", p=P)).then_inc(s_ctx, 16)
            sp.wait_ge(s_ctx, 48)

        @block.gpsimd
        def _(pool):
            pool.memset(K.ident[:, :], 0.0).then_inc(s_const, 1)
            pool.memset(K.shift[:, :], 0.0).then_inc(s_const, 1)
            pool.memset(K.headmask[:, :], HD ** -0.5).then_inc(s_const, 1)
            pool.memset(K.ones[:, :], 1.0).then_inc(s_const, 1)
            pool.memset(K.npow[:, :], -0.5).then_inc(s_const, 1)
            pool.memset(K.hpow[:, :], 0.5).then_inc(s_const, 1)
            pool.memset(K.zeros[:, :], 0.0).then_inc(s_const, 1)
            pool.wait_ge(s_const, 7)
            pool.affine_select(out=K.ident[:, :], in_=K.ident[:, :], compare_op=ALU.not_equal, fill=1.0, base=0,
                               pattern=[[-1, P]], channel_multiplier=1).then_inc(s_const, 1)
            pool.affine_select(out=K.shift[:, :], in_=K.shift[:, :], compare_op=ALU.not_equal, fill=1.0, base=P,
                               pattern=[[-1, 336]], channel_multiplier=1).then_inc(s_const, 1)
            pool.affine_select(out=K.headmask[:, :], in_=K.headmask[:, :], compare_op=ALU.is_ge, fill=0.0, base=0,
                               pattern=[[-HD, 8]], channel_multiplier=1).then_inc(s_const, 1)
            pool.wait_ge(s_const, 10)
            pool.affine_select(out=K.headmask[:, :], in_=K.headmask[:, :], compare_op=ALU.is_ge, fill=0.0,
                               base=HD - 1, pattern=[[HD, 8]], channel_multiplier=-1).then_inc(s_const, 1)

        @block.tensor
        def _(pe):
            pe.wait_ge(s_const, 8)
            pe.wait_ge(s_ctx, 48)
            for b in range(B):
                for k in range(KT):
                    m = pe.transpose(K.ps[:, 0, (k * B + b) * L:(k * B + b + 1) * L],
                                     K.ctx_nat[:, b, k * P:(k + 1) * P], K.ident[0:L, 0:L])
            m.then_inc(s_tr, 1)

        @block.scalar
        def _(act):
            act.wait_ge(s_ctx, 48)
            act.activation(K.gate[:, :, :], K.gate[:, :, :], ACT.Tanh).then_inc(s_dve, 1)

        @block.vector
        def _(dve):
            dve.wait_ge(s_const, 8)
            dve.tensor_copy(K.identb[:, :], K.ident[:, :]).then_inc(s_dve, 1)
            dve.wait_ge(s_tr, 1)
            dve.tensor_copy(K.ctxT[:, :, :].rearrange("p k c -> p (k c)"), K.ps[:, 0, 0:KT * B * L]).then_inc(s_dve, 1)


class Weights:

    def __init__(self, nc, ctx, ins):
        self.nc, self.ctx, self.ins, self.loads = nc, ctx, ins, []

    def add(self, name, shape, src):
        t = sbuf(self.nc, self.ctx, "w_" + name, shape)
        self.loads.append((t[tuple([slice(None)] * len(shape))], src))
        return t

    def rows(self, name):
        src = self.ins[name].rearrange("(k p) o -> p k o", p=P)
        return self.add(name, list(src.shape), src)

    def experts(self, name):
        src = self.ins[name].rearrange("e (k p) o -> p e k o", p=P)
        t = sbuf(self.nc, self.ctx, "w_" + name, list(src.shape))
        for e in range(src.shape[1]):
            self.loads.append((t[:, e, :, :], src[:, e, :, :]))
        return t

    def same(self, name):
        return self.add(name, list(self.ins[name].shape), self.ins[name])

    def repeated(self, name, n=P):
        return self.add(name, [n, self.ins[name].shape[0]], self.ins[name].partition_broadcast(n))


class Norm:

    def __init__(self, nc, ctx, K, tag, loads, ternary=False, to_dram=None, prefetch=(), banks=8):
        self.K, self.loads, self.ternary, self.to_dram, self.prefetch = K, loads, ternary, to_dram, prefetch
        self.banks = banks
        self.s_stat, self.s_vec, self.s_pow, self.rows, self.s_tr, self.turned, self.s_out, self.loaded = semaphores(
            nc, ctx, tag, "stat vec pow rows tr turned out weights")
        self.all_loaded = 16 * len(loads)

    def vector(self, dve):
        K, nv, st, s_vec = self.K, self.K.nv, self.K.st, self.s_vec
        with dve.Fori(0, NT) as t:
            dve.bn_stats(st[:, t, :], K.x[:, t, :]).then_inc(self.s_stat, 1)
        dve.wait_ge(self.s_stat, NT)
        v = Steps(s_vec)
        v.did(dve.tensor_tensor(nv[:, 0, :], st[:, :, 1], st[:, :, 4], ALU.add))
        v.did(dve.tensor_tensor(nv[:, 1, :], st[:, :, 1], st[:, :, 4], ALU.subtract))
        v.did(dve.tensor_tensor(nv[:, 2, :], st[:, :, 2], st[:, :, 5], ALU.add))
        dve.wait_ge(s_vec, v.last())
        v.did(dve.tensor_scalar(nv[:, 3, :], nv[:, 0, :], 0.5, None, ALU.mult))
        v.did(dve.tensor_tensor(nv[:, 4, :], nv[:, 1, :], nv[:, 1, :], ALU.mult))
        dve.wait_ge(s_vec, v.last())
        v.did(dve.scalar_tensor_tensor(nv[:, 5, :], nv[:, 4, :], D / 4.0, nv[:, 2, :], ALU.mult, ALU.add))
        dve.wait_ge(s_vec, v.last())
        v.did(dve.tensor_scalar(nv[:, 6, :], nv[:, 5, :], 1.0 / D, LN_EPS, ALU.mult, ALU.add))
        dve.wait_ge(self.s_pow, 1)
        scale = nv[:, 7, :]
        if self.ternary:
            v.did(dve.tensor_scalar(nv[:, 8, :], nv[:, 5, :], 1.0 / D, None, ALU.mult))
            v.did(dve.tensor_tensor(nv[:, 0, :], nv[:, 7, :], nv[:, 7, :], ALU.mult))
            dve.wait_ge(s_vec, v.last())
            v.did(dve.tensor_tensor(nv[:, 8, :], nv[:, 8, :], nv[:, 0, :], ALU.mult))
            dve.wait_ge(self.s_pow, 2)
            v.did(dve.tensor_scalar(nv[:, 0, :], nv[:, 9, :], 1e-8, None, ALU.add))
            dve.wait_ge(s_vec, v.last())
            v.did(dve.reciprocal(nv[:, 1, :], nv[:, 0, :]))
            dve.wait_ge(s_vec, v.last())
            v.did(dve.tensor_tensor(nv[:, 8, :], nv[:, 1, :], nv[:, 7, :], ALU.mult))
            dve.wait_ge(s_vec, v.last())
            scale = nv[:, 8, :]
        with dve.Fori(0, NT) as t:
            dve.tensor_scalar(K.xn[:, t, :], K.x[:, t, :], nv[:, 3, bass.ds(t, 1)], scale[:, bass.ds(t, 1)],
                              ALU.subtract, ALU.mult).then_inc(self.rows, 1)

    def gpsimd(self, pool):
        nv = self.K.nv
        pool.wait_ge(self.s_vec, 7)
        pool.tensor_tensor(nv[:, 7, :], nv[:, 6, :], self.K.npow[:, :], ALU.pow).then_inc(self.s_pow, 1)
        if self.ternary:
            pool.wait_ge(self.s_vec, 10)
            pool.tensor_tensor(nv[:, 9, :], nv[:, 8, :], self.K.hpow[:, :], ALU.pow).then_inc(self.s_pow, 1)

    def sync(self, sp):
        for dst, src in self.loads:
            sp.dma_start(dst, src).then_inc(self.loaded, 16)
        for dst, src in self.prefetch:
            sp.dma_start(dst, src).then_inc(self.K.experts_in, 16)
        if self.to_dram is not None:
            for q in range(4):
                sp.wait_ge(self.rows, 4 * (q + 1))
                sp.dma_start(self.to_dram[q * 512:(q + 1) * 512, :].rearrange("(t p) d -> p t d", p=P),
                             self.K.xn[:, 4 * q:4 * q + 4, :]).then_inc(self.s_out, 16)
            sp.wait_ge(self.s_out, 64)
        if self.loads:
            sp.wait_ge(self.loaded, self.all_loaded)

    def tensor(self, pe):
        K = self.K
        for t in range(NT):
            u = t // 2
            pe.wait_ge(self.rows, t + 1)
            if t % 2 == 0 and u >= self.banks:
                pe.wait_ge(self.turned, u - self.banks + 1)
            for k in range(KT):
                m = pe.transpose(K.ps[:, u % self.banks, (2 * k + t % 2) * P:(2 * k + t % 2 + 1) * P],
                                 K.xn[:, t, k * P:(k + 1) * P], K.ident[:, :])
            if t % 2:
                m.then_inc(self.s_tr, 1)

    def scalar(self, act):
        K = self.K
        for u in range(NT // 2):
            act.wait_ge(self.s_tr, u + 1)
            act.activation(K.xnT[:, :, 2 * u * P:(2 * u + 2) * P],
                           K.ps[:, u % self.banks, :].rearrange("p (k c) -> p k c", k=KT), ACT.Copy).then_inc(self.turned, 1)


def norm_block(nc, ctx, K, tag, loads, transposed=True, **how):
    norm = Norm(nc, ctx, K, tag, loads, **how)
    with nc.Block() as block:
        @block.vector
        def _(dve):
            norm.vector(dve)

        @block.gpsimd
        def _(pool):
            norm.gpsimd(pool)

        @block.sync
        def _(sp):
            norm.sync(sp)

        if transposed:
            @block.tensor
            def _(pe):
                norm.tensor(pe)

            @block.scalar
            def _(act):
                norm.scalar(act)


def multihead(nc, ctx, K, tag, norm, layer, wq, wk, wv, wo, bq=None, bk=None, bv=None, bo=None, mask=None):
    NC = -(-H * L // P)
    HV = HD + 1
    heads = [sorted({r // L for r in range(c * P, min((c + 1) * P, H * L))}) for c in range(NC)]
    rows = [min(P, H * L - c * P) for c in range(NC)]
    G4 = 4 * L
    rounds = [(0, 4), (4, 8), (8, NC)]
    ps = K.ps
    with ExitStack() as c:
        kT = sbuf(nc, c, tag + "kT", [P, KT, B * L])
        kblk = sbuf(nc, c, tag + "kblk", [P, B, KT, 8 * L])
        vaug = sbuf(nc, c, tag + "vaug", [L, B, H, HV])
        vblk = sbuf(nc, c, tag + "vblk", [P, B, NC * 3 * HV])
        qT = sbuf(nc, c, tag + "qT", [P, KT, S])
        sm = sbuf(nc, c, tag + "sm", [P, 2, H * L])
        pr = sbuf(nc, c, tag + "pr", [P, 2, H * L])
        pT = sbuf(nc, c, tag + "pT", [P, 2, NC, P])
        mx = sbuf(nc, c, tag + "mx", [P, 2, H])
        rden = sbuf(nc, c, tag + "rden", [P, 2, H])
        on = sbuf(nc, c, tag + "on", [P, 2, D])
        oT = sbuf(nc, c, tag + "oT", [P, D])
        gbo = sbuf(nc, c, tag + "gbo", [P, D])
        if mask is not None:
            mi = sbuf(nc, c, tag + "mi", [P, TB, L], I32)
            mf = sbuf(nc, c, tag + "mf", [P, TB, L])
        (s_mask, s_kv, s_kt, s_ones, s_set, s_bias, s_vb, s_vc, q_ps, q_sb, s_ready, s_used, sh_step, mx_ready, p_in, p_ready, pt_ps, pt_sb,
         o_ready, n_step, o_used, on_ready, oT_ps, oT_sb, y_ready, x_done) = semaphores(
            nc, ctx, tag, "mask kv kt ones set bias vb vc q_ps q_sb s_ready s_used sh_step mx_ready p_in p_ready pt_ps pt_sb "
            "o_ready n_step o_used on_ready oT_ps oT_sb y_ready x_done")
        gate = K.gate[:, 0, layer:layer + 1]
        SET = B * KT + B
        with nc.Block() as block:
            @block.sync
            def _(sp):
                norm.sync(sp)
                if mask is not None:
                    sp.dma_start(mi[:, :, :], mask.rearrange("(t p) k -> p t k", p=P)).then_inc(s_mask, 16)

            @block.tensor
            def _(pe):
                pe.wait_ge(norm.loaded, norm.all_loaded)
                for ct in range(KT):
                    for k in range(KT):
                        pe.matmul(ps[:, 4, ct * 256:ct * 256 + B * L], wk[:, k, ct * P:(ct + 1) * P],
                                  K.ctxT[:, k, :], start=(k == 0), stop=(k == KT - 1))
                for b in range(B):
                    for k in range(KT):
                        m = pe.matmul(ps[0:L, 5, b * D:(b + 1) * D], K.ctxT[:, k, b * L:(b + 1) * L],
                                      wv[:, k, :], start=(k == 0), stop=(k == KT - 1 and bv is None))
                    if bv is not None:
                        m = pe.matmul(ps[0:L, 5, b * D:(b + 1) * D], K.ones[0:1, 0:L], bv[0:1, :], start=False, stop=True)
                m.then_inc(s_kv, 1)
                pe.wait_ge(s_vb, B)
                for b in range(B):
                    for part in range(NC):
                        for j, h in enumerate(heads[part]):
                            down = h * L - part * P
                            m = pe.matmul(ps[:, 6 + b, (3 * part + j) * HV:(3 * part + j + 1) * HV],
                                          K.shift[0:L, P - down:2 * P - down], vaug[:, b, h, :],
                                          start=True, stop=True)
                m.then_inc(s_vc, 1)
                norm.tensor(pe)

                def scores(b, i):
                    pe.wait_ge(s_used, b * TB + i + 1)
                    for g in range(4):
                        m = pe.matmul(ps[:, g, 0:G4], qT[:, g // 2, i * P:(i + 1) * P],
                                      kblk[:, b, g // 2, (g % 2) * G4:(g % 2 + 1) * G4], start=True, stop=True)
                    m.then_inc(s_ready, 1)

                def turn(b, i, which):
                    pe.wait_ge(p_ready, b * TB + i + 1)
                    for r in which:
                        lo, hi = rounds[r]
                        if r != 1:
                            pe.wait_ge(pt_sb, b * 3 * TB + 3 * i + (r == 2) + 1)
                        for part in range(lo, hi):
                            n = rows[part]
                            m = pe.transpose(ps[0:n, 4 + r % 2, (part - lo) * P:(part - lo + 1) * P],
                                             pr[:, i % 2, part * P:part * P + n], K.ident[:, :])
                        m.then_inc(pt_ps, 1)

                def values(b, i):
                    pe.wait_ge(o_used, b * TB + i + 1)
                    for r, (lo, hi) in enumerate(rounds):
                        pe.wait_ge(pt_sb, b * 3 * TB + 3 * i + r + 2)
                        for part in range(lo, hi):
                            n, hs = rows[part], heads[part]
                            m = pe.matmul(ps[:, 6, hs[0] * HV:(hs[-1] + 1) * HV], pT[0:n, i % 2, part, :],
                                          vblk[0:n, b, 3 * part * HV:(3 * part + len(hs)) * HV],
                                          start=(part == 0), stop=(part == NC - 1), skip_group_check=True)
                    m.then_inc(o_ready, 1)

                def turn_heads(b, i):
                    pe.wait_ge(on_ready, b * TB + i + 1)
                    pe.wait_ge(x_done, b * TB + i + 1)
                    for k in range(KT):
                        m = pe.transpose(ps[:, 7, k * P:(k + 1) * P], on[:, i % 2, k * P:(k + 1) * P], K.ident[:, :])
                    m.then_inc(oT_ps, 1)

                def project(b, i):
                    pe.wait_ge(oT_sb, b * TB + i + 1)
                    for k in range(KT):
                        m = pe.matmul(ps[:, 7, D:2 * D], oT[:, k * P:(k + 1) * P], wo[:, k, :],
                                      start=(k == 0), stop=(k == KT - 1))
                    m.then_inc(y_ready, 1)

                pe.wait_ge(norm.turned, NT // 2)
                with pe.Fori(0, B) as b:
                    pe.wait_ge(x_done, b * TB + 1)
                    for n in range(4):
                        for k in range(KT):
                            m = pe.matmul(ps[:, n, :], wq[:, k, (n // 2) * P:(n // 2 + 1) * P],
                                          K.xnT[:, k, bass.ds(b * S + (n % 2) * 512, 512)],
                                          start=(k == 0), stop=(k == KT - 1))
                        m.then_inc(q_ps, 1)
                    pe.wait_ge(q_sb, b * 4 + 4)
                    pe.wait_ge(s_set, SET)
                    pe.wait_ge(s_used, b * TB + 1)
                    scores(b, 0)
                    scores(b, 1)
                    for i in range(TB):
                        if i + 2 < TB:
                            scores(b, i + 2)
                        turn(b, i, (0, 1))
                        if i:
                            turn_heads(b, i - 1)
                        turn(b, i, (2,))
                        values(b, i)
                        if i:
                            project(b, i - 1)
                    turn_heads(b, TB - 1)
                    project(b, TB - 1)

            @block.scalar
            def _(act):
                act.wait_ge(norm.loaded, norm.all_loaded)
                act.wait_ge(s_kv, 1)
                for ct in range(KT):
                    if bk is None:
                        act.activation(kT[:, ct, :], ps[:, 4, ct * 256:ct * 256 + B * L], ACT.Copy).then_inc(s_kt, 1)
                    else:
                        act.activation(kT[:, ct, :], ps[:, 4, ct * 256:ct * 256 + B * L], ACT.Identity,
                                       bias=bk[:, ct:ct + 1]).then_inc(s_kt, 1)
                act.wait_ge(s_ones, 1)
                for b in range(B):
                    act.activation(vaug[:, b, :, 0:HD], ps[0:L, 5, b * D:(b + 1) * D].rearrange("p (h c) -> p h c", h=H),
                                   ACT.Copy).then_inc(s_vb, 1)
                norm.scalar(act)

                def exps(b, i):
                    act.wait_ge(p_in, b * TB + i + 1)
                    if i >= 2:
                        act.wait_ge(pt_ps, b * 3 * TB + 3 * (i - 1))
                    act.activation(pr[:, i % 2, :], sm[:, i % 2, :], ACT.Exp).then_inc(p_ready, 1)

                with act.Fori(0, B) as b:
                    act.wait_ge(x_done, b * TB + 1)
                    for n in range(4):
                        act.wait_ge(q_ps, b * 4 + n + 1)
                        dst = qT[:, n // 2, (n % 2) * 512:(n % 2 + 1) * 512]
                        if bq is None:
                            act.activation(dst, ps[:, n, :], ACT.Copy).then_inc(q_sb, 1)
                        else:
                            act.activation(dst, ps[:, n, :], ACT.Identity,
                                           bias=bq[:, n // 2:n // 2 + 1]).then_inc(q_sb, 1)
                    exps(b, 0)
                    for i in range(TB):
                        if i + 1 < TB:
                            exps(b, i + 1)
                        for r, (lo, hi) in enumerate(rounds):
                            if i and r == 2:
                                act.wait_ge(oT_ps, b * TB + i)
                                act.activation(oT[:, :], ps[:, 7, 0:D], ACT.Copy).then_inc(oT_sb, 1)
                            act.wait_ge(pt_ps, b * 3 * TB + 3 * i + r + 1)
                            if i >= 2 and r == 0:
                                act.wait_ge(o_ready, b * TB + i - 1)
                            if r < 2:
                                act.activation(pT[:, i % 2, lo:hi, :].rearrange("p a b -> p (a b)"),
                                               ps[:, 4 + r, :], ACT.Copy).then_inc(pt_sb, 1)
                            else:
                                act.activation(pT[:, i % 2, lo, :], ps[:, 4, 0:P], ACT.Copy)
                                act.activation(pT[0:rows[-1], i % 2, lo + 1, :], ps[0:rows[-1], 4, P:2 * P],
                                               ACT.Copy).then_inc(pt_sb, 1)
                    act.wait_ge(oT_ps, b * TB + TB)
                    act.activation(oT[:, :], ps[:, 7, 0:D], ACT.Copy).then_inc(oT_sb, 1)

            @block.gpsimd
            def _(pool):
                pool.memset(vaug[:, :, :, :], 1.0).then_inc(s_ones, 1)
                norm.gpsimd(pool)
                pool.wait_ge(norm.loaded, norm.all_loaded)
                pool.wait_ge(norm.rows, NT)
                if bo is not None:
                    pool.tensor_tensor(gbo[:, :], bo[:, :], gate.broadcast_to([P, D]), ALU.mult).then_inc(s_bias, 1)
                    pool.wait_ge(s_bias, 1)
                    pool.tensor_tensor(K.x[:, :, :], K.x[:, :, :],
                                       gbo[:, :].unsqueeze(1).broadcast_to([P, NT, D]), ALU.add).then_inc(s_bias, 1)

            @block.vector
            def _(dve):
                norm.vector(dve)
                dve.wait_ge(norm.rows, NT)
                dve.wait_ge(norm.loaded, norm.all_loaded)
                s = Steps(s_set)
                dve.wait_ge(s_kt, KT)
                dve.sem_inc(x_done, 1)
                for b in range(B):
                    for ct in range(KT):
                        s.did(dve.tensor_tensor(
                            kblk[:, b, ct, :].rearrange("p (h k) -> p h k", h=8),
                            kT[:, ct, b * L:(b + 1) * L].unsqueeze(1).broadcast_to([P, 8, L]),
                            K.headmask[:, :].unsqueeze(2).broadcast_to([P, 8, L]), ALU.mult))
                if mask is not None:
                    dve.wait_ge(s_mask, 16)
                    dve.tensor_scalar(mf[:, :, :], mi[:, :, :], 0, -3e38, ALU.is_equal, ALU.mult).then_inc(n_step, 1)
                    dve.wait_ge(n_step, 1)
                dve.wait_ge(s_vc, 1)
                W = NC * 3 * HV
                used = [3 * part * HV + n for part in range(NC) for n in range(len(heads[part]) * HV)]
                full = used == list(range(len(used)))
                for b in range(B):
                    if full:
                        s.did(dve.tensor_copy(vblk[:, b, 0:len(used)], ps[:, 6 + b, 0:len(used)]))
                    else:
                        for part in range(NC):
                            lo, n = 3 * part * HV, len(heads[part]) * HV
                            m = dve.tensor_copy(vblk[:, b, lo:lo + n], ps[:, 6 + b, lo:lo + n])
                            if part == NC - 1:
                                s.did(m)
                dve.wait_ge(s_set, s.last())
                assert s.last() == SET

                if bo is not None:
                    dve.wait_ge(s_bias, 2)
                for free in (s_used, pt_sb, o_used):
                    dve.sem_inc(free, 1)

                def front(b, i):
                    dve.wait_ge(s_ready, b * TB + i + 1)
                    if i >= 2:
                        dve.wait_ge(p_ready, b * TB + i - 1)
                    sc = ps[:, 0:4, 0:G4].rearrange("p g (h k) -> p g h k", h=4)
                    smt = sm[:, i % 2, :].rearrange("p (g h k) -> p g h k", g=4, h=4)
                    sm2 = sm[:, i % 2, :].rearrange("p (h k) -> p h k", h=H)
                    mxt = mx[:, i % 2, :]
                    if mask is not None:
                        dve.tensor_tensor(sm[:, i % 2, :].rearrange("p (g c) -> p g c", g=4).rearrange("p g (h k) -> p g h k", h=4),
                                          sc, mf[:, i, :].unsqueeze(1).unsqueeze(1).broadcast_to([P, 4, 4, L]),
                                          ALU.add).then_inc(s_used, 1)
                        dve.wait_ge(s_used, b * TB + i + 2)
                        dve.tensor_reduce(mxt, sm2, AX.X, ALU.max).then_inc(sh_step, 1)
                        dve.wait_ge(sh_step, b * TB + i + 1)
                        dve.tensor_tensor(sm2, sm2, mxt.unsqueeze(2).broadcast_to([P, H, L]),
                                          ALU.subtract).then_inc(p_in, 1)
                    else:
                        dve.tensor_reduce(mxt.rearrange("p (g h) -> p g h", g=4), sc, AX.X, ALU.max).then_inc(sh_step, 1)
                        dve.wait_ge(sh_step, b * TB + i + 1)
                        m = dve.tensor_tensor(smt, sc, mxt.rearrange("p (g h) -> p g h", g=4).unsqueeze(3)
                                              .broadcast_to([P, 4, 4, L]), ALU.subtract)
                        m.then_inc(p_in, 1)
                        dve.wait_ge(p_in, b * TB + i + 1)
                        dve.sem_inc(s_used, 1)

                def normalise(b, i):
                    o = ps[:, 6, 0:H * HV].rearrange("p (h c) -> p h c", h=H)
                    dve.wait_ge(o_ready, b * TB + i + 1)
                    dve.reciprocal(rden[:, i % 2, :], o[:, :, HD]).then_inc(mx_ready, 1)
                    dve.wait_ge(mx_ready, b * TB + i + 1)
                    if i >= 2:
                        dve.wait_ge(oT_ps, b * TB + i - 1)
                    dve.tensor_tensor(on[:, i % 2, :].rearrange("p (h c) -> p h c", h=H), o[:, :, 0:HD],
                                      rden[:, i % 2, :].unsqueeze(2).broadcast_to([P, H, HD]),
                                      ALU.mult).then_inc(on_ready, 1)
                    dve.wait_ge(on_ready, b * TB + i + 1)
                    dve.sem_inc(o_used, 1)

                def residual(b, i):
                    dve.wait_ge(y_ready, b * TB + i + 1)
                    xt = K.x[:, b * TB + i, :]
                    dve.scalar_tensor_tensor(xt, ps[:, 7, D:2 * D], gate, xt, ALU.mult, ALU.add).then_inc(x_done, 1)

                with dve.Fori(0, B) as b:
                    dve.wait_ge(x_done, b * TB + 1)
                    front(b, 0)
                    front(b, 1)
                    for i in range(TB):
                        if i + 2 < TB:
                            front(b, i + 2)
                        normalise(b, i)
                        if i:
                            residual(b, i - 1)
                    residual(b, TB - 1)


def sigmoid_attention(nc, ctx, K, tag, layer, wqn, wk, wv, bq, bk, bv):
    QK = 64
    ps = K.ps
    with ExitStack() as c:
        kp = sbuf(nc, c, tag + "kp", [QK, B * L])
        v = sbuf(nc, c, tag + "v", [L, B, D])
        a = sbuf(nc, c, tag + "a", [P, KT, B * L])
        cb = sbuf(nc, c, tag + "cb", [L, B])
        zT = sbuf(nc, c, tag + "zT", [L, 2, 512])
        s_kv, s_kvb, s_a, s_ab, s_ps, s_z, s_y, s_x = semaphores(nc, c, tag, "kv kvb a ab s_ps z y x")
        gate = K.gate[:, 0, layer:layer + 1]
        groups = B * S // 512
        with nc.Block() as block:
            @block.tensor
            def _(pe):
                for k in range(KT):
                    pe.matmul(ps[0:QK, 0, 0:B * L], wk[:, k, :], K.ctxT[:, k, :], start=(k == 0), stop=(k == KT - 1))
                for b in range(B):
                    for k in range(KT):
                        m = pe.matmul(ps[0:L, 1, b * D:(b + 1) * D], K.ctxT[:, k, b * L:(b + 1) * L],
                                      wv[:, k, :], start=(k == 0), stop=(k == KT - 1))
                m.then_inc(s_kv, 1)
                pe.wait_ge(s_kvb, 2)
                for k in range(KT):
                    pe.matmul(ps[:, 2, k * 256:k * 256 + B * L], wqn[:, k * P:(k + 1) * P], kp[:, :],
                              start=True, stop=True)
                for b in range(B):
                    m = pe.matmul(ps[0:L, 3, b:b + 1], kp[:, b * L:(b + 1) * L], bq[:, 0:1], start=True, stop=True)
                m.then_inc(s_a, 1)
                pe.wait_ge(s_ab, 2)

                def scores(g):
                    b = g * 512 // S
                    if g >= 2:
                        pe.wait_ge(s_z, g - 1)
                    for k in range(KT):
                        m = pe.matmul(ps[0:L, 4 + g % 2, :], a[:, k, b * L:(b + 1) * L],
                                      K.xnT[:, k, g * 512:(g + 1) * 512], start=(k == 0), stop=(k == KT - 1))
                    m.then_inc(s_ps, 1)

                scores(0)
                for g in range(groups):
                    b = g * 512 // S
                    if g + 1 < groups:
                        scores(g + 1)
                    pe.wait_ge(s_z, g + 1)
                    for u in range(2):
                        n = 2 * g + u
                        if n >= 2:
                            pe.wait_ge(s_x, n - 1)
                        for j in range(2):
                            m = pe.matmul(ps[:, 6 + n % 2, j * D:(j + 1) * D],
                                          zT[:, g % 2, (2 * u + j) * P:(2 * u + j + 1) * P], v[:, b, :],
                                          start=True, stop=True)
                        m.then_inc(s_y, 1)

            @block.scalar
            def _(act):
                act.wait_ge(s_a, 1)
                act.activation(cb[:, :], ps[0:L, 3, 0:B], ACT.Copy, scale=QK ** -0.5).then_inc(s_ab, 1)
                act.wait_ge(s_ab, 2)
                for g in range(groups):
                    b = g * 512 // S
                    act.wait_ge(s_ps, g + 1)
                    if g >= 2:
                        act.wait_ge(s_y, 2 * (g - 1))
                    act.activation(zT[:, g % 2, :], ps[0:L, 4 + g % 2, :], ACT.Sigmoid, bias=cb[:, b:b + 1],
                                   scale=QK ** -0.5).then_inc(s_z, 1)

            @block.vector
            def _(dve):
                dve.wait_ge(s_kv, 1)
                dve.tensor_scalar(kp[:, :], ps[0:QK, 0, 0:B * L], bk[:, 0:1], None, ALU.add).then_inc(s_kvb, 1)
                dve.tensor_tensor(v[:, :, :], ps[0:L, 1, :].rearrange("p (b d) -> p b d", b=B),
                                  bv[:, :].unsqueeze(1).broadcast_to([L, B, D]), ALU.add).then_inc(s_kvb, 1)
                dve.wait_ge(s_a, 1)
                dve.tensor_copy(a[:, :, :], ps[:, 2, :].rearrange("p (k c) -> p k c", k=KT)[:, :, 0:B * L]).then_inc(s_ab, 1)
                for n in range(2 * groups):
                    dve.wait_ge(s_y, n + 1)
                    xt = K.x[:, 2 * n:2 * n + 2, :].rearrange("p t d -> p (t d)")
                    dve.scalar_tensor_tensor(xt, ps[:, 6 + n % 2, :], gate, xt, ALU.mult, ALU.add).then_inc(s_x, 1)


def align_attention(nc, ctx, K, tag, layer, wT, wn, bc):
    ps = K.ps
    with ExitStack() as c:
        eo = sbuf(nc, c, tag + "eo", [P, KT, B * L])
        a = sbuf(nc, c, tag + "a", [P, KT, B * L])
        cr = sbuf(nc, c, tag + "cr", [1, B * L])
        sm = sbuf(nc, c, tag + "sm", [P, 2, 4, L])
        pr = sbuf(nc, c, tag + "pr", [P, 2, 4, L])
        pT = sbuf(nc, c, tag + "pT", [L, 2, 512])
        vec = sbuf(nc, c, tag + "vec", [P, 2, 4, 4])
        s_e, s_eb, s_a, s_ab, s_ps, s_mx, s_sh, s_p, s_sum, s_tp, s_tb, s_y, s_x = semaphores(
            nc, c, tag, "e eb a ab s_ps mx sh p sum tp tb y x")
        gate = K.gate[:, 0, layer:layer + 1]
        groups = B * S // 512
        with nc.Block() as block:
            @block.tensor
            def _(pe):
                for e in range(KT):
                    for k in range(KT):
                        m = pe.matmul(ps[:, 0, e * 256:e * 256 + B * L], wT[:, k, e * P:(e + 1) * P], K.ctxT[:, k, :],
                                      start=(k == 0), stop=(k == KT - 1))
                m.then_inc(s_e, 1)
                pe.wait_ge(s_eb, 2)
                for d in range(KT):
                    for e in range(KT):
                        pe.matmul(ps[:, 1, d * 256:d * 256 + B * L], wn[:, e, d * P:(d + 1) * P], eo[:, e, :],
                                  start=(e == 0), stop=(e == KT - 1))
                for e in range(KT):
                    m = pe.matmul(ps[0:1, 2, 0:B * L], bc[:, e:e + 1], eo[:, e, :], start=(e == 0), stop=(e == KT - 1))
                m.then_inc(s_a, 1)
                pe.wait_ge(s_ab, 2)

                def scores(g):
                    b = g * 512 // S
                    if g >= 2:
                        pe.wait_ge(s_sh, g - 1)
                    for i in range(4):
                        t = 4 * g + i
                        o = ps[:, g % 2, i * L:(i + 1) * L]
                        for k in range(KT):
                            pe.matmul(o, K.xnT[:, k, t * P:(t + 1) * P], a[:, k, b * L:(b + 1) * L],
                                      start=(k == 0), stop=False)
                        m = pe.matmul(o, K.ones[0:1, :], cr[:, b * L:(b + 1) * L], start=False, stop=True)
                    m.then_inc(s_ps, 1)

                scores(0)
                for g in range(groups):
                    b = g * 512 // S
                    if g + 1 < groups:
                        scores(g + 1)
                    pe.wait_ge(s_p, g + 1)
                    for i in range(4):
                        m = pe.transpose(ps[0:L, 2 + g % 2, i * P:(i + 1) * P], pr[:, g % 2, i, :], K.ident[:, :])
                    m.then_inc(s_tp, 1)
                    pe.wait_ge(s_tb, g + 1)
                    for u in range(2):
                        n = 2 * g + u
                        if n >= 4:
                            pe.wait_ge(s_x, n - 3)
                        for j in range(2):
                            m = pe.matmul(ps[:, 4 + n % 4, j * D:(j + 1) * D],
                                          pT[:, g % 2, (2 * u + j) * P:(2 * u + j + 1) * P], K.ctx_nat[:, b, :],
                                          start=True, stop=True)
                        m.then_inc(s_y, 1)

            @block.scalar
            def _(act):
                act.wait_ge(s_a, 1)
                act.activation(cr[:, :], ps[0:1, 2, 0:B * L], ACT.Copy).then_inc(s_ab, 1)
                for g in range(groups):
                    act.wait_ge(s_sh, g + 1)
                    if g >= 2:
                        act.wait_ge(s_tp, g - 1)
                        act.wait_ge(s_sum, g - 1)
                    act.activation(pr[:, g % 2, :, :], sm[:, g % 2, :, :], ACT.Exp).then_inc(s_p, 1)
                    act.wait_ge(s_tp, g + 1)
                    if g >= 2:
                        act.wait_ge(s_y, 2 * (g - 1))
                    act.activation(pT[:, g % 2, :], ps[0:L, 2 + g % 2, :], ACT.Copy).then_inc(s_tb, 1)

            @block.vector
            def _(dve):
                dve.wait_ge(s_e, 1)
                for e in range(KT):
                    dve.tensor_scalar(eo[:, e, :], ps[:, 0, e * 256:e * 256 + B * L], bc[:, e:e + 1], None,
                                      ALU.add).then_inc(s_eb, 1)
                dve.wait_ge(s_a, 1)
                dve.tensor_copy(a[:, :, :], ps[:, 1, :].rearrange("p (k c) -> p k c", k=KT)[:, :, 0:B * L]).then_inc(s_ab, 1)

                def front(g):
                    dve.wait_ge(s_ps, g + 1)
                    sc = ps[:, g % 2, 0:4 * L].rearrange("p (i k) -> p i k", i=4)
                    dve.tensor_reduce(vec[:, g % 2, 0, :], sc, AX.X, ALU.max).then_inc(s_mx, 1)
                    dve.wait_ge(s_mx, g + 1)
                    if g >= 2:
                        dve.wait_ge(s_p, g - 1)
                    dve.tensor_tensor(sm[:, g % 2, :, :], sc, vec[:, g % 2, 0, :].unsqueeze(2).broadcast_to([P, 4, L]),
                                      ALU.subtract).then_inc(s_sh, 1)

                front(0)
                s_c = s_eb
                st = Steps(s_c, 2)
                for g in range(groups):
                    if g + 1 < groups:
                        front(g + 1)
                    dve.wait_ge(s_p, g + 1)
                    vg = vec[:, g % 2, :, :]
                    dve.tensor_reduce(vg[:, 1, :], pr[:, g % 2, :, :], AX.X, ALU.add).then_inc(s_sum, 1)
                    dve.wait_ge(s_sum, g + 1)
                    st.did(dve.reciprocal(vg[:, 2, :], vg[:, 1, :]))
                    dve.wait_ge(s_c, st.last())
                    st.did(dve.tensor_scalar(vg[:, 3, :], vg[:, 2, :], gate, None, ALU.mult))
                    dve.wait_ge(s_c, st.last())
                    for u in range(2):
                        dve.wait_ge(s_y, 2 * g + u + 1)
                        for j in range(2):
                            i = 2 * u + j
                            xt = K.x[:, 4 * g + i, :]
                            m = dve.scalar_tensor_tensor(xt, ps[:, 4 + (2 * g + u) % 4, j * D:(j + 1) * D],
                                                         vg[:, 3, i:i + 1], xt, ALU.mult, ALU.add)
                        m.then_inc(s_x, 1)


def sum_magnitudes(dve, s_part, weights, part, out, steps):
    for n, w in enumerate(weights):
        dve.tensor_reduce(part[:, n, :], w[:, :, :].rearrange("p k f -> p (k f)").rearrange("p (a c) -> p a c", c=64),
                          AX.X, ALU.add, apply_absolute_value=True).then_inc(s_part, 1)
    dve.wait_ge(s_part, 2)
    for n in range(2):
        steps.did(dve.tensor_reduce(out[:, n:n + 1], part[:, n, :], AX.X, ALU.add))


def bitnet_ffn(nc, ctx, K, tag, layer, w1, w2, cw, cbias):
    F = 1024
    FT = F // P
    ps = K.ps
    psb = [ps[:, k, :].bitcast(BF16) for k in range(8)]
    with ExitStack() as c:
        q1 = sbuf(nc, c, tag + "q1", [P, KT, F], BF16)
        q2 = sbuf(nc, c, tag + "q2", [P, FT, D], BF16)
        wt = sbuf(nc, c, tag + "wt", [P, 2, 2048])
        xq = sbuf(nc, c, tag + "xq", [P, NT, D], BF16)
        xqT = sbuf(nc, c, tag + "xqT", [P, KT, B * S], BF16)
        dqb = sbuf(nc, c, tag + "dqb", [P, B * S])
        diag = sbuf(nc, c, tag + "diag", [P, 4, P])
        vec = sbuf(nc, c, tag + "vec", [P, 8, NT])
        wv = sbuf(nc, c, tag + "wv", [P, 4, 2])
        magic = sbuf(nc, c, tag + "magic", [P, 1])
        hb = sbuf(nc, c, tag + "hb", [P, 2, S + 2])
        yb = sbuf(nc, c, tag + "yb", [P, 2, S])
        act_s = sbuf(nc, c, tag + "act", [P, FT, S])
        tv = sbuf(nc, c, tag + "tv", [P, 6, TB])
        qf = sbuf(nc, c, tag + "qf", [P, 2, F])
        qb = sbuf(nc, c, tag + "qb", [P, 2, F], BF16)
        qT = sbuf(nc, c, tag + "qT", [P, 2, F], BF16)
        part = sbuf(nc, c, tag + "part", [P, 2, 32])
        (s_part,) = semaphores(nc, c, tag, "part")
        (s_set, s_sum, s_xq, s_xt, s_xe, s_dg, s_db, s_de, h_ps, h_sb, y0, tap, y_sb, a_sb, t_ps, t_step, sc_ready,
         qf_sb, qb_sb, u_ps, u_sb, y_ps, x_done) = semaphores(
            nc, c, tag, "set sum xq xt xe dg db de h_ps h_sb y0 tap y_sb a_sb t_ps t_step sc qf qb u_ps u_sb y_ps xd")
        gate = K.gate[:, 1, layer:layer + 1]
        TURNED = (4, 0)

        def turned(i):
            return ps[:, TURNED[i % 2]:TURNED[i % 2] + 2, :].rearrange("p a c -> p (a c)")

        with nc.Block() as block:
            @block.tensor
            def _(pe):
                pe.wait_ge(s_set, 2)
                pe.matmul(ps[:, 7, 0:2], K.ones[:, :], wv[:, 0, :], start=True, stop=True).then_inc(s_sum, 1)
                for q in range(4):
                    pe.wait_ge(s_xq, 1)
                    for k in range(KT):
                        for i in range(4):
                            t = 4 * q + i
                            m = pe.transpose(psb[q][:, (4 * k + i) * P:(4 * k + i + 1) * P],
                                             xq[:, t, k * P:(k + 1) * P], K.identb[:, :])
                    m.then_inc(s_xt, 1)
                for t in range(NT):
                    pe.wait_ge(s_dg, t + 1)
                    if t % 4 == 0:
                        pe.wait_ge(s_xe, 4)
                        if t >= 8:
                            pe.wait_ge(s_de, t // 4 - 1)
                    m = pe.matmul(ps[:, 4 + (t // 4) % 2, (t % 4) * P:(t % 4 + 1) * P], K.ones[:, :], diag[:, t % 4, :],
                                  start=True, stop=True)
                    m.then_inc(s_db, 1)
                pe.wait_ge(s_de, 4)
                with pe.Fori(0, B) as b:
                    pe.wait_ge(x_done, b * TB + 1)
                    for f in range(FT):
                        if f >= 2:
                            pe.wait_ge(h_sb, b * FT + f - 1)
                        for hf in range(2):
                            for k in range(KT):
                                m = pe.matmul(ps[:, 2 * (f % 2) + hf, :], q1[:, k, f * P:(f + 1) * P],
                                              xqT[:, k, bass.ds(b * S + hf * 512, 512)],
                                              start=(k == 0), stop=(k == KT - 1))
                        m.then_inc(h_ps, 1)
                    pe.wait_ge(a_sb, b * FT + FT)

                    def turn(i):
                        if i >= 2:
                            pe.wait_ge(qf_sb, b * TB + i - 1)
                        for f in range(FT):
                            m = pe.transpose(ps[:, TURNED[i % 2] + f // 4, (f % 4) * P:(f % 4 + 1) * P],
                                             act_s[:, f, i * P:(i + 1) * P], K.ident[:, :])
                        m.then_inc(t_ps, 1)

                    def turn_back(i):
                        pe.wait_ge(qb_sb, b * TB + i + 1)
                        if i:
                            pe.wait_ge(u_sb, b * TB + i)
                        for f in range(FT):
                            m = pe.transpose(psb[6][:, f * P:(f + 1) * P], qb[:, i % 2, f * P:(f + 1) * P],
                                             K.identb[:, :])
                        m.then_inc(u_ps, 1)

                    def down(i):
                        pe.wait_ge(u_sb, b * TB + i + 1)
                        if i:
                            pe.wait_ge(x_done, b * TB + i + 1)
                        for f in range(FT):
                            m = pe.matmul(ps[:, 7, 0:D], qT[:, i % 2, f * P:(f + 1) * P], q2[:, f, :],
                                          start=(f == 0), stop=(f == FT - 1))
                        m.then_inc(y_ps, 1)

                    turn(0)
                    turn(1)
                    turn_back(0)
                    for i in range(TB):
                        if i + 2 < TB:
                            turn(i + 2)
                        if i + 1 < TB:
                            turn_back(i + 1)
                        down(i)

            @block.scalar
            def _(act):
                for q in range(4):
                    act.wait_ge(s_xt, q + 1)
                    act.activation(xqT[:, :, q * 512:(q + 1) * 512], psb[q].rearrange("p (k c) -> p k c", k=KT),
                                   ACT.Copy).then_inc(s_xe, 1)
                for q in range(4):
                    act.wait_ge(s_db, 4 * q + 4)
                    act.activation(dqb[:, q * 512:(q + 1) * 512], ps[:, 4 + q % 2, :], ACT.Copy).then_inc(s_de, 1)
                with act.Fori(0, B) as b:
                    def centre(f):
                        act.wait_ge(h_sb, b * FT + f + 1)
                        if f >= 2:
                            act.wait_ge(a_sb, b * FT + f - 1)
                        act.activation(yb[:, f % 2, :], hb[:, f % 2, 1:S + 1], ACT.Identity, bias=cbias[:, f:f + 1],
                                       scale=cw[:, f, 1:2]).then_inc(y0, 1)

                    centre(0)
                    for f in range(FT):
                        if f + 1 < FT:
                            centre(f + 1)
                        act.wait_ge(y_sb, b * FT + f + 1)
                        act.activation(act_s[:, f, :], yb[:, f % 2, :], ACT.Silu).then_inc(a_sb, 1)

                    def scaled(i):
                        act.wait_ge(sc_ready, b * TB + i + 1)
                        if i >= 2:
                            act.wait_ge(qb_sb, b * TB + i - 1)
                        act.activation(qf[:, i % 2, :], turned(i), ACT.Identity,
                                       bias=magic[:, 0:1], scale=tv[:, 3, i:i + 1]).then_inc(qf_sb, 1)

                    def copy_back(i):
                        act.wait_ge(u_ps, b * TB + i + 1)
                        if i >= 2:
                            act.wait_ge(y_ps, b * TB + i - 1)
                        act.activation(qT[:, i % 2, :], psb[6], ACT.Copy).then_inc(u_sb, 1)

                    scaled(0)
                    scaled(1)
                    copy_back(0)
                    for i in range(TB):
                        if i + 1 < TB:
                            copy_back(i + 1)
                        if i + 2 < TB:
                            scaled(i + 2)

            @block.vector
            def _(dve):
                s = Steps(s_set)

                def then(ins):
                    s.did(ins)
                    dve.wait_ge(s_set, s.last())

                sum_magnitudes(dve, s_part, (w1, w2), part, wv[:, 0, :], s)
                dve.memset(hb[:, :, :], 0.0).then_inc(tap, 1)
                dve.memset(magic[:, :], MAGIC).then_inc(tap, 1)
                dve.wait_ge(tap, 2)
                then(dve.tensor_reduce(vec[:, 0, :], K.xn[:, :, :], AX.X, ALU.max, apply_absolute_value=True))
                then(dve.tensor_scalar(vec[:, 1, :], vec[:, 0, :], 1e-5, None, ALU.max))
                then(dve.reciprocal(vec[:, 2, :], vec[:, 1, :]))
                then(dve.tensor_scalar(vec[:, 3, :], vec[:, 2, :], 127.0, None, ALU.mult))
                then(dve.tensor_tensor(K.xn[:, :, :], K.xn[:, :, :],
                                       vec[:, 3, :].unsqueeze(2).broadcast_to([P, NT, D]), ALU.mult))
                dve.tensor_scalar(xq[:, :, :], K.xn[:, :, :], MAGIC, MAGIC, ALU.add, ALU.subtract).then_inc(s_xq, 1)
                dve.wait_ge(s_sum, 1)
                then(dve.tensor_scalar(wv[:, 1, :], ps[:, 7, 0:2], 1.0 / (F * D), 1e-5, ALU.mult, ALU.max))
                then(dve.reciprocal(wv[:, 2, :], wv[:, 1, :]))
                for n, (w, q) in enumerate(((w1, q1), (w2, q2))):
                    flat, qflat = (z[:, :, :].rearrange("p k f -> p (k f)") for z in (w, q))
                    then(dve.tensor_scalar(wt[:, 0, :], flat, wv[:, 2, n:n + 1], MAGIC, ALU.mult, ALU.add))
                    then(dve.tensor_scalar(wt[:, 1, :], wt[:, 0, :], MAGIC, 1.0, ALU.subtract, ALU.min))
                    then(dve.tensor_scalar(qflat, wt[:, 1, :], -1.0, None, ALU.max))
                then(dve.tensor_scalar(vec[:, 4, :], vec[:, 1, :], wv[:, 1, 0:1], 1.0 / 127, ALU.mult, ALU.mult))
                then(dve.tensor_scalar(wv[:, 3, 1:2], wv[:, 1, 1:2], gate, 1.0 / 127, ALU.mult, ALU.mult))
                for t in range(NT):
                    if t >= 4:
                        dve.wait_ge(s_db, t - 3)
                    dve.tensor_scalar(diag[:, t % 4, :], K.ident[:, :], vec[:, 4, t:t + 1], None,
                                      ALU.mult).then_inc(s_dg, 1)
                dve.wait_ge(s_de, 4)
                dve.sem_inc(x_done, 1)
                TS = 4
                with dve.Fori(0, B) as b:
                    def dequant(f):
                        dve.wait_ge(h_ps, b * FT + f + 1)
                        if f >= 2:
                            dve.wait_ge(y_sb, b * FT + f - 1)
                        dve.tensor_tensor(hb[:, f % 2, 1:S + 1], ps[:, 2 * (f % 2):2 * (f % 2) + 2, :].rearrange("p a c -> p (a c)"),
                                          dqb[:, bass.ds(b * S, S)], ALU.mult).then_inc(h_sb, 1)

                    dequant(0)
                    for f in range(FT):
                        if f + 1 < FT:
                            dequant(f + 1)
                        dve.wait_ge(y0, b * FT + f + 1)
                        y = yb[:, f % 2, :]
                        dve.scalar_tensor_tensor(y, hb[:, f % 2, 0:S], cw[:, f, 0:1], y, ALU.mult, ALU.add).then_inc(tap, 1)
                        dve.wait_ge(tap, b * FT + f + 3)
                        dve.scalar_tensor_tensor(y, hb[:, f % 2, 2:S + 2], cw[:, f, 2:3], y, ALU.mult,
                                                 ALU.add).then_inc(y_sb, 1)

                    def scale(i):
                        dve.wait_ge(t_ps, b * TB + i + 1)
                        t = Steps(t_step, b * TS * TB + TS * i)
                        t.did(dve.tensor_reduce(tv[:, 0, i:i + 1], turned(i), AX.X, ALU.max,
                                                apply_absolute_value=True))
                        dve.wait_ge(t_step, t.last())
                        t.did(dve.tensor_scalar(tv[:, 1, i:i + 1], tv[:, 0, i:i + 1], 1e-5, None, ALU.max))
                        dve.wait_ge(t_step, t.last())
                        t.did(dve.reciprocal(tv[:, 2, i:i + 1], tv[:, 1, i:i + 1]))
                        t.did(dve.tensor_scalar(tv[:, 4, i:i + 1], tv[:, 1, i:i + 1], wv[:, 3, 1:2], None, ALU.mult))
                        dve.wait_ge(t_step, t.last())
                        dve.tensor_scalar(tv[:, 3, i:i + 1], tv[:, 2, i:i + 1], 127.0, None, ALU.mult).then_inc(sc_ready, 1)

                    def residual(i):
                        dve.wait_ge(y_ps, b * TB + i + 1)
                        xt = K.x[:, b * TB + i, :]
                        dve.scalar_tensor_tensor(xt, ps[:, 7, 0:D], tv[:, 4, i:i + 1], xt, ALU.mult,
                                                 ALU.add).then_inc(x_done, 1)

                    def whole(i):
                        dve.wait_ge(qf_sb, b * TB + i + 1)
                        if i >= 2:
                            dve.wait_ge(u_ps, b * TB + i - 1)
                        dve.tensor_scalar(qb[:, i % 2, :], qf[:, i % 2, :], MAGIC, None, ALU.subtract).then_inc(qb_sb, 1)

                    scale(0)
                    scale(1)
                    whole(0)
                    for i in range(TB):
                        if i + 1 < TB:
                            whole(i + 1)
                        if i + 2 < TB:
                            scale(i + 2)
                        residual(i)


def ternary_ffn(nc, ctx, K, tag, layer, wu, wd):
    F = 1024
    FT = F // P
    W = 512
    NH = S // W
    ps = K.ps
    with ExitStack() as c:
        tu = sbuf(nc, c, tag + "tu", [P, KT, F], F32R)
        td = sbuf(nc, c, tag + "td", [P, FT, D], F32R)
        wneg = sbuf(nc, c, tag + "wneg", [P, 2048])
        wv = sbuf(nc, c, tag + "wv", [P, 4, 2])
        xh = sbuf(nc, c, tag + "xh", [P, 2, KT, W], F32R)
        xl = sbuf(nc, c, tag + "xl", [P, 2, KT, W], F32R)
        h = sbuf(nc, c, tag + "h", [P, 4, W])
        hh = sbuf(nc, c, tag + "hh", [P, FT, W], F32R)
        hl = sbuf(nc, c, tag + "hl", [P, FT, W], F32R)
        sq = sbuf(nc, c, tag + "sq", [P, FT, W])
        vec = sbuf(nc, c, tag + "vec", [P, 5, 4])
        part = sbuf(nc, c, tag + "part", [P, 2, 32])
        (s_part,) = semaphores(nc, c, tag, "part")
        s_set, s_sum, x_hi, x_lo, u_ps, h_sb, h_hi, h_lo, h_sq, q_ps, vstep, rms, y_ps, x_done = semaphores(
            nc, c, tag, "set sum x_hi x_lo u_ps h_sb h_hi h_lo h_sq q_ps vstep rms y_ps xd")
        gate = K.gate[:, 1, layer:layer + 1]
        with nc.Block() as block:
            @block.tensor
            def _(pe):
                pe.wait_ge(s_set, 2)
                pe.matmul(ps[:, 7, 0:2], K.ones[:, :], wv[:, 0, :], start=True, stop=True).then_inc(s_sum, 1)
                pe.wait_ge(s_set, 8)
                with pe.Fori(0, B) as b:
                    for g in range(NH):
                        pe.wait_ge(x_done, (b * NH + g) * 4 + 1)
                        pe.wait_ge(x_lo, b * NH + g + 1)
                        for f in range(FT):
                            if f >= 4:
                                pe.wait_ge(h_sb, (b * NH + g) * FT + f - 3)
                            for k in range(KT):
                                for n, xs in enumerate((xh, xl)):
                                    m = pe.matmul(ps[:, f % 4, :], tu[:, k, f * P:(f + 1) * P], xs[:, g, k, :],
                                                  start=(k == 0 and n == 0), stop=(k == KT - 1 and n == 1))
                            m.then_inc(u_ps, 1)
                        pe.wait_ge(h_lo, (b * NH + g) * FT + FT)
                        for i in range(4):
                            if i >= 2:
                                pe.wait_ge(x_done, (b * NH + g) * 4 + i)
                            for f in range(FT):
                                for n, hs in enumerate((hh, hl)):
                                    m = pe.matmul(ps[:, 4 + i % 2, 0:D], hs[:, f, i * P:(i + 1) * P], td[:, f, :],
                                                  start=(f == 0 and n == 0), stop=(f == FT - 1 and n == 1))
                            m.then_inc(y_ps, 1)
                            if i == 0:
                                pe.wait_ge(h_sq, (b * NH + g) * FT + FT)
                                for j in range(4):
                                    for f in range(FT):
                                        m = pe.matmul(ps[:, 6, j:j + 1], sq[:, f, j * P:(j + 1) * P], K.ones[:, 0:1],
                                                      start=(f == 0), stop=(f == FT - 1))
                                m.then_inc(q_ps, 1)

            @block.scalar
            def _(act):
                with act.Fori(0, B) as b:
                    for g in range(NH):
                        for f in range(FT):
                            act.wait_ge(u_ps, (b * NH + g) * FT + f + 1)
                            if f >= 4:
                                act.wait_ge(h_lo, (b * NH + g) * FT + f - 3)
                                act.wait_ge(h_sq, (b * NH + g) * FT + f - 3)
                            act.activation(h[:, f % 4, :], ps[:, f % 4, :], ACT.Gelu).then_inc(h_sb, 1)

            @block.gpsimd
            def _(pool):
                with pool.Fori(0, B) as b:
                    for g in range(NH):
                        for f in range(FT):
                            pool.wait_ge(h_sb, (b * NH + g) * FT + f + 1)
                            pool.tensor_tensor(sq[:, f, :], h[:, f % 4, :], h[:, f % 4, :], ALU.mult).then_inc(h_sq, 1)
                        pool.wait_ge(vstep, (b * NH + g) * 3 + 1)
                        pool.tensor_tensor(vec[:, 1, :], vec[:, 0, :], K.hpow[:, 0:4], ALU.pow).then_inc(rms, 1)

            @block.vector
            def _(dve):
                s = Steps(s_set)

                def then(ins):
                    s.did(ins)
                    dve.wait_ge(s_set, s.last())

                flats = [z[:, :, :].rearrange("p k f -> p (k f)") for z in (wu, wd)]
                sum_magnitudes(dve, s_part, (wu, wd), part, wv[:, 0, :], s)
                dve.wait_ge(s_sum, 1)
                s.did(dve.tensor_scalar(wv[:, 1, :], ps[:, 7, 0:2], 0.5 / (F * D), None, ALU.mult))
                then(dve.tensor_scalar(wv[:, 2, :], ps[:, 7, 0:2], -0.5 / (F * D), None, ALU.mult))
                for n, q in enumerate((tu, td)):
                    then(dve.tensor_scalar(wneg[:, :], flats[n], wv[:, 2, n:n + 1], None, ALU.is_lt))
                    then(dve.scalar_tensor_tensor(q[:, :, :].rearrange("p k f -> p (k f)"), flats[n],
                                                  wv[:, 1, n:n + 1], wneg[:, :], ALU.is_gt, ALU.subtract))
                dve.sem_inc(x_done, 1)
                with dve.Fori(0, B) as b:
                    for g in range(NH):
                        xs = K.xnT[:, :, bass.ds(b * S + g * W, W)]
                        dve.tensor_copy(xh[:, g, :, :], xs).then_inc(x_hi, 1)
                        dve.wait_ge(x_hi, b * NH + g + 1)
                        dve.tensor_tensor(xl[:, g, :, :], xs, xh[:, g, :, :].bitcast(F32), ALU.subtract).then_inc(x_lo, 1)
                        for f in range(FT):
                            n = (b * NH + g) * FT + f + 1
                            dve.wait_ge(h_sb, n)
                            if f == 0:
                                dve.wait_ge(x_done, (b * NH + g) * 4 + 1)
                            dve.tensor_copy(hh[:, f, :], h[:, f % 4, :]).then_inc(h_hi, 1)
                            dve.wait_ge(h_hi, n)
                            dve.tensor_tensor(hl[:, f, :], h[:, f % 4, :], hh[:, f, :].bitcast(F32),
                                              ALU.subtract).then_inc(h_lo, 1)
                        dve.wait_ge(q_ps, b * NH + g + 1)
                        v = (b * NH + g) * 3
                        dve.tensor_scalar(vec[:, 0, :], ps[:, 6, 0:4], 1.0 / F, None, ALU.mult).then_inc(vstep, 1)
                        dve.wait_ge(rms, b * NH + g + 1)
                        dve.tensor_scalar(vec[:, 2, :], vec[:, 1, :], 1e-8, None, ALU.add).then_inc(vstep, 1)
                        dve.wait_ge(vstep, v + 2)
                        dve.reciprocal(vec[:, 3, :], vec[:, 2, :]).then_inc(vstep, 1)
                        dve.wait_ge(vstep, v + 3)
                        dve.tensor_scalar(vec[:, 4, :], vec[:, 3, :], gate, None, ALU.mult).then_inc(s_sum, 1)
                        dve.wait_ge(s_sum, b * NH + g + 2)
                        for i in range(4):
                            dve.wait_ge(y_ps, (b * NH + g) * 4 + i + 1)
                            xt = K.x[:, b * TB + 4 * g + i, :]
                            dve.scalar_tensor_tensor(xt, ps[:, 4 + i % 2, 0:D], vec[:, 4, i:i + 1], xt, ALU.mult,
                                                     ALU.add).then_inc(x_done, 1)


def expert_choice_ffn(nc, ctx, K, tag, layer, gw, sg, su, sd, wg_d, wu_d, wd_d, xn_dram, acc_dram):
    E, F = 16, 512
    CAP = S * 2 // E
    FT = F // P
    NS = B * S // 256
    W = 2 * P
    ps = K.ps
    ROUNDS = CAP // 8
    per_unit = [3, 3, 3, 3, 2, 2]
    assert sum(per_unit) == ROUNDS
    with ExitStack() as c:
        lg = sbuf(nc, c, tag + "lg", [P, NT, E])
        sc = sbuf(nc, c, tag + "sc", [P, TB, B, E])
        vec = sbuf(nc, c, tag + "vec", [P, 3, NT])
        va = [sbuf(nc, c, tag + f"va{i}", [B * E, S]) for i in range(2)]
        tw = sbuf(nc, c, tag + "tw", [B * E, CAP])
        ti = sbuf(nc, c, tag + "ti", [B * E, CAP], U32)
        tf = sbuf(nc, c, tag + "tf", [B * E, CAP])
        boff = sbuf(nc, c, tag + "boff", [B * E, 1])
        wcol = sbuf(nc, c, tag + "wcol", [P, B * E])
        idx = sbuf(nc, c, tag + "idx", [P, B * E], U32)
        wg = [sbuf(nc, c, tag + f"wg{i}", [P, KT, F]) for i in range(2)]
        wu = [sbuf(nc, c, tag + f"wu{i}", [P, KT, F]) for i in range(2)]
        wd = [sbuf(nc, c, tag + f"wd{i}", [P, FT, D]) for i in range(2)]
        xg = [sbuf(nc, c, tag + f"xg{i}", [P, B, D]) for i in range(2)]
        xgT = [sbuf(nc, c, tag + f"xgT{i}", [P, KT, W]) for i in range(2)]
        ge = [sbuf(nc, c, tag + f"ge{i}", [P, FT * W]) for i in range(2)]
        hT = [sbuf(nc, c, tag + f"hT{i}", [P, FT, W]) for i in range(2)]
        eo = [sbuf(nc, c, tag + f"eo{i}", [P, B, D]) for i in range(2)]
        acc = [sbuf(nc, c, tag + f"acc{i}", [P, 4, D]) for i in range(2)]
        (l_ps, smx, exp_in, exp_done, sc_rdy, v_ps, rnd, off, t_rdy, t_ps, i_rdy, xt_ps, xt_sb,
         g_ps, u_ps, ge_sb, h_sb, y_ps, y_sb, x_done, added) = semaphores(
            nc, c, tag, "l_ps smx exp_in exp_done sc_rdy v_ps rnd off t_rdy t_ps i_rdy xt_ps xt_sb "
            "g_ps u_ps ge_sb h_sb y_ps y_sb x_done added")
        w_in, d_in, out_dma, acc_in = (semaphores(nc, c, tag, f"{n}0 {n}1") for n in
                                       ("w_in", "d_in", "out_dma", "acc_in"))
        gat, scat = K.row_gathered, K.row_scattered
        gate = K.gate[:, 1, layer:layer + 1]
        with nc.Block() as block:
            @block.sync
            def _(sp):
                def store_shared(u, p):
                    sp.wait_ge(y_sb, u + 3)
                    for j in range(2):
                        sp.dma_start(acc_dram[bass.ds(u * W + j * P, P), :], eo[p][:, j, :]).then_inc(out_dma[p], 16)

                with sp.Fori(0, NS // 2) as pair:
                    u = 2 * pair
                    for p in range(2):
                        store_shared(u + p, p)
                with sp.Fori(0, E // 2) as pair:
                    e = 2 * pair
                    for p in range(2):
                        sp.wait_ge(u_ps, e + p + NS - 1)
                        sp.dma_start(wg[p][:, :, :], wg_d[e + p].rearrange("(k q) f -> q k f", q=P)).then_inc(w_in[p], 16)
                        sp.dma_start(wu[p][:, :, :], wu_d[e + p].rearrange("(k q) f -> q k f", q=P)).then_inc(w_in[p], 16)
                        sp.wait_ge(y_ps, e + p + NS + 1)
                        sp.dma_start(wd[p][:, :, :], wd_d[e + p].rearrange("(k q) f -> q k f", q=P)).then_inc(d_in[p], 16)
                sp.wait_ge(added, E + 2)
                for q in range(4):
                    if q >= 2:
                        sp.wait_ge(x_done, q - 1)
                    sp.dma_start(acc[q % 2][:, :, :],
                                 acc_dram[q * 512:(q + 1) * 512, :].rearrange("(t p) d -> p t d", p=P)).then_inc(acc_in[q % 2], 16)

            @block.gpsimd
            def _(pool):
                pool.memset(boff[:, :], float(S)).then_inc(off, 1)
                pool.wait_ge(off, 1)
                pool.affine_select(out=boff[:, :], in_=boff[:, :], compare_op=ALU.is_ge, fill=0.0, base=-E,
                                   pattern=[[0, 1]], channel_multiplier=1).then_inc(off, 1)

                def gather(e):
                    if e >= 2:
                        pool.wait_ge(xt_ps, e - 1)
                    for b in range(B):
                        n = b * E + e
                        pool.indirect_dma_start(xg[e % 2][:, b, :], None, xn_dram[:, :],
                                                bass.IndirectOffsetOnAxis(ap=idx[:, n:n + 1], axis=0)).then_inc(gat[e % 2], 16)

                pool.sem_inc(added, 2)
                pool.wait_ge(i_rdy, 2)
                gather(0)
                gather(1)
                for e in range(E):
                    if e % 2 == 0 and e + 2 < E:
                        gather(e + 2)
                        gather(e + 3)
                    if e == 0:
                        for q in range(2):
                            pool.wait_ge(out_dma[q], 32 + 32 * NS // 2)
                    else:
                        pool.wait_ge(scat[(e - 1) % 2], 32 * ((e - 1) // 2 + 1))
                        pool.sem_inc(added, 1)
                    pool.wait_ge(y_sb, NS + e + 3)
                    for b in range(B):
                        n = b * E + e
                        pool.indirect_dma_start(acc_dram[:, :], bass.IndirectOffsetOnAxis(ap=idx[:, n:n + 1], axis=0),
                                                eo[e % 2][:, b, :], None, compute_op=ALU.add).then_inc(scat[e % 2], 16)
                pool.wait_ge(scat[(E - 1) % 2], 32 * (E // 2))
                pool.sem_inc(added, 1)

            def up(pe, n, p, g, u, rhs):
                pe.wait_ge(ge_sb, n + 1)
                for f in range(FT):
                    for k in range(KT):
                        m = pe.matmul(ps[:, f // 2, (f % 2) * W:(f % 2 + 1) * W], g[:, k, f * P:(f + 1) * P], rhs[k],
                                      start=(k == 0), stop=(k == KT - 1))
                m.then_inc(g_ps, 1)
                pe.wait_ge(h_sb, n + 2)
                for f in range(FT):
                    for k in range(KT):
                        m = pe.matmul(ps[:, 2 + f // 2, (f % 2) * W:(f % 2 + 1) * W], u[:, k, f * P:(f + 1) * P], rhs[k],
                                      start=(k == 0), stop=(k == KT - 1))
                m.then_inc(u_ps, 1)

            def down(pe, n, p, w):
                pe.wait_ge(h_sb, n + 3)
                pe.wait_ge(y_sb, n + 1)
                for j in range(2):
                    for f in range(FT):
                        m = pe.matmul(ps[:, 4 + p, j * D:(j + 1) * D], hT[p][:, f, j * P:(j + 1) * P], w[:, f, :],
                                      start=(f == 0), stop=(f == FT - 1))
                m.then_inc(y_ps, 1)

            @block.tensor
            def _(pe):
                for t in range(NT):
                    for k in range(KT):
                        m = pe.matmul(ps[:, 7, t * E:(t + 1) * E], K.xnT[:, k, t * P:(t + 1) * P], gw[:, k, :],
                                      start=(k == 0), stop=(k == KT - 1))
                m.then_inc(l_ps, 1)
                pe.sem_inc(y_ps, 2)
                pe.wait_ge(sc_rdy, 1)
                for i in range(TB):
                    m = pe.transpose(ps[0:B * E, 6 + i // 4, (i % 4) * P:(i % 4 + 1) * P],
                                     sc[:, i, :, :].rearrange("p b e -> p (b e)"), K.ident[:, :])
                m.then_inc(v_ps, 1)

                def shared_pair(u):
                    for p in range(2):
                        rhs = [K.xnT[:, k, bass.ds((u + p) * W, W)] for k in range(KT)]
                        up(pe, u + p, p, sg, su, rhs)
                    for p in range(2):
                        down(pe, u + p, p, sd)

                with pe.Fori(0, (NS - 2) // 2) as pair:
                    u = 2 * pair
                    shared_pair(u)
                pe.wait_ge(t_rdy, 1)
                pe.transpose(ps[:, 6, 0:B * E], tf[:, :], K.ident[0:B * E, 0:B * E])
                pe.transpose(ps[:, 6, 128:128 + B * E], tw[:, :], K.ident[0:B * E, 0:B * E]).then_inc(t_ps, 1)
                shared_pair(NS - 2)
                pe.wait_ge(i_rdy, 2)
                with pe.Fori(0, E // 2) as pair:
                    e = 2 * pair
                    for p in range(2):
                        pe.wait_ge(gat[p], 32 * pair + 32)
                        pe.wait_ge(xt_sb, e + p + 1)
                        for k in range(KT):
                            for b in range(B):
                                m = pe.transpose(ps[:, 6 + p, (k * B + b) * P:(k * B + b + 1) * P],
                                                 xg[p][:, b, k * P:(k + 1) * P], K.ident[:, :])
                        m.then_inc(xt_ps, 1)
                    for p in range(2):
                        pe.wait_ge(xt_sb, e + p + 3)
                        pe.wait_ge(w_in[p], 32 * pair + 32)
                        up(pe, e + p + NS, p, wg[p], wu[p], [xgT[p][:, k, :] for k in range(KT)])
                    for p in range(2):
                        pe.wait_ge(d_in[p], 16 * pair + 16)
                        down(pe, e + p + NS, p, wd[p])

            @block.scalar
            def _(act):
                def gelu(n, p):
                    act.wait_ge(g_ps, n + 1)
                    act.wait_ge(h_sb, n + 1)
                    act.activation(ge[p][:, :], ps[:, 0:2, :].rearrange("p a c -> p (a c)"), ACT.Gelu).then_inc(ge_sb, 1)

                act.sem_inc(ge_sb, 1)
                act.sem_inc(y_sb, 2)
                act.sem_inc(xt_sb, 2)
                act.wait_ge(exp_in, 1)
                act.activation(lg[:, :, :], lg[:, :, :], ACT.Exp).then_inc(exp_done, 1)
                with act.Fori(0, NS // 2) as pair:
                    u = 2 * pair
                    for p in range(2):
                        gelu(u + p, p)
                    for p in range(2):
                        act.wait_ge(y_ps, u + p + 3)
                        act.wait_ge(out_dma[p], 32 * pair + 32)
                        act.activation(eo[p][:, :, :].rearrange("p a c -> p (a c)"), ps[:, 4 + p, :],
                                       ACT.Copy).then_inc(y_sb, 1)
                with act.Fori(0, E // 2) as pair:
                    e = 2 * pair
                    for p in range(2):
                        act.wait_ge(xt_ps, e + p + 1)
                        act.wait_ge(u_ps, e + p + NS - 1)
                        act.activation(xgT[p][:, :, :].rearrange("p a c -> p (a c)"), ps[:, 6 + p, :],
                                       ACT.Copy).then_inc(xt_sb, 1)
                    for p in range(2):
                        gelu(e + p + NS, p)

            @block.vector
            def _(dve):
                dve.sem_inc(h_sb, 2)
                for p in range(2):
                    dve.sem_inc(out_dma[p], 32)
                s = Steps(smx)

                def then(ins):
                    s.did(ins)
                    dve.wait_ge(smx, s.last())

                dve.wait_ge(l_ps, 1)
                logits = ps[:, 7, 0:NT * E].rearrange("p (t e) -> p t e", t=NT)
                then(dve.tensor_reduce(vec[:, 0, :], logits, AX.X, ALU.max))
                dve.tensor_tensor(lg[:, :, :], logits, vec[:, 0, :].unsqueeze(2).broadcast_to([P, NT, E]),
                                  ALU.subtract).then_inc(exp_in, 1)
                dve.wait_ge(exp_done, 1)
                then(dve.tensor_reduce(vec[:, 1, :], lg[:, :, :], AX.X, ALU.add))
                then(dve.reciprocal(vec[:, 2, :], vec[:, 1, :]))
                dve.tensor_tensor(sc[:, :, :, :].rearrange("p i b e -> p b i e"),
                                  lg[:, :, :].rearrange("p (b i) e -> p b i e", b=B),
                                  vec[:, 2, :].rearrange("p (b i) -> p b i", b=B).unsqueeze(3).broadcast_to([P, B, TB, E]),
                                  ALU.mult).then_inc(sc_rdy, 1)
                dve.wait_ge(v_ps, 1)
                then(dve.tensor_copy(va[0][:, :], ps[0:B * E, 6:8, :].rearrange("p a c -> p (a c)")))

                def pick(r):
                    best = tw[:, 8 * r:8 * r + 8]
                    then(dve.max(best, va[r % 2][:, :]))
                    dve.max_index(ti[:, 8 * r:8 * r + 8], best, va[r % 2][:, :]).then_inc(rnd, 1)
                    then(dve.match_replace(va[1 - r % 2][:, :], best, va[r % 2][:, :], -1.0))

                def hidden(n, p):
                    dve.wait_ge(ge_sb, n + 2)
                    dve.wait_ge(u_ps, n + 1)
                    dve.wait_ge(y_ps, n + 1)
                    dve.tensor_tensor(hT[p][:, :, :].rearrange("p a c -> p (a c)"), ge[p][:, :],
                                      ps[:, 2:4, :].rearrange("p a c -> p (a c)"), ALU.mult).then_inc(h_sb, 1)

                r = 0
                for u in range(NS):
                    if u < len(per_unit):
                        for _ in range(per_unit[u]):
                            pick(r)
                            r += 1
                    hidden(u, u % 2)
                    if r == ROUNDS and u == len(per_unit) - 1:
                        dve.wait_ge(rnd, ROUNDS)
                        dve.wait_ge(off, 2)
                        dve.tensor_scalar(tf[:, :], ti[:, :], boff[:, 0:1], None, ALU.add).then_inc(t_rdy, 1)
                        dve.wait_ge(t_ps, 1)
                        dve.tensor_copy(idx[:, :], ps[:, 6, 0:B * E]).then_inc(i_rdy, 1)
                        dve.tensor_copy(wcol[:, :], ps[:, 6, 128:128 + B * E]).then_inc(i_rdy, 1)
                dve.wait_ge(i_rdy, 2)
                for p in range(2):
                    dve.wait_ge(out_dma[p], 32 + 32 * NS // 2)
                with dve.Fori(0, E // 2) as pair:
                    e = 2 * pair
                    for p in range(2):
                        hidden(e + p + NS, p)
                    for p in range(2):
                        dve.wait_ge(y_ps, e + p + NS + 3)
                        dve.wait_ge(added, e + p + 1)
                        for b in range(B):
                            m = dve.tensor_scalar(eo[p][:, b, :], ps[:, 4 + p, b * D:(b + 1) * D],
                                                  wcol[:, bass.ds(e + p + b * E, 1)], None, ALU.mult)
                        m.then_inc(y_sb, 1)
                for q in range(4):
                    dve.wait_ge(acc_in[q % 2], 16 * (q // 2 + 1))
                    xt = K.x[:, 4 * q:4 * q + 4, :]
                    dve.scalar_tensor_tensor(xt, acc[q % 2][:, :, :], gate, xt, ALU.mult, ALU.add).then_inc(x_done, 1)


def top2_ffn(nc, ctx, K, tag, layer, gw, w1, w3, w2, n_weights, xn_dram, acc_dram, out):
    E, F, TOP = 8, 512, 2
    FT = F // P
    ps = K.ps
    NTILE = (TOP * B * S + E * (P - 1)) // P
    NTILE += NTILE % 2
    NPAIR = NTILE // 2
    gate = K.gate[:, 1, layer:layer + 1]
    with ExitStack() as c:
        take = sbuf(nc, c, tag + "take", [P, NTILE], U32)
        give = sbuf(nc, c, tag + "give", [P, NTILE], U32)
        weight = sbuf(nc, c, tag + "weight", [P, NTILE])
        te = sbuf(nc, c, tag + "te", [1, NTILE], I32)

        with ExitStack() as r:
            pr = sbuf(nc, r, tag + "pr", [P, NT, E])
            oh = sbuf(nc, r, tag + "oh", [P, TOP, NT, E])
            both = sbuf(nc, r, tag + "both", [P, NT, E])
            tmp = sbuf(nc, r, tag + "tmp", [P, 3, NT, E])
            vec = sbuf(nc, r, tag + "vec", [P, 8, NT])
            ev = sbuf(nc, r, tag + "ev", [P, 6, E])
            gwt = sbuf(nc, r, tag + "gwt", [P, TOP, NT])
            slf = sbuf(nc, r, tag + "slf", [P, TOP, NT])
            hi = sbuf(nc, r, tag + "hi", [P, TOP, NT])
            lo = sbuf(nc, r, tag + "lo", [P, TOP, NT])
            in_lane = sbuf(nc, r, tag + "in_lane", [P, TOP, NT, P])
            in_tile = sbuf(nc, r, tag + "in_tile", [P, TOP, NT, 2, NTILE])
            empty = sbuf(nc, r, tag + "empty", [P, NTILE])
            tri = sbuf(nc, r, tag + "tri", [P, P])
            rev_i = sbuf(nc, r, tag + "rev_i", [P, E], I32)
            rev = sbuf(nc, r, tag + "rev", [P, E])
            jrow_i = sbuf(nc, r, tag + "jrow_i", [P, NTILE], I32)
            jrow = sbuf(nc, r, tag + "jrow", [P, NTILE])
            lane_i = sbuf(nc, r, tag + "lane_i", [P, P], I32)
            lane = sbuf(nc, r, tag + "lane", [P, P])
            tok_i = sbuf(nc, r, tag + "tok_i", [P, NT], I32)
            tok = sbuf(nc, r, tag + "tok", [P, NT])
            dump_i = sbuf(nc, r, tag + "dump_i", [P, 1], I32)
            dump = sbuf(nc, r, tag + "dump", [P, 1])
            cmp = sbuf(nc, r, tag + "cmp", [1, NTILE, E])
            cnt = sbuf(nc, r, tag + "cnt", [1, 2, NTILE])
            l_ps, step, exp_in, exp_done, const, oh_rdy, rank_ps, lo_rdy, lane_rdy, tile_rdy, slot_ps, rows_out = semaphores(
                nc, r, tag, "l_ps step exp_in exp_done const oh_rdy rank_ps lo_rdy lane_rdy tile_rdy slot_ps rows_out")
            with nc.Block() as block:
                @block.sync
                def _(sp):
                    for dst, src in ((xn_dram, K.xn), (acc_dram, K.x)):
                        for q in range(2):
                            sp.dma_start(dst[q * S:(q + 1) * S, :].rearrange("(t p) d -> p t d", p=P),
                                         src[:, TB * q:TB * (q + 1), :]).then_inc(rows_out, 16)
                    sp.dma_start(acc_dram[B * S:B * S + P, :], K.zeros[:, :]).then_inc(rows_out, 16)
                    sp.wait_ge(rows_out, 5 * 16)

                @block.tensor
                def _(pe):
                    for t in range(NT):
                        for k in range(KT):
                            m = pe.matmul(ps[:, 0, t * E:(t + 1) * E], K.xnT[:, k, t * P:(t + 1) * P], gw[:, k, :],
                                          start=(k == 0), stop=(k == KT - 1))
                    m.then_inc(l_ps, 1)
                    pe.wait_ge(oh_rdy, 1)
                    pe.wait_ge(const, 6)
                    flat = both[:, :, :].rearrange("p t e -> p (t e)")
                    pe.matmul(ps[:, 2, 0:NT * E], K.ones[:, :], flat, start=True, stop=True)
                    pe.matmul(ps[:, 1, 0:NT * E], tri[:, :], flat, start=True, stop=False, skip_group_check=True)
                    for n in range(1, NT):
                        m = pe.matmul(ps[:, 1, n * E:NT * E], K.ones[:, :], flat[:, 0:(NT - n) * E], start=False,
                                      stop=(n == NT - 1), skip_group_check=True)
                    m.then_inc(rank_ps, 1)
                    pe.wait_ge(tile_rdy, 1)
                    for n in range(TOP):
                        pe.wait_ge(lane_rdy, n + 1)
                        for t in range(NT):
                            m = pe.matmul(ps[:, 3, 0:2 * NTILE], in_lane[:, n, t, :],
                                          in_tile[:, n, t, :, :].rearrange("p a j -> p (a j)"),
                                          start=(n == 0 and t == 0), stop=(n == TOP - 1 and t == NT - 1))
                    m.then_inc(slot_ps, 1)

                @block.scalar
                def _(act):
                    act.wait_ge(exp_in, 1)
                    act.activation(pr[:, :, :], pr[:, :, :], ACT.Exp).then_inc(exp_done, 1)

                @block.gpsimd
                def _(pool):
                    pool.iota(rev_i[:, :], [[-1, E]], base=E, channel_multiplier=0).then_inc(const, 1)
                    pool.iota(jrow_i[:, :], [[1, NTILE]], base=0, channel_multiplier=0).then_inc(const, 1)
                    pool.iota(lane_i[:, :], [[1, P]], base=0, channel_multiplier=0).then_inc(const, 1)
                    pool.iota(tok_i[:, :], [[P, NT]], base=1, channel_multiplier=1).then_inc(const, 1)
                    pool.iota(dump_i[:, :], [[1, 1]], base=B * S + 1, channel_multiplier=1).then_inc(const, 1)
                    pool.affine_select(out=tri[:, :], in_=K.ones[:, :], compare_op=ALU.is_ge, fill=0.0, base=-1,
                                       pattern=[[1, P]], channel_multiplier=-1).then_inc(const, 1)

                @block.vector
                def _(dve):
                    s = Steps(step)

                    def then(ins):
                        s.did(ins)
                        dve.wait_ge(step, s.last())

                    def wide(v):
                        return v.unsqueeze(2).broadcast_to([P, NT, E])

                    def per_expert(v):
                        return v.unsqueeze(1).broadcast_to([P, NT, E])

                    dve.wait_ge(const, 5)
                    for f, i in ((rev, rev_i), (jrow, jrow_i), (lane, lane_i), (tok, tok_i), (dump, dump_i)):
                        s.did(dve.tensor_copy(f[:, :], i[:, :]))
                    dve.wait_ge(step, s.last())
                    dve.wait_ge(l_ps, 1)
                    logits = ps[:, 0, 0:NT * E].rearrange("p (t e) -> p t e", t=NT)
                    then(dve.tensor_reduce(vec[:, 0, :], logits, AX.X, ALU.max))
                    dve.tensor_tensor(pr[:, :, :], logits, wide(vec[:, 0, :]), ALU.subtract).then_inc(exp_in, 1)
                    dve.wait_ge(exp_done, 1)
                    then(dve.tensor_reduce(vec[:, 1, :], pr[:, :, :], AX.X, ALU.add))
                    then(dve.reciprocal(vec[:, 2, :], vec[:, 1, :]))
                    then(dve.tensor_tensor(pr[:, :, :], pr[:, :, :], wide(vec[:, 2, :]), ALU.mult))
                    src = pr
                    for n in range(TOP):
                        best = vec[:, 3 + n, :]
                        then(dve.tensor_reduce(best, src[:, :, :], AX.X, ALU.max))
                        then(dve.tensor_tensor(tmp[:, 0, :, :], src[:, :, :], wide(best), ALU.is_equal))
                        then(dve.tensor_tensor(tmp[:, 1, :, :], tmp[:, 0, :, :], per_expert(rev[:, :]), ALU.mult))
                        then(dve.tensor_reduce(vec[:, 5, :], tmp[:, 1, :, :], AX.X, ALU.max))
                        then(dve.tensor_tensor(oh[:, n, :, :], tmp[:, 1, :, :], wide(vec[:, 5, :]), ALU.is_equal))
                        if n == 0:
                            then(dve.scalar_tensor_tensor(tmp[:, 2, :, :], oh[:, 0, :, :], -2.0, pr[:, :, :],
                                                          ALU.mult, ALU.add))
                            src = tmp[:, 2, :, :]
                    dve.tensor_tensor(both[:, :, :], oh[:, 0, :, :], oh[:, 1, :, :], ALU.add).then_inc(oh_rdy, 1)
                    then(dve.tensor_tensor(vec[:, 6, :], vec[:, 3, :], vec[:, 4, :], ALU.add))
                    then(dve.reciprocal(vec[:, 7, :], vec[:, 6, :]))
                    then(dve.tensor_scalar(vec[:, 7, :], vec[:, 7, :], gate, None, ALU.mult))
                    for n in range(TOP):
                        s.did(dve.tensor_tensor(gwt[:, n, :], vec[:, 3 + n, :], vec[:, 7, :], ALU.mult))
                    dve.wait_ge(rank_ps, 1)
                    then(dve.tensor_reduce(ev[:, 0, :], ps[:, 2, 0:NT * E].rearrange("p (t e) -> p e t", t=NT), AX.X, ALU.add))
                    then(dve.tensor_scalar(ev[:, 1, :], ev[:, 0, :], 1.0 / P, (P - 1.0) / (2 * P), ALU.mult, ALU.add))
                    then(dve.tensor_scalar(ev[:, 2, :], ev[:, 1, :], MAGIC, MAGIC, ALU.add, ALU.subtract))
                    then(dve.tensor_tensor_scan(ev[:, 3, :], K.ones[:, 0:E], ev[:, 2, :], 0.0, ALU.mult, ALU.add))
                    then(dve.tensor_tensor(ev[:, 4, :], ev[:, 3, :], ev[:, 2, :], ALU.subtract))
                    then(dve.scalar_tensor_tensor(tmp[:, 0, :, :], per_expert(ev[:, 4, :]), float(P),
                                                  ps[:, 1, 0:NT * E].rearrange("p (t e) -> p t e", t=NT),
                                                  ALU.mult, ALU.add))
                    for n in range(TOP):
                        then(dve.tensor_tensor(tmp[:, 1, :, :], oh[:, n, :, :], tmp[:, 0, :, :], ALU.mult))
                        then(dve.tensor_reduce(slf[:, n, :], tmp[:, 1, :, :], AX.X, ALU.add))
                    then(dve.tensor_scalar(hi[:, :, :], slf[:, :, :], 1.0 / P, (P - 1.0) / (2 * P), ALU.mult, ALU.subtract))
                    then(dve.tensor_scalar(hi[:, :, :], hi[:, :, :], MAGIC, MAGIC, ALU.add, ALU.subtract))
                    then(dve.scalar_tensor_tensor(lo[:, :, :], hi[:, :, :], -float(P), slf[:, :, :], ALU.mult, ALU.add))
                    for n in range(TOP):
                        def tiles(v):
                            return v.unsqueeze(2).broadcast_to([P, NT, NTILE])
                        then(dve.tensor_tensor(in_tile[:, n, :, 0, :], tiles(hi[:, n, :]),
                                               jrow[:, :].unsqueeze(1).broadcast_to([P, NT, NTILE]), ALU.is_equal))
                        then(dve.tensor_tensor(in_tile[:, n, :, 1, :], in_tile[:, n, :, 0, :], tiles(gwt[:, n, :]), ALU.mult))
                        m = dve.tensor_tensor(in_tile[:, n, :, 0, :], in_tile[:, n, :, 0, :], tiles(tok[:, :]), ALU.mult)
                    m.then_inc(tile_rdy, 1)
                    for n in range(TOP):
                        dve.tensor_tensor(in_lane[:, n, :, :], lo[:, n, :].unsqueeze(2).broadcast_to([P, NT, P]),
                                          lane[:, :].unsqueeze(1).broadcast_to([P, NT, P]), ALU.is_equal).then_inc(lane_rdy, 1)
                    then(dve.tensor_tensor(cmp[:, :, :], ev[0:1, 3, :].unsqueeze(1).broadcast_to([1, NTILE, E]),
                                           jrow[0:1, :].unsqueeze(2).broadcast_to([1, NTILE, E]), ALU.is_le))
                    then(dve.tensor_reduce(cnt[:, 0, :], cmp[:, :, :], AX.X, ALU.add))
                    then(dve.tensor_scalar(te[:, :], cnt[:, 0, :], E - 1.0, None, ALU.min))
                    dve.wait_ge(slot_ps, 1)
                    of_slot = ps[:, 3, 0:NTILE]
                    s.did(dve.tensor_scalar(take[:, :], of_slot, -1.0, 0.0, ALU.add, ALU.max))
                    then(dve.tensor_scalar(empty[:, :], of_slot, 0.0, dump[:, 0:1], ALU.is_equal, ALU.mult))
                    s.did(dve.scalar_tensor_tensor(give[:, :], of_slot, -1.0, empty[:, :], ALU.add, ALU.add))
                    s.did(dve.tensor_copy(weight[:, :], ps[:, 3, NTILE:2 * NTILE]))

        with ExitStack() as r:
            xs = [sbuf(nc, r, tag + f"xs{i}", [P, D]) for i in range(2)]
            xsT = sbuf(nc, r, tag + "xsT", [P, 2 * KT * P])
            s1 = [sbuf(nc, r, tag + f"s1{i}", [P, F]) for i in range(2)]
            hid = [sbuf(nc, r, tag + f"hid{i}", [P, F]) for i in range(2)]
            hT = [sbuf(nc, r, tag + f"hT{i}", [P, F]) for i in range(2)]
            yo = [sbuf(nc, r, tag + f"yo{i}", [P, D]) for i in range(2)]
            X_BANK, HT_BANK, Y_BANK = 6, (4, 7), (5, 4)
            xt_ps, xt_sb, h1_ps, up_ps, silu, h_sb, ht_ps, ht_sb, y_ps, y_sb, yo_free, all_in, stored = semaphores(
                nc, r, tag, "xt_ps xt_sb h1_ps up_ps silu h_sb ht_ps ht_sb y_ps y_sb yo_free all_in stored")
            x_in, y_out = K.rows_taken, K.rows_given
            with nc.Block() as block:
                @block.gpsimd
                def _(pool):
                    def gather(j):
                        pool.indirect_dma_start(xs[j % 2][:, :], None, xn_dram[:, :],
                                                bass.IndirectOffsetOnAxis(ap=take[:, j:j + 1], axis=0)).then_inc(x_in[j % 2], 16)

                    for p in range(2):
                        gather(p)
                    pool.sem_inc(yo_free, 2)
                    pool.wait_ge(xt_ps, 1)
                    for p in range(2):
                        gather(2 + p)
                    for j in range(NTILE):
                        if j % 2 == 0 and j + 4 < NTILE:
                            pool.wait_ge(xt_ps, j // 2 + 2)
                            for p in range(2):
                                gather(j + 4 + p)
                        if j:
                            pool.wait_ge(y_out[(j - 1) % 2], 16 * ((j - 1) // 2 + 1))
                            pool.sem_inc(yo_free, 1)
                        pool.wait_ge(y_sb, j + 3)
                        pool.indirect_dma_start(acc_dram[:, :], bass.IndirectOffsetOnAxis(ap=give[:, j:j + 1], axis=0),
                                                yo[j % 2][:, :], None, compute_op=ALU.add).then_inc(y_out[j % 2], 16)
                    for p in range(2):
                        pool.wait_ge(y_out[p], 16 * NPAIR)
                    pool.sem_inc(all_in, 1)

                @block.sync
                def _(sp):
                    flat = out.rearrange("b s d -> (b s) d")
                    sp.wait_ge(all_in, 1)
                    for q in range(4):
                        rows = slice(q * B * S // 4, (q + 1) * B * S // 4)
                        sp.dma_start(flat[rows, :], acc_dram[rows, :]).then_inc(stored, 16)
                    sp.wait_ge(stored, 64)

                @block.tensor
                def _(pe):
                    def turn(k):
                        pe.wait_ge(xt_sb, k + 1)
                        for p in range(2):
                            pe.wait_ge(x_in[p], 16 * k + 16)
                            for n in range(KT):
                                m = pe.transpose(ps[:, X_BANK, (p * KT + n) * P:(p * KT + n + 1) * P],
                                                 xs[p][:, n * P:(n + 1) * P], K.ident[:, :])
                        m.then_inc(xt_ps, 1)

                    def pair(k, last):
                        expert = []
                        pe.wait_ge(xt_sb, k + 2)
                        for p in range(2):
                            j = 2 * k + p
                            where = te[0:1, j:j + 1] if last else te[0:1, bass.ds(j, 1)]
                            e = pe.value_load(where, min_val=0, max_val=E - 1)
                            expert.append(e)
                            pe.wait_ge(h_sb, j + 1)
                            for n, w in enumerate((w1, w3)):
                                for i in range(KT):
                                    m = pe.matmul(ps[:, 2 * p + n, :], xsT[:, (p * KT + i) * P:(p * KT + i + 1) * P],
                                                  w[:, e, i, :], start=(i == 0), stop=(i == KT - 1))
                                m.then_inc((h1_ps, up_ps)[n], 1)
                        if not last:
                            turn(k + 1)
                        pe.wait_ge(y_sb, 2 * k + 2)
                        for p in range(2):
                            j = 2 * k + p
                            pe.wait_ge(h_sb, j + 3)
                            pe.wait_ge(ht_sb, j + 1)
                            for f in range(FT):
                                m = pe.transpose(ps[:, HT_BANK[p], f * P:(f + 1) * P], hid[p][:, f * P:(f + 1) * P],
                                                 K.ident[:, :])
                            m.then_inc(ht_ps, 1)
                        for p in range(2):
                            j = 2 * k + p
                            pe.wait_ge(ht_sb, j + 3)
                            pe.wait_ge(y_sb, j + 1)
                            for f in range(FT):
                                m = pe.matmul(ps[:, Y_BANK[p], 0:D], hT[p][:, f * P:(f + 1) * P], w2[:, expert[p], f, :],
                                              start=(f == 0), stop=(f == FT - 1))
                            m.then_inc(y_ps, 1)

                    for sem in (ht_ps, y_ps):
                        pe.sem_inc(sem, 2)
                    pe.wait_ge(K.experts_in, 16 * n_weights)
                    turn(0)
                    with pe.Fori(0, NPAIR - 1) as k:
                        pair(k, False)
                    pair(NPAIR - 1, True)

                @block.scalar
                def _(act):
                    with act.Fori(0, NPAIR) as k:
                        for p in range(2):
                            j = 2 * k + p
                            act.wait_ge(h1_ps, j + 1)
                            act.wait_ge(h_sb, j + 1)
                            act.activation(s1[p][:, :], ps[:, 2 * p, :], ACT.Silu).then_inc(silu, 1)

                @block.vector
                def _(dve):
                    def copy_turned(k):
                        dve.wait_ge(xt_ps, k + 1)
                        dve.tensor_copy(xsT[:, :], ps[:, X_BANK, :]).then_inc(xt_sb, 1)

                    def pair(k, last):
                        for p in range(2):
                            j = 2 * k + p
                            dve.wait_ge(silu, j + 1)
                            dve.wait_ge(up_ps, j + 1)
                            dve.wait_ge(ht_ps, j + 1)
                            dve.tensor_tensor(hid[p][:, :], s1[p][:, :], ps[:, 2 * p + 1, :], ALU.mult).then_inc(h_sb, 1)
                        if not last:
                            copy_turned(k + 1)
                        for p in range(2):
                            j = 2 * k + p
                            dve.wait_ge(ht_ps, j + 3)
                            dve.wait_ge(y_ps, j + 1)
                            dve.tensor_copy(hT[p][:, :], ps[:, HT_BANK[p], :]).then_inc(ht_sb, 1)
                        for p in range(2):
                            j = 2 * k + p
                            dve.wait_ge(y_ps, j + 3)
                            dve.wait_ge(yo_free, j + 1)
                            of_tile = weight[:, j:j + 1] if last else weight[:, bass.ds(j, 1)]
                            dve.tensor_scalar(yo[p][:, :], ps[:, Y_BANK[p], 0:D], of_tile, None, ALU.mult).then_inc(y_sb, 1)

                    dve.sem_inc(h_sb, 2)
                    dve.sem_inc(ht_sb, 2)
                    dve.sem_inc(y_sb, 2)
                    dve.sem_inc(xt_sb, 1)
                    copy_turned(0)
                    with dve.Fori(0, NPAIR - 1) as k:
                        pair(k, False)
                    pair(NPAIR - 1, True)


def store_result(nc, ctx, K, out):
    (s_st,) = semaphores(nc, ctx, "store_", "dma")
    with nc.Block() as block:
        @block.sync
        def _(sp):
            sp.dma_start(out.rearrange("b (t p) d -> p (b t) d", p=P), K.x[:, :, :]).then_inc(s_st, 16)
            sp.wait_ge(s_st, 16)


def flamingo(nc, ins, out):
    K = Core()
    with ExitStack() as ctx:
        load_and_constants(nc, ctx, K, ins)
        K.row_gathered = software_dma_semaphores(nc, ctx, "row_gathered", "0 1")
        K.row_scattered = software_dma_semaphores(nc, ctx, "row_scattered", "0 1")
        K.rows_taken = software_dma_semaphores(nc, ctx, "rows_taken", "0 1")
        K.rows_given = software_dma_semaphores(nc, ctx, "rows_given", "0 1")

        def stage(n):
            sub = ExitStack()
            return sub, Weights(nc, sub, ins)

        def transposed_rows(sub):
            K.xnT = sbuf(nc, sub, "xnT_sb", [P, KT, B * S])

        if 0 in _STAGES:
            sub, w = stage(0)
            with sub:
                transposed_rows(sub)
                wq, wk, wv, wo = (w.rows("L0_xattn_W" + n) for n in "qkvo")
                bq, bk = w.same("L0_xattn_bq"), w.same("L0_xattn_bk")
                bv, bo = w.repeated("L0_xattn_bv", 1), w.repeated("L0_xattn_bo")
                norm = Norm(nc, sub, K, "n0_", w.loads, banks=4)
                multihead(nc, sub, K, "a0_", norm, 0, wq, wk, wv, wo, bq, bk, bv, bo, mask=ins["mask_1x1xSxS2_ik0"])
        if 1 in _STAGES:
            sub, w = stage(1)
            with sub:
                transposed_rows(sub)
                gw, sg, su, sd = (w.rows("L0_ffn_" + n) for n in ("gate_w", "Ws_g", "Ws_u", "Ws_d"))
                xn_dram = nc.dram_tensor("xn_rows_1", (B * S, D), F32, kind="Internal").ap()
                acc_dram = nc.dram_tensor("acc_rows_1", (B * S, D), F32, kind="Internal").ap()
                norm_block(nc, sub, K, "n1_", w.loads, to_dram=xn_dram)
                expert_choice_ffn(nc, sub, K, "f1_", 0, gw, sg, su, sd, ins["L0_ffn_Wg"], ins["L0_ffn_Wu"],
                                  ins["L0_ffn_Wd"], xn_dram, acc_dram)
        if 2 in _STAGES:
            sub, w = stage(2)
            with sub:
                transposed_rows(sub)
                wq, wk, wv = w.same("L1_xattn_Wq"), w.rows("L1_xattn_Wk"), w.rows("L1_xattn_Wv")
                bq, bk, bv = w.same("L1_xattn_bq"), w.same("L1_xattn_bk"), w.repeated("L1_xattn_bv", L)
                norm_block(nc, sub, K, "n2_", w.loads)
                sigmoid_attention(nc, sub, K, "a2_", 1, wq, wk, wv, bq, bk, bv)
        if 3 in _STAGES:
            sub, w = stage(3)
            with sub:
                w1, w2 = w.rows("L1_ffn_w1"), w.rows("L1_ffn_w2")
                cw, cb = w.same("L1_ffn_conv_w"), w.same("L1_ffn_conv_b")
                norm_block(nc, sub, K, "n3_", w.loads, transposed=False)
                bitnet_ffn(nc, sub, K, "f3_", 1, w1, w2, cw, cb)
        clear_semaphores(nc)
        if 4 in _STAGES:
            sub, w = stage(4)
            with sub:
                transposed_rows(sub)
                wT, wn, bc = w.rows("L2_xattn_W"), w.rows("L2_xattn_Wn"), w.same("L2_xattn_b")
                norm_block(nc, sub, K, "n4_", w.loads)
                align_attention(nc, sub, K, "a4_", 2, wT, wn, bc)
        if 5 in _STAGES:
            sub, w = stage(5)
            with sub:
                transposed_rows(sub)
                wu, wd = w.rows("L2_ffn_w_up"), w.rows("L2_ffn_w_down")
                norm_block(nc, sub, K, "n5_", w.loads, ternary=True)
                ternary_ffn(nc, sub, K, "f5_", 2, wu, wd)
        late = Weights(nc, ctx, ins)
        w1, w3 = (late.experts("L3_ffn_" + n) for n in ("w1", "w3"))
        (K.experts_in,) = semaphores(nc, ctx, "experts_", "in")
        if 6 in _STAGES:
            sub, w = stage(6)
            with sub:
                transposed_rows(sub)
                wq, wk, wv, wo = (w.rows("L3_xattn_w_" + n) for n in "qkvo")
                norm = Norm(nc, sub, K, "n6_", w.loads, banks=4, prefetch=late.loads)
                multihead(nc, sub, K, "a6_", norm, 3, wq, wk, wv, wo)
        if 7 in _STAGES:
            sub, w = stage(7)
            with sub:
                transposed_rows(sub)
                gw = w.rows("L3_ffn_wg")
                xn_dram = nc.dram_tensor("xn_rows_7", (B * S, D), F32, kind="Internal").ap()
                acc_dram = nc.dram_tensor("acc_rows_7", (B * S + P, D), F32, kind="Internal").ap()
                down = Weights(nc, sub, ins)
                w2 = down.experts("L3_ffn_w2")
                norm_block(nc, sub, K, "n7_", w.loads, prefetch=down.loads if 6 in _STAGES else late.loads + down.loads)
                top2_ffn(nc, sub, K, "f7_", 3, gw, w1, w3, w2, len(late.loads + down.loads), xn_dram, acc_dram, out)
        else:
            store_result(nc, ctx, K, out)


def kernel(**inputs):
    import concourse.bacc as _bacc
    from concourse.bass_utils import run_bass_kernel_spmd as _run

    nc = _bacc.Bacc("TRN2", target_bir_lowering=False, num_devices=1)

    def laid(name):
        a = np.asarray(inputs[name])
        if name in _FLIP:
            a = np.swapaxes(a, -1, -2)
        if name == "L1_ffn_conv_w":
            a = a.reshape(8, P, 3).transpose(1, 0, 2)
        if name in ("L1_xattn_bq", "L1_xattn_bk"):
            a = a.reshape(64, 1)
        if name in _COLUMNS:
            a = a.reshape(-1, P).T
        if name == "mask_1x1xSxS2_ik0":
            a = a.reshape(S, L)
        return np.ascontiguousarray(a)

    arrays = {n: laid(n) for n in _NAMES}
    arrays["L2_xattn_Wn"] = np.ascontiguousarray(np.asarray(inputs["L2_xattn_W"]))
    arrays["gates"] = np.stack([np.asarray(inputs["g_xattn"]), np.asarray(inputs["g_ffn"])])
    aps = {n: nc.dram_tensor("in_" + n, a.shape, mybir.dt.from_np(a.dtype), kind="ExternalInput").ap()
           for n, a in arrays.items()}
    out = nc.dram_tensor("out_x", (B, S, D), F32, kind="ExternalOutput").ap()
    flamingo(nc, aps, out)
    r = _run(nc, [{"in_" + n: a for n, a in arrays.items()}], core_ids=[0])
    return r.results[0]["out_x"]


_COLUMNS = ("L0_xattn_bq", "L0_xattn_bk", "L1_ffn_conv_b", "L2_xattn_b")
_FLIP = ("L3_ffn_wg", "L3_ffn_w1", "L3_ffn_w3", "L3_ffn_w2", "L0_ffn_gate_w", "L0_ffn_Ws_g", "L0_ffn_Ws_u", "L0_ffn_Ws_d", "L0_ffn_Wg", "L0_ffn_Wu", "L0_ffn_Wd",
         "L0_xattn_Wq", "L0_xattn_Wk", "L0_xattn_Wv", "L0_xattn_Wo", "L1_xattn_Wk", "L1_xattn_Wv",
         "L1_ffn_w1", "L1_ffn_w2", "L2_xattn_W", "L2_ffn_w_up", "L2_ffn_w_down",
         "L3_xattn_w_q", "L3_xattn_w_k", "L3_xattn_w_v", "L3_xattn_w_o")
_NAMES = ("x", "ctx_1024", "mask_1x1xSxS2_ik0", "L0_xattn_bv", "L0_xattn_bo", "L1_xattn_Wq",
          "L1_xattn_bq", "L1_xattn_bk", "L1_xattn_bv", "L1_ffn_conv_w") + _COLUMNS + _FLIP
```

```python
from contextlib import ExitStack

import numpy as np

import concourse.bass as bass
from concourse import mybir

F32 = mybir.dt.float32
F32R = mybir.dt.float32r
BF16 = mybir.dt.bfloat16
I32 = mybir.dt.int32
U32 = mybir.dt.uint32
ALU = mybir.AluOpType
ACT = mybir.ActivationFunctionType
AX = mybir.AxisListType

P = 128
B, S, D = 2, 1024, 256
NT = B * S // P
TB = S // P
KT = D // P
L = 77
H, HD = 16, 16
LN_EPS = 1e-5
MAGIC = 1.5 * 2.0 ** 23

_used = {}
_made = []


class Steps:

    def __init__(self, sem, base=0):
        self.sem, self.base, self.n = sem, base, 0

    def did(self, ins):
        self.n += 1
        return ins.then_inc(self.sem, 1)

    def last(self):
        return self.base + self.n


class Core:
    pass


def sbuf(nc, ctx, name, shape, dt=F32):
    _used[name] = _used.get(name, 0) + 1
    name = f"{name}_{_used[name]}"
    return ctx.enter_context(nc.sbuf_tensor(name, shape, dt))


def semaphores(nc, ctx, prefix, names):
    made = [ctx.enter_context(nc.semaphore(prefix + n)) for n in names.split()]
    _made.extend(made)
    return made


def lasting_semaphores(nc, ctx, prefix, names):
    return [ctx.enter_context(nc.semaphore(prefix + n)) for n in names.split()]


def clear_semaphores(nc):
    with nc.Block() as block:
        @block.gpsimd
        def _(pool):
            for sem in _made:
                pool.sem_clear(sem)
    _made.clear()


def load_and_constants(nc, ctx, K, ins):
    K.ps = ctx.enter_context(nc.psum_tensor("ps", [P, 8, 512], F32))
    K.x = sbuf(nc, ctx, "x_sb", [P, NT, D])
    K.xn = sbuf(nc, ctx, "xn_sb", [P, NT, D])
    K.ident = sbuf(nc, ctx, "ident", [P, P])
    K.identb = sbuf(nc, ctx, "identb", [P, P], BF16)
    K.zeros = sbuf(nc, ctx, "zeros", [P, D])
    K.ones = sbuf(nc, ctx, "ones", [P, P])
    K.shift = sbuf(nc, ctx, "shift", [P, 336])
    K.headmask = sbuf(nc, ctx, "headmask", [P, 8])
    K.npow = sbuf(nc, ctx, "npow", [P, NT])
    K.hpow = sbuf(nc, ctx, "hpow", [P, NT])
    K.gate = sbuf(nc, ctx, "gates", [P, 2, 4])
    K.ctx_nat = sbuf(nc, ctx, "ctx_nat", [L, B, D])
    K.ctxT = sbuf(nc, ctx, "ctxT", [P, KT, B * L])
    K.st = sbuf(nc, ctx, "bn_st", [P, NT, 6])
    K.nv = sbuf(nc, ctx, "norm_vec", [P, 10, NT])
    K.have_stats = False
    K.x_in = semaphores(nc, ctx, "x_in", "0 1")
    s_const, s_ctx, s_tr, s_dve = semaphores(nc, ctx, "load_", "const ctx tr dve")
    with nc.Block() as block:
        @block.sync
        def _(sp):
            sp.dma_start(K.ctx_nat[:, :, :], ins["ctx_1024"].rearrange("b k d -> k b d")).then_inc(s_ctx, 16)
            sp.dma_start(K.gate[:, :, :], ins["gates"].partition_broadcast(P)).then_inc(s_ctx, 16)
            for b in range(B):
                sp.dma_start(K.x[:, b * TB:(b + 1) * TB, :],
                             ins["x"][b].rearrange("(t p) d -> p t d", p=P)).then_inc(K.x_in[b], 16)

        @block.gpsimd
        def _(pool):
            pool.memset(K.ident[:, :], 0.0).then_inc(s_const, 1)
            pool.memset(K.shift[:, :], 0.0).then_inc(s_const, 1)
            pool.memset(K.headmask[:, :], HD ** -0.5).then_inc(s_const, 1)
            pool.memset(K.ones[:, :], 1.0).then_inc(s_const, 1)
            pool.memset(K.npow[:, :], -0.5).then_inc(s_const, 1)
            pool.memset(K.hpow[:, :], 0.5).then_inc(s_const, 1)
            pool.memset(K.zeros[:, :], 0.0).then_inc(s_const, 1)
            pool.wait_ge(s_const, 7)
            pool.affine_select(out=K.ident[:, :], in_=K.ident[:, :], compare_op=ALU.not_equal, fill=1.0, base=0,
                               pattern=[[-1, P]], channel_multiplier=1).then_inc(s_const, 1)
            pool.affine_select(out=K.shift[:, :], in_=K.shift[:, :], compare_op=ALU.not_equal, fill=1.0, base=P,
                               pattern=[[-1, 336]], channel_multiplier=1).then_inc(s_const, 1)
            pool.affine_select(out=K.headmask[:, :], in_=K.headmask[:, :], compare_op=ALU.is_ge, fill=0.0, base=0,
                               pattern=[[-HD, 8]], channel_multiplier=1).then_inc(s_const, 1)
            pool.wait_ge(s_const, 10)
            pool.affine_select(out=K.headmask[:, :], in_=K.headmask[:, :], compare_op=ALU.is_ge, fill=0.0,
                               base=HD - 1, pattern=[[HD, 8]], channel_multiplier=-1).then_inc(s_const, 1)

        @block.tensor
        def _(pe):
            pe.wait_ge(s_const, 8)
            pe.wait_ge(s_ctx, 32)
            for b in range(B):
                for k in range(KT):
                    m = pe.transpose(K.ps[:, 0, (k * B + b) * L:(k * B + b + 1) * L],
                                     K.ctx_nat[:, b, k * P:(k + 1) * P], K.ident[0:L, 0:L])
            m.then_inc(s_tr, 1)

        @block.scalar
        def _(act):
            act.wait_ge(s_ctx, 32)
            act.activation(K.gate[:, :, :], K.gate[:, :, :], ACT.Tanh).then_inc(s_dve, 1)

        @block.vector
        def _(dve):
            dve.wait_ge(s_const, 8)
            dve.tensor_copy(K.identb[:, :], K.ident[:, :]).then_inc(s_dve, 1)
            dve.wait_ge(s_tr, 1)
            dve.tensor_copy(K.ctxT[:, :, :].rearrange("p k c -> p (k c)"), K.ps[:, 0, 0:KT * B * L]).then_inc(s_dve, 1)


class Weights:

    def __init__(self, nc, ctx, ins):
        self.nc, self.ctx, self.ins, self.loads = nc, ctx, ins, []

    def add(self, name, shape, src):
        t = sbuf(self.nc, self.ctx, "w_" + name, shape)
        self.loads.append((t[tuple([slice(None)] * len(shape))], src))
        return t

    def rows(self, name):
        src = self.ins[name].rearrange("(k p) o -> p k o", p=P)
        return self.add(name, list(src.shape), src)

    def experts(self, name):
        src = self.ins[name].rearrange("e (k p) o -> p e k o", p=P)
        t = sbuf(self.nc, self.ctx, "w_" + name, list(src.shape))
        for e in range(src.shape[1]):
            self.loads.append((t[:, e, :, :], src[:, e, :, :]))
        return t

    def same(self, name):
        return self.add(name, list(self.ins[name].shape), self.ins[name])

    def repeated(self, name, n=P):
        return self.add(name, [n, self.ins[name].shape[0]], self.ins[name].partition_broadcast(n))


class Norm:

    def __init__(self, nc, ctx, K, tag, loads, ternary=False, to_dram=None, prefetch=(), banks=range(8),
                 loaded=None):
        self.K, self.loads, self.ternary, self.to_dram, self.prefetch = K, loads, ternary, to_dram, prefetch
        self.banks = banks
        self.have_stats, K.have_stats = K.have_stats, True
        self.s_stat, self.s_vec, self.s_pow, self.rows, self.s_tr, self.turned, self.s_out, self.loaded = semaphores(
            nc, ctx, tag, "stat vec pow rows tr turned out weights")
        self.all_loaded = 16 * len(loads)
        if loaded is not None:
            self.loaded, self.all_loaded = loaded

    def bank(self, u):
        return self.banks[u % len(self.banks)]

    def vector(self, dve):
        K, nv, st, s_vec = self.K, self.K.nv, self.K.st, self.s_vec
        if not self.have_stats:
            for b in range(B):
                dve.wait_ge(K.x_in[b], 16)
                with dve.Fori(b * TB, (b + 1) * TB) as t:
                    dve.bn_stats(st[:, t, :], K.x[:, t, :]).then_inc(self.s_stat, 1)
            dve.wait_ge(self.s_stat, NT)
        v = Steps(s_vec)
        v.did(dve.tensor_tensor(nv[:, 0, :], st[:, :, 1], st[:, :, 4], ALU.add))
        v.did(dve.tensor_tensor(nv[:, 1, :], st[:, :, 1], st[:, :, 4], ALU.subtract))
        v.did(dve.tensor_tensor(nv[:, 2, :], st[:, :, 2], st[:, :, 5], ALU.add))
        dve.wait_ge(s_vec, v.last())
        v.did(dve.tensor_scalar(nv[:, 3, :], nv[:, 0, :], 0.5, None, ALU.mult))
        v.did(dve.tensor_tensor(nv[:, 4, :], nv[:, 1, :], nv[:, 1, :], ALU.mult))
        dve.wait_ge(s_vec, v.last())
        v.did(dve.scalar_tensor_tensor(nv[:, 5, :], nv[:, 4, :], D / 4.0, nv[:, 2, :], ALU.mult, ALU.add))
        dve.wait_ge(s_vec, v.last())
        v.did(dve.tensor_scalar(nv[:, 6, :], nv[:, 5, :], 1.0 / D, LN_EPS, ALU.mult, ALU.add))
        dve.wait_ge(self.s_pow, 1)
        scale = nv[:, 7, :]
        if self.ternary:
            v.did(dve.tensor_scalar(nv[:, 8, :], nv[:, 5, :], 1.0 / D, None, ALU.mult))
            v.did(dve.tensor_tensor(nv[:, 0, :], nv[:, 7, :], nv[:, 7, :], ALU.mult))
            dve.wait_ge(s_vec, v.last())
            v.did(dve.tensor_tensor(nv[:, 8, :], nv[:, 8, :], nv[:, 0, :], ALU.mult))
            dve.wait_ge(self.s_pow, 2)
            v.did(dve.tensor_scalar(nv[:, 0, :], nv[:, 9, :], 1e-8, None, ALU.add))
            dve.wait_ge(s_vec, v.last())
            v.did(dve.reciprocal(nv[:, 1, :], nv[:, 0, :]))
            dve.wait_ge(s_vec, v.last())
            v.did(dve.tensor_tensor(nv[:, 8, :], nv[:, 1, :], nv[:, 7, :], ALU.mult))
            dve.wait_ge(s_vec, v.last())
            scale = nv[:, 8, :]
        with dve.Fori(0, NT) as t:
            dve.tensor_scalar(K.xn[:, t, :], K.x[:, t, :], nv[:, 3, bass.ds(t, 1)], scale[:, bass.ds(t, 1)],
                              ALU.subtract, ALU.mult).then_inc(self.rows, 1)

    def gpsimd(self, pool):
        nv = self.K.nv
        pool.wait_ge(self.s_vec, 7)
        pool.tensor_tensor(nv[:, 7, :], nv[:, 6, :], self.K.npow[:, :], ALU.pow).then_inc(self.s_pow, 1)
        if self.ternary:
            pool.wait_ge(self.s_vec, 10)
            pool.tensor_tensor(nv[:, 9, :], nv[:, 8, :], self.K.hpow[:, :], ALU.pow).then_inc(self.s_pow, 1)

    def sync(self, sp):
        for dst, src in self.loads:
            sp.dma_start(dst, src).then_inc(self.loaded, 16)
        for dst, src, sem in self.prefetch:
            sp.dma_start(dst, src).then_inc(sem, 16)
        if self.to_dram is not None:
            for q in range(4):
                sp.wait_ge(self.rows, 4 * (q + 1))
                sp.dma_start(self.to_dram[q * 512:(q + 1) * 512, :].rearrange("(t p) d -> p t d", p=P),
                             self.K.xn[:, 4 * q:4 * q + 4, :]).then_inc(self.s_out, 16)
            sp.wait_ge(self.s_out, 64)
        if self.loads:
            sp.wait_ge(self.loaded, self.all_loaded)

    def tensor(self, pe):
        K = self.K
        for t in range(NT):
            u = t // 2
            pe.wait_ge(self.rows, t + 1)
            if t % 2 == 0 and u >= len(self.banks):
                pe.wait_ge(self.turned, u - len(self.banks) + 1)
            for k in range(KT):
                m = pe.transpose(K.ps[:, self.bank(u), (2 * k + t % 2) * P:(2 * k + t % 2 + 1) * P],
                                 K.xn[:, t, k * P:(k + 1) * P], K.ident[:, :])
            if t % 2:
                m.then_inc(self.s_tr, 1)

    def scalar(self, act):
        K = self.K
        for u in range(NT // 2):
            act.wait_ge(self.s_tr, u + 1)
            act.activation(K.xnT[:, :, 2 * u * P:(2 * u + 2) * P],
                           K.ps[:, self.bank(u), :].rearrange("p (k c) -> p k c", k=KT), ACT.Copy).then_inc(self.turned, 1)


def multihead(nc, ctx, K, tag, norm, layer, wq, wk, wv, wo, bq=None, bk=None, bv=None, bo=None, mask=None):
    NC = -(-H * L // P)
    HV = HD + 1
    heads = [sorted({r // L for r in range(c * P, min((c + 1) * P, H * L))}) for c in range(NC)]
    rows = [min(P, H * L - c * P) for c in range(NC)]
    G4 = 4 * L
    rounds = [(0, 4), (4, 8), (8, NC)]
    ps = K.ps
    with ExitStack() as c:
        kT = sbuf(nc, c, tag + "kT", [P, KT, B * L])
        kblk = sbuf(nc, c, tag + "kblk", [P, B, KT, 8 * L])
        vaug = sbuf(nc, c, tag + "vaug", [L, B, H, HV])
        vblk = sbuf(nc, c, tag + "vblk", [P, B, NC * 3 * HV])
        qT = sbuf(nc, c, tag + "qT", [P, KT, S])
        sm = sbuf(nc, c, tag + "sm", [P, 2, H * L])
        pr = sbuf(nc, c, tag + "pr", [P, 2, H * L])
        pT = sbuf(nc, c, tag + "pT", [P, 2, NC, P])
        mx = sbuf(nc, c, tag + "mx", [P, 2, H])
        rden = sbuf(nc, c, tag + "rden", [P, 2, H])
        on = sbuf(nc, c, tag + "on", [P, 2, D])
        oT = sbuf(nc, c, tag + "oT", [P, D])
        gbo = sbuf(nc, c, tag + "gbo", [P, D])
        if mask is not None:
            mi = sbuf(nc, c, tag + "mi", [P, TB, L], I32)
            mf = sbuf(nc, c, tag + "mf", [P, TB, L])
        (s_mask, s_kv, s_kt, s_ones, s_set, s_bias, s_vb, s_vc, q_ps, q_sb, s_ready, s_used, sh_step, mx_ready, p_in, p_ready, pt_ps, pt_sb,
         o_ready, n_step, o_used, on_ready, oT_ps, oT_sb, y_ready, x_done) = semaphores(
            nc, ctx, tag, "mask kv kt ones set bias vb vc q_ps q_sb s_ready s_used sh_step mx_ready p_in p_ready pt_ps pt_sb "
            "o_ready n_step o_used on_ready oT_ps oT_sb y_ready x_done")
        gate = K.gate[:, 0, layer:layer + 1]
        SET = B * KT + B
        with nc.Block() as block:
            @block.sync
            def _(sp):
                norm.sync(sp)
                if mask is not None:
                    sp.dma_start(mi[:, :, :], mask.rearrange("(t p) k -> p t k", p=P)).then_inc(s_mask, 16)

            @block.tensor
            def _(pe):
                pe.wait_ge(norm.loaded, norm.all_loaded)
                for ct in range(KT):
                    for k in range(KT):
                        pe.matmul(ps[:, 4, ct * 256:ct * 256 + B * L], wk[:, k, ct * P:(ct + 1) * P],
                                  K.ctxT[:, k, :], start=(k == 0), stop=(k == KT - 1))
                for b in range(B):
                    for k in range(KT):
                        m = pe.matmul(ps[0:L, 5, b * D:(b + 1) * D], K.ctxT[:, k, b * L:(b + 1) * L],
                                      wv[:, k, :], start=(k == 0), stop=(k == KT - 1 and bv is None))
                    if bv is not None:
                        m = pe.matmul(ps[0:L, 5, b * D:(b + 1) * D], K.ones[0:1, 0:L], bv[0:1, :], start=False, stop=True)
                m.then_inc(s_kv, 1)
                pe.wait_ge(s_vb, B)
                for b in range(B):
                    for part in range(NC):
                        for j, h in enumerate(heads[part]):
                            down = h * L - part * P
                            m = pe.matmul(ps[:, 6 + b, (3 * part + j) * HV:(3 * part + j + 1) * HV],
                                          K.shift[0:L, P - down:2 * P - down], vaug[:, b, h, :],
                                          start=True, stop=True)
                m.then_inc(s_vc, 1)
                norm.tensor(pe)

                def scores(b, i):
                    pe.wait_ge(s_used, b * TB + i + 1)
                    for g in range(4):
                        m = pe.matmul(ps[:, g, 0:G4], qT[:, g // 2, i * P:(i + 1) * P],
                                      kblk[:, b, g // 2, (g % 2) * G4:(g % 2 + 1) * G4], start=True, stop=True)
                    m.then_inc(s_ready, 1)

                def turn(b, i, which):
                    pe.wait_ge(p_ready, b * TB + i + 1)
                    for r in which:
                        lo, hi = rounds[r]
                        if r != 1:
                            pe.wait_ge(pt_sb, b * 3 * TB + 3 * i + (r == 2) + 1)
                        for part in range(lo, hi):
                            n = rows[part]
                            m = pe.transpose(ps[0:n, 4 + r % 2, (part - lo) * P:(part - lo + 1) * P],
                                             pr[:, i % 2, part * P:part * P + n], K.ident[:, :])
                        m.then_inc(pt_ps, 1)

                def values(b, i):
                    pe.wait_ge(o_used, b * TB + i + 1)
                    for r, (lo, hi) in enumerate(rounds):
                        pe.wait_ge(pt_sb, b * 3 * TB + 3 * i + r + 2)
                        for part in range(lo, hi):
                            n, hs = rows[part], heads[part]
                            m = pe.matmul(ps[:, 6, hs[0] * HV:(hs[-1] + 1) * HV], pT[0:n, i % 2, part, :],
                                          vblk[0:n, b, 3 * part * HV:(3 * part + len(hs)) * HV],
                                          start=(part == 0), stop=(part == NC - 1), skip_group_check=True)
                    m.then_inc(o_ready, 1)

                def turn_heads(b, i):
                    pe.wait_ge(on_ready, b * TB + i + 1)
                    pe.wait_ge(x_done, b * TB + i + 1)
                    for k in range(KT):
                        m = pe.transpose(ps[:, 7, k * P:(k + 1) * P], on[:, i % 2, k * P:(k + 1) * P], K.ident[:, :])
                    m.then_inc(oT_ps, 1)

                def project(b, i):
                    pe.wait_ge(oT_sb, b * TB + i + 1)
                    for k in range(KT):
                        m = pe.matmul(ps[:, 7, D:2 * D], oT[:, k * P:(k + 1) * P], wo[:, k, :],
                                      start=(k == 0), stop=(k == KT - 1))
                    m.then_inc(y_ready, 1)

                pe.wait_ge(norm.turned, NT // 2)
                with pe.Fori(0, B) as b:
                    pe.wait_ge(x_done, b * TB + 1)
                    for n in range(4):
                        for k in range(KT):
                            m = pe.matmul(ps[:, n, :], wq[:, k, (n // 2) * P:(n // 2 + 1) * P],
                                          K.xnT[:, k, bass.ds(b * S + (n % 2) * 512, 512)],
                                          start=(k == 0), stop=(k == KT - 1))
                        m.then_inc(q_ps, 1)
                    pe.wait_ge(q_sb, b * 4 + 4)
                    pe.wait_ge(s_set, SET)
                    pe.wait_ge(s_used, b * TB + 1)
                    scores(b, 0)
                    scores(b, 1)
                    for i in range(TB):
                        if i + 2 < TB:
                            scores(b, i + 2)
                        turn(b, i, (0, 1))
                        if i:
                            turn_heads(b, i - 1)
                        turn(b, i, (2,))
                        values(b, i)
                        if i:
                            project(b, i - 1)
                    turn_heads(b, TB - 1)
                    project(b, TB - 1)

            @block.scalar
            def _(act):
                act.wait_ge(norm.loaded, norm.all_loaded)
                act.wait_ge(s_kv, 1)
                for ct in range(KT):
                    if bk is None:
                        act.activation(kT[:, ct, :], ps[:, 4, ct * 256:ct * 256 + B * L], ACT.Copy).then_inc(s_kt, 1)
                    else:
                        act.activation(kT[:, ct, :], ps[:, 4, ct * 256:ct * 256 + B * L], ACT.Identity,
                                       bias=bk[:, ct:ct + 1]).then_inc(s_kt, 1)
                act.wait_ge(s_ones, 1)
                for b in range(B):
                    act.activation(vaug[:, b, :, 0:HD], ps[0:L, 5, b * D:(b + 1) * D].rearrange("p (h c) -> p h c", h=H),
                                   ACT.Copy).then_inc(s_vb, 1)
                norm.scalar(act)

                def exps(b, i):
                    act.wait_ge(p_in, b * TB + i + 1)
                    if i >= 2:
                        act.wait_ge(pt_ps, b * 3 * TB + 3 * (i - 1))
                    act.activation(pr[:, i % 2, :], sm[:, i % 2, :], ACT.Exp).then_inc(p_ready, 1)

                with act.Fori(0, B) as b:
                    act.wait_ge(x_done, b * TB + 1)
                    for n in range(4):
                        act.wait_ge(q_ps, b * 4 + n + 1)
                        dst = qT[:, n // 2, (n % 2) * 512:(n % 2 + 1) * 512]
                        if bq is None:
                            act.activation(dst, ps[:, n, :], ACT.Copy).then_inc(q_sb, 1)
                        else:
                            act.activation(dst, ps[:, n, :], ACT.Identity,
                                           bias=bq[:, n // 2:n // 2 + 1]).then_inc(q_sb, 1)
                    exps(b, 0)
                    for i in range(TB):
                        if i + 1 < TB:
                            exps(b, i + 1)
                        for r, (lo, hi) in enumerate(rounds):
                            if i and r == 2:
                                act.wait_ge(oT_ps, b * TB + i)
                                act.activation(oT[:, :], ps[:, 7, 0:D], ACT.Copy).then_inc(oT_sb, 1)
                            act.wait_ge(pt_ps, b * 3 * TB + 3 * i + r + 1)
                            if i >= 2 and r == 0:
                                act.wait_ge(o_ready, b * TB + i - 1)
                            if r < 2:
                                act.activation(pT[:, i % 2, lo:hi, :].rearrange("p a b -> p (a b)"),
                                               ps[:, 4 + r, :], ACT.Copy).then_inc(pt_sb, 1)
                            else:
                                act.activation(pT[:, i % 2, lo, :], ps[:, 4, 0:P], ACT.Copy)
                                act.activation(pT[0:rows[-1], i % 2, lo + 1, :], ps[0:rows[-1], 4, P:2 * P],
                                               ACT.Copy).then_inc(pt_sb, 1)
                    act.wait_ge(oT_ps, b * TB + TB)
                    act.activation(oT[:, :], ps[:, 7, 0:D], ACT.Copy).then_inc(oT_sb, 1)

            @block.gpsimd
            def _(pool):
                pool.memset(vaug[:, :, :, :], 1.0).then_inc(s_ones, 1)
                norm.gpsimd(pool)
                pool.wait_ge(norm.loaded, norm.all_loaded)
                pool.wait_ge(norm.rows, NT)
                if bo is not None:
                    pool.tensor_tensor(gbo[:, :], bo[:, :], gate.broadcast_to([P, D]), ALU.mult).then_inc(s_bias, 1)
                    pool.wait_ge(s_bias, 1)
                    pool.tensor_tensor(K.x[:, :, :], K.x[:, :, :],
                                       gbo[:, :].unsqueeze(1).broadcast_to([P, NT, D]), ALU.add).then_inc(s_bias, 1)

            @block.vector
            def _(dve):
                norm.vector(dve)
                dve.wait_ge(norm.rows, NT)
                dve.wait_ge(norm.loaded, norm.all_loaded)
                s = Steps(s_set)
                dve.wait_ge(s_kt, KT)
                dve.sem_inc(x_done, 1)
                for b in range(B):
                    for ct in range(KT):
                        s.did(dve.tensor_tensor(
                            kblk[:, b, ct, :].rearrange("p (h k) -> p h k", h=8),
                            kT[:, ct, b * L:(b + 1) * L].unsqueeze(1).broadcast_to([P, 8, L]),
                            K.headmask[:, :].unsqueeze(2).broadcast_to([P, 8, L]), ALU.mult))
                if mask is not None:
                    dve.wait_ge(s_mask, 16)
                    dve.tensor_scalar(mf[:, :, :], mi[:, :, :], 0, -3e38, ALU.is_equal, ALU.mult).then_inc(n_step, 1)
                    dve.wait_ge(n_step, 1)
                dve.wait_ge(s_vc, 1)
                W = NC * 3 * HV
                used = [3 * part * HV + n for part in range(NC) for n in range(len(heads[part]) * HV)]
                full = used == list(range(len(used)))
                for b in range(B):
                    if full:
                        s.did(dve.tensor_copy(vblk[:, b, 0:len(used)], ps[:, 6 + b, 0:len(used)]))
                    else:
                        for part in range(NC):
                            lo, n = 3 * part * HV, len(heads[part]) * HV
                            m = dve.tensor_copy(vblk[:, b, lo:lo + n], ps[:, 6 + b, lo:lo + n])
                            if part == NC - 1:
                                s.did(m)
                dve.wait_ge(s_set, s.last())
                assert s.last() == SET

                if bo is not None:
                    dve.wait_ge(s_bias, 2)
                for free in (s_used, pt_sb, o_used):
                    dve.sem_inc(free, 1)

                def front(b, i):
                    dve.wait_ge(s_ready, b * TB + i + 1)
                    if i >= 2:
                        dve.wait_ge(p_ready, b * TB + i - 1)
                    sc = ps[:, 0:4, 0:G4].rearrange("p g (h k) -> p g h k", h=4)
                    smt = sm[:, i % 2, :].rearrange("p (g h k) -> p g h k", g=4, h=4)
                    sm2 = sm[:, i % 2, :].rearrange("p (h k) -> p h k", h=H)
                    mxt = mx[:, i % 2, :]
                    if mask is not None:
                        dve.tensor_tensor(sm[:, i % 2, :].rearrange("p (g c) -> p g c", g=4).rearrange("p g (h k) -> p g h k", h=4),
                                          sc, mf[:, i, :].unsqueeze(1).unsqueeze(1).broadcast_to([P, 4, 4, L]),
                                          ALU.add).then_inc(s_used, 1)
                        dve.wait_ge(s_used, b * TB + i + 2)
                        dve.tensor_reduce(mxt, sm2, AX.X, ALU.max).then_inc(sh_step, 1)
                        dve.wait_ge(sh_step, b * TB + i + 1)
                        dve.tensor_tensor(sm2, sm2, mxt.unsqueeze(2).broadcast_to([P, H, L]),
                                          ALU.subtract).then_inc(p_in, 1)
                    else:
                        dve.tensor_reduce(mxt.rearrange("p (g h) -> p g h", g=4), sc, AX.X, ALU.max).then_inc(sh_step, 1)
                        dve.wait_ge(sh_step, b * TB + i + 1)
                        m = dve.tensor_tensor(smt, sc, mxt.rearrange("p (g h) -> p g h", g=4).unsqueeze(3)
                                              .broadcast_to([P, 4, 4, L]), ALU.subtract)
                        m.then_inc(p_in, 1)
                        dve.wait_ge(p_in, b * TB + i + 1)
                        dve.sem_inc(s_used, 1)

                def normalise(b, i):
                    o = ps[:, 6, 0:H * HV].rearrange("p (h c) -> p h c", h=H)
                    dve.wait_ge(o_ready, b * TB + i + 1)
                    dve.reciprocal(rden[:, i % 2, :], o[:, :, HD]).then_inc(mx_ready, 1)
                    dve.wait_ge(mx_ready, b * TB + i + 1)
                    if i >= 2:
                        dve.wait_ge(oT_ps, b * TB + i - 1)
                    dve.tensor_tensor(on[:, i % 2, :].rearrange("p (h c) -> p h c", h=H), o[:, :, 0:HD],
                                      rden[:, i % 2, :].unsqueeze(2).broadcast_to([P, H, HD]),
                                      ALU.mult).then_inc(on_ready, 1)
                    dve.wait_ge(on_ready, b * TB + i + 1)
                    dve.sem_inc(o_used, 1)

                def residual(b, i):
                    dve.wait_ge(y_ready, b * TB + i + 1)
                    xt = K.x[:, b * TB + i, :]
                    dve.scalar_tensor_tensor(xt, ps[:, 7, D:2 * D], gate, xt, ALU.mult, ALU.add).then_inc(x_done, 1)
                    dve.wait_ge(x_done, b * TB + i + 2)
                    dve.bn_stats(K.st[:, b * TB + i, :], xt)

                with dve.Fori(0, B) as b:
                    dve.wait_ge(x_done, b * TB + 1)
                    front(b, 0)
                    front(b, 1)
                    for i in range(TB):
                        if i + 2 < TB:
                            front(b, i + 2)
                        normalise(b, i)
                        if i:
                            residual(b, i - 1)
                    residual(b, TB - 1)


def sigmoid_attention(nc, ctx, K, tag, norm, layer, wqn, wk, wv, bq, bk, bv):
    QK = 64
    ps = K.ps
    with ExitStack() as c:
        kp = sbuf(nc, c, tag + "kp", [QK, B * L])
        v = sbuf(nc, c, tag + "v", [L, B, D])
        a = sbuf(nc, c, tag + "a", [P, KT, B * L])
        cb = sbuf(nc, c, tag + "cb", [L, B])
        zT = sbuf(nc, c, tag + "zT", [L, 2, 512])
        s_kv, s_kvb, s_a, s_ab, s_ps, s_z, s_y, s_x = semaphores(nc, c, tag, "kv kvb a ab s_ps z y x")
        gate = K.gate[:, 0, layer:layer + 1]
        groups = B * S // 512
        with nc.Block() as block:
            @block.sync
            def _(sp):
                norm.sync(sp)

            @block.gpsimd
            def _(pool):
                norm.gpsimd(pool)

            @block.tensor
            def _(pe):
                pe.wait_ge(norm.loaded, norm.all_loaded)
                for k in range(KT):
                    pe.matmul(ps[0:QK, 0, 0:B * L], wk[:, k, :], K.ctxT[:, k, :], start=(k == 0), stop=(k == KT - 1))
                for b in range(B):
                    for k in range(KT):
                        m = pe.matmul(ps[0:L, 1, b * D:(b + 1) * D], K.ctxT[:, k, b * L:(b + 1) * L],
                                      wv[:, k, :], start=(k == 0), stop=False)
                    m = pe.matmul(ps[0:L, 1, b * D:(b + 1) * D], K.ones[0:1, 0:L], bv[0:1, :], start=False, stop=True)
                m.then_inc(s_kv, 1)
                pe.wait_ge(s_kvb, 2)
                for k in range(KT):
                    pe.matmul(ps[:, 2, k * 256:k * 256 + B * L], wqn[:, k * P:(k + 1) * P], kp[:, :],
                              start=True, stop=True)
                for b in range(B):
                    m = pe.matmul(ps[0:L, 3, b:b + 1], kp[:, b * L:(b + 1) * L], bq[:, 0:1], start=True, stop=True)
                m.then_inc(s_a, 1)
                norm.tensor(pe)
                pe.wait_ge(s_ab, 2)
                pe.wait_ge(norm.turned, NT // 2)

                def scores(g):
                    b = g * 512 // S
                    if g >= 2:
                        pe.wait_ge(s_z, g - 1)
                    for k in range(KT):
                        m = pe.matmul(ps[0:L, 4 + g % 2, :], a[:, k, b * L:(b + 1) * L],
                                      K.xnT[:, k, g * 512:(g + 1) * 512], start=(k == 0), stop=(k == KT - 1))
                    m.then_inc(s_ps, 1)

                scores(0)
                for g in range(groups):
                    b = g * 512 // S
                    if g + 1 < groups:
                        scores(g + 1)
                    pe.wait_ge(s_z, g + 1)
                    for u in range(2):
                        n = 2 * g + u
                        if n >= 2:
                            pe.wait_ge(s_x, n - 1)
                        for j in range(2):
                            m = pe.matmul(ps[:, 6 + n % 2, j * D:(j + 1) * D],
                                          zT[:, g % 2, (2 * u + j) * P:(2 * u + j + 1) * P], v[:, b, :],
                                          start=True, stop=True)
                        m.then_inc(s_y, 1)

            @block.scalar
            def _(act):
                act.wait_ge(norm.loaded, norm.all_loaded)
                act.wait_ge(s_kv, 1)
                act.activation(kp[:, :], ps[0:QK, 0, 0:B * L], ACT.Identity, bias=bk[:, 0:1]).then_inc(s_kvb, 1)
                act.activation(v[:, :, :].rearrange("p b d -> p (b d)"), ps[0:L, 1, :], ACT.Copy).then_inc(s_kvb, 1)
                act.wait_ge(s_a, 1)
                act.activation(cb[:, :], ps[0:L, 3, 0:B], ACT.Copy, scale=QK ** -0.5).then_inc(s_ab, 1)
                act.activation(a[:, :, :], ps[:, 2, :].rearrange("p (k c) -> p k c", k=KT)[:, :, 0:B * L],
                               ACT.Copy).then_inc(s_ab, 1)
                norm.scalar(act)
                act.wait_ge(s_ab, 2)
                for g in range(groups):
                    b = g * 512 // S
                    act.wait_ge(s_ps, g + 1)
                    if g >= 2:
                        act.wait_ge(s_y, 2 * (g - 1))
                    act.activation(zT[:, g % 2, :], ps[0:L, 4 + g % 2, :], ACT.Sigmoid, bias=cb[:, b:b + 1],
                                   scale=QK ** -0.5).then_inc(s_z, 1)

            @block.vector
            def _(dve):
                norm.vector(dve)
                dve.wait_ge(norm.rows, NT)
                for n in range(2 * groups):
                    dve.wait_ge(s_y, n + 1)
                    xt = K.x[:, 2 * n:2 * n + 2, :].rearrange("p t d -> p (t d)")
                    dve.scalar_tensor_tensor(xt, ps[:, 6 + n % 2, :], gate, xt, ALU.mult, ALU.add).then_inc(s_x, 1)
                    dve.wait_ge(s_x, n + 1)
                    for t in (2 * n, 2 * n + 1):
                        dve.bn_stats(K.st[:, t, :], K.x[:, t, :])


def align_attention(nc, ctx, K, tag, norm, layer, wT, wn, bc):
    ps = K.ps
    with ExitStack() as c:
        eo = sbuf(nc, c, tag + "eo", [P, KT, B * L])
        a = sbuf(nc, c, tag + "a", [P, KT, B * L])
        cr = sbuf(nc, c, tag + "cr", [1, B * L])
        sm = sbuf(nc, c, tag + "sm", [P, 2, 4, L])
        pr = sbuf(nc, c, tag + "pr", [P, 2, 4, L])
        pT = sbuf(nc, c, tag + "pT", [L, 2, 512])
        vec = sbuf(nc, c, tag + "vec", [P, 2, 4, 4])
        s_e, s_eb, s_a, s_ab, s_ps, s_mx, s_sh, s_p, s_sum, s_c, s_tp, s_tb, s_y, s_x = semaphores(
            nc, c, tag, "e eb a ab s_ps mx sh p sum c tp tb y x")
        gate = K.gate[:, 0, layer:layer + 1]
        groups = B * S // 512
        with nc.Block() as block:
            @block.sync
            def _(sp):
                norm.sync(sp)

            @block.gpsimd
            def _(pool):
                norm.gpsimd(pool)

            @block.tensor
            def _(pe):
                pe.wait_ge(norm.loaded, norm.all_loaded)
                for e in range(KT):
                    for k in range(KT):
                        m = pe.matmul(ps[:, 0, e * 256:e * 256 + B * L], wT[:, k, e * P:(e + 1) * P], K.ctxT[:, k, :],
                                      start=(k == 0), stop=(k == KT - 1))
                m.then_inc(s_e, 1)
                pe.wait_ge(s_eb, 2)
                for d in range(KT):
                    for e in range(KT):
                        pe.matmul(ps[:, 1, d * 256:d * 256 + B * L], wn[:, e, d * P:(d + 1) * P], eo[:, e, :],
                                  start=(e == 0), stop=(e == KT - 1))
                for e in range(KT):
                    m = pe.matmul(ps[0:1, 2, 0:B * L], bc[:, e:e + 1], eo[:, e, :], start=(e == 0), stop=(e == KT - 1))
                m.then_inc(s_a, 1)
                norm.tensor(pe)
                pe.wait_ge(s_ab, 2)
                pe.wait_ge(norm.turned, NT // 2)

                def scores(g):
                    b = g * 512 // S
                    if g >= 2:
                        pe.wait_ge(s_sh, g - 1)
                    for i in range(4):
                        t = 4 * g + i
                        o = ps[:, g % 2, i * L:(i + 1) * L]
                        for k in range(KT):
                            pe.matmul(o, K.xnT[:, k, t * P:(t + 1) * P], a[:, k, b * L:(b + 1) * L],
                                      start=(k == 0), stop=False)
                        m = pe.matmul(o, K.ones[0:1, :], cr[:, b * L:(b + 1) * L], start=False, stop=True)
                    m.then_inc(s_ps, 1)

                scores(0)
                for g in range(groups):
                    b = g * 512 // S
                    if g + 1 < groups:
                        scores(g + 1)
                    pe.wait_ge(s_p, g + 1)
                    for i in range(4):
                        m = pe.transpose(ps[0:L, 2 + g % 2, i * P:(i + 1) * P], pr[:, g % 2, i, :], K.ident[:, :])
                    m.then_inc(s_tp, 1)
                    pe.wait_ge(s_tb, g + 1)
                    for u in range(2):
                        n = 2 * g + u
                        if n >= 4:
                            pe.wait_ge(s_x, n - 3)
                        for j in range(2):
                            m = pe.matmul(ps[:, 4 + n % 4, j * D:(j + 1) * D],
                                          pT[:, g % 2, (2 * u + j) * P:(2 * u + j + 1) * P], K.ctx_nat[:, b, :],
                                          start=True, stop=True)
                        m.then_inc(s_y, 1)

            @block.scalar
            def _(act):
                act.wait_ge(norm.loaded, norm.all_loaded)
                act.wait_ge(s_e, 1)
                for e in range(KT):
                    act.activation(eo[:, e, :], ps[:, 0, e * 256:e * 256 + B * L], ACT.Identity,
                                   bias=bc[:, e:e + 1]).then_inc(s_eb, 1)
                act.wait_ge(s_a, 1)
                act.activation(cr[:, :], ps[0:1, 2, 0:B * L], ACT.Copy).then_inc(s_ab, 1)
                act.activation(a[:, :, :], ps[:, 1, :].rearrange("p (k c) -> p k c", k=KT)[:, :, 0:B * L],
                               ACT.Copy).then_inc(s_ab, 1)
                norm.scalar(act)
                for g in range(groups):
                    act.wait_ge(s_sh, g + 1)
                    if g >= 2:
                        act.wait_ge(s_tp, g - 1)
                        act.wait_ge(s_sum, g - 1)
                    act.activation(pr[:, g % 2, :, :], sm[:, g % 2, :, :], ACT.Exp).then_inc(s_p, 1)
                    act.wait_ge(s_tp, g + 1)
                    if g >= 2:
                        act.wait_ge(s_y, 2 * (g - 1))
                    act.activation(pT[:, g % 2, :], ps[0:L, 2 + g % 2, :], ACT.Copy).then_inc(s_tb, 1)

            @block.vector
            def _(dve):
                norm.vector(dve)
                dve.wait_ge(norm.rows, NT)

                def front(g):
                    dve.wait_ge(s_ps, g + 1)
                    sc = ps[:, g % 2, 0:4 * L].rearrange("p (i k) -> p i k", i=4)
                    dve.tensor_reduce(vec[:, g % 2, 0, :], sc, AX.X, ALU.max).then_inc(s_mx, 1)
                    dve.wait_ge(s_mx, g + 1)
                    if g >= 2:
                        dve.wait_ge(s_p, g - 1)
                    dve.tensor_tensor(sm[:, g % 2, :, :], sc, vec[:, g % 2, 0, :].unsqueeze(2).broadcast_to([P, 4, L]),
                                      ALU.subtract).then_inc(s_sh, 1)

                front(0)
                st = Steps(s_c)
                for g in range(groups):
                    if g + 1 < groups:
                        front(g + 1)
                    dve.wait_ge(s_p, g + 1)
                    vg = vec[:, g % 2, :, :]
                    dve.tensor_reduce(vg[:, 1, :], pr[:, g % 2, :, :], AX.X, ALU.add).then_inc(s_sum, 1)
                    dve.wait_ge(s_sum, g + 1)
                    st.did(dve.reciprocal(vg[:, 2, :], vg[:, 1, :]))
                    dve.wait_ge(s_c, st.last())
                    st.did(dve.tensor_scalar(vg[:, 3, :], vg[:, 2, :], gate, None, ALU.mult))
                    dve.wait_ge(s_c, st.last())
                    for u in range(2):
                        dve.wait_ge(s_y, 2 * g + u + 1)
                        for j in range(2):
                            i = 2 * u + j
                            xt = K.x[:, 4 * g + i, :]
                            m = dve.scalar_tensor_tensor(xt, ps[:, 4 + (2 * g + u) % 4, j * D:(j + 1) * D],
                                                         vg[:, 3, i:i + 1], xt, ALU.mult, ALU.add)
                        m.then_inc(s_x, 1)
                        dve.wait_ge(s_x, 2 * g + u + 1)
                        for t in (4 * g + 2 * u, 4 * g + 2 * u + 1):
                            dve.bn_stats(K.st[:, t, :], K.x[:, t, :])


def sum_magnitudes(dve, s_part, weights, part, out, steps):
    for n, w in enumerate(weights):
        dve.tensor_reduce(part[:, n, :], w[:, :, :].rearrange("p k f -> p (k f)").rearrange("p (a c) -> p a c", c=64),
                          AX.X, ALU.add, apply_absolute_value=True).then_inc(s_part, 1)
    dve.wait_ge(s_part, 2)
    for n in range(2):
        steps.did(dve.tensor_reduce(out[:, n:n + 1], part[:, n, :], AX.X, ALU.add))


def bitnet_ffn(nc, ctx, K, tag, norm, layer, w1, w2, cw, cbias):
    F = 1024
    FT = F // P
    ps = K.ps
    psb = [ps[:, k, :].bitcast(BF16) for k in range(8)]
    with ExitStack() as c:
        q1 = sbuf(nc, c, tag + "q1", [P, KT, F], BF16)
        q2 = sbuf(nc, c, tag + "q2", [P, FT, D], BF16)
        wt = sbuf(nc, c, tag + "wt", [P, 2, 2048])
        xq = sbuf(nc, c, tag + "xq", [P, NT, D], BF16)
        xqT = sbuf(nc, c, tag + "xqT", [P, KT, B * S], BF16)
        dqb = sbuf(nc, c, tag + "dqb", [P, B * S])
        diag = sbuf(nc, c, tag + "diag", [P, 4, P])
        vec = sbuf(nc, c, tag + "vec", [P, 8, NT])
        wv = sbuf(nc, c, tag + "wv", [P, 4, 2])
        magic = sbuf(nc, c, tag + "magic", [P, 1])
        hb = sbuf(nc, c, tag + "hb", [P, 2, S + 2])
        yb = sbuf(nc, c, tag + "yb", [P, 2, S])
        act_s = sbuf(nc, c, tag + "act", [P, FT, S])
        scaled_xn = act_s[:, 0:NT * D // S, :].rearrange("p f s -> p (f s)").rearrange("p (t d) -> p t d", t=NT)
        tv = sbuf(nc, c, tag + "tv", [P, 6, TB])
        qf = sbuf(nc, c, tag + "qf", [P, 2, F])
        qb = sbuf(nc, c, tag + "qb", [P, 2, F], BF16)
        qT = sbuf(nc, c, tag + "qT", [P, 2, F], BF16)
        part = sbuf(nc, c, tag + "part", [P, 2, 32])
        s_part, s_xm, s_wm = semaphores(nc, c, tag, "part xm wm")
        (s_set, s_sum, s_xq, s_xt, s_xe, s_dg, s_db, s_de, h_ps, h_sb, y0, tap, y_sb, a_sb, t_ps, t_step, sc_ready,
         qf_sb, qb_sb, u_ps, u_sb, y_ps, x_done) = semaphores(
            nc, c, tag, "set sum xq xt xe dg db de h_ps h_sb y0 tap y_sb a_sb t_ps t_step sc qf qb u_ps u_sb y_ps xd")
        gate = K.gate[:, 1, layer:layer + 1]
        SCALED, SUMS, MEANS, UNITS = 4, 6, 8, 10
        TURNED = (4, 0)

        def turned(i):
            return ps[:, TURNED[i % 2]:TURNED[i % 2] + 2, :].rearrange("p a c -> p (a c)")

        with nc.Block() as block:
            @block.sync
            def _(sp):
                norm.sync(sp)

            @block.gpsimd
            def _(pool):
                pool.memset(hb[:, :, :], 0.0).then_inc(tap, 1)
                pool.memset(magic[:, :], MAGIC).then_inc(tap, 1)
                norm.gpsimd(pool)
                pool.wait_ge(s_set, UNITS)
                for t in range(NT):
                    if t >= 4:
                        pool.wait_ge(s_db, t - 3)
                    pool.tensor_scalar(diag[:, t % 4, :], K.ident[:, :], vec[:, 4, t:t + 1], None,
                                       ALU.mult).then_inc(s_dg, 1)

            @block.tensor
            def _(pe):
                pe.wait_ge(s_set, SUMS)
                pe.matmul(ps[:, 7, 0:2], K.ones[:, :], wv[:, 0, :], start=True, stop=True).then_inc(s_sum, 1)
                for q in range(4):
                    pe.wait_ge(s_xq, 1)
                    for k in range(KT):
                        for i in range(4):
                            t = 4 * q + i
                            m = pe.transpose(psb[q][:, (4 * k + i) * P:(4 * k + i + 1) * P],
                                             xq[:, t, k * P:(k + 1) * P], K.identb[:, :])
                    m.then_inc(s_xt, 1)
                for t in range(NT):
                    pe.wait_ge(s_dg, t + 1)
                    if t % 4 == 0:
                        pe.wait_ge(s_xe, 4)
                        if t >= 8:
                            pe.wait_ge(s_de, t // 4 - 1)
                    m = pe.matmul(ps[:, 4 + (t // 4) % 2, (t % 4) * P:(t % 4 + 1) * P], K.ones[:, :], diag[:, t % 4, :],
                                  start=True, stop=True)
                    m.then_inc(s_db, 1)
                pe.wait_ge(s_de, 4)
                with pe.Fori(0, B) as b:
                    pe.wait_ge(x_done, b * TB + 1)
                    for f in range(FT):
                        if f >= 2:
                            pe.wait_ge(h_sb, b * FT + f - 1)
                        for hf in range(2):
                            for k in range(KT):
                                m = pe.matmul(ps[:, 2 * (f % 2) + hf, :], q1[:, k, f * P:(f + 1) * P],
                                              xqT[:, k, bass.ds(b * S + hf * 512, 512)],
                                              start=(k == 0), stop=(k == KT - 1))
                        m.then_inc(h_ps, 1)
                    pe.wait_ge(a_sb, b * FT + FT)

                    def turn(i):
                        if i >= 2:
                            pe.wait_ge(qf_sb, b * TB + i - 1)
                        for f in range(FT):
                            m = pe.transpose(ps[:, TURNED[i % 2] + f // 4, (f % 4) * P:(f % 4 + 1) * P],
                                             act_s[:, f, i * P:(i + 1) * P], K.ident[:, :])
                        m.then_inc(t_ps, 1)

                    def turn_back(i):
                        pe.wait_ge(qb_sb, b * TB + i + 1)
                        if i:
                            pe.wait_ge(u_sb, b * TB + i)
                        for f in range(FT):
                            m = pe.transpose(psb[6][:, f * P:(f + 1) * P], qb[:, i % 2, f * P:(f + 1) * P],
                                             K.identb[:, :])
                        m.then_inc(u_ps, 1)

                    def down(i):
                        pe.wait_ge(u_sb, b * TB + i + 1)
                        if i:
                            pe.wait_ge(x_done, b * TB + i + 1)
                        for f in range(FT):
                            m = pe.matmul(ps[:, 7, 0:D], qT[:, i % 2, f * P:(f + 1) * P], q2[:, f, :],
                                          start=(f == 0), stop=(f == FT - 1))
                        m.then_inc(y_ps, 1)

                    turn(0)
                    turn(1)
                    turn_back(0)
                    for i in range(TB):
                        if i + 2 < TB:
                            turn(i + 2)
                        if i + 1 < TB:
                            turn_back(i + 1)
                        down(i)

            @block.scalar
            def _(act):
                act.wait_ge(tap, 2)
                act.wait_ge(s_set, SCALED)
                for t in range(NT):
                    act.activation(scaled_xn[:, t, :], K.xn[:, t, :], ACT.Identity, bias=magic[:, 0:1],
                                   scale=vec[:, 3, t:t + 1]).then_inc(s_xm, 1)
                act.wait_ge(s_set, MEANS)
                for n, w in enumerate((w1, w2)):
                    act.activation(wt[:, n, :], w[:, :, :].rearrange("p k f -> p (k f)"), ACT.Identity,
                                   bias=magic[:, 0:1], scale=wv[:, 2, n:n + 1]).then_inc(s_wm, 1)
                for q in range(4):
                    act.wait_ge(s_xt, q + 1)
                    act.activation(xqT[:, :, q * 512:(q + 1) * 512], psb[q].rearrange("p (k c) -> p k c", k=KT),
                                   ACT.Copy).then_inc(s_xe, 1)
                for q in range(4):
                    act.wait_ge(s_db, 4 * q + 4)
                    act.activation(dqb[:, q * 512:(q + 1) * 512], ps[:, 4 + q % 2, :], ACT.Copy).then_inc(s_de, 1)
                with act.Fori(0, B) as b:
                    def centre(f):
                        act.wait_ge(h_sb, b * FT + f + 1)
                        if f >= 2:
                            act.wait_ge(a_sb, b * FT + f - 1)
                        act.activation(yb[:, f % 2, :], hb[:, f % 2, 1:S + 1], ACT.Identity, bias=cbias[:, f:f + 1],
                                       scale=cw[:, f, 1:2]).then_inc(y0, 1)

                    centre(0)
                    for f in range(FT):
                        if f + 1 < FT:
                            centre(f + 1)
                        act.wait_ge(y_sb, b * FT + f + 1)
                        act.activation(act_s[:, f, :], yb[:, f % 2, :], ACT.Silu).then_inc(a_sb, 1)

                    def scaled(i):
                        act.wait_ge(sc_ready, b * TB + i + 1)
                        if i >= 2:
                            act.wait_ge(qb_sb, b * TB + i - 1)
                        act.activation(qf[:, i % 2, :], turned(i), ACT.Identity,
                                       bias=magic[:, 0:1], scale=tv[:, 3, i:i + 1]).then_inc(qf_sb, 1)

                    def copy_back(i):
                        act.wait_ge(u_ps, b * TB + i + 1)
                        if i >= 2:
                            act.wait_ge(y_ps, b * TB + i - 1)
                        act.activation(qT[:, i % 2, :], psb[6], ACT.Copy).then_inc(u_sb, 1)

                    scaled(0)
                    scaled(1)
                    copy_back(0)
                    for i in range(TB):
                        if i + 1 < TB:
                            copy_back(i + 1)
                        if i + 2 < TB:
                            scaled(i + 2)

            @block.vector
            def _(dve):
                s = Steps(s_set)

                def then(ins):
                    s.did(ins)
                    dve.wait_ge(s_set, s.last())

                norm.vector(dve)
                dve.wait_ge(norm.rows, NT)
                dve.wait_ge(tap, 2)
                then(dve.tensor_reduce(vec[:, 0, :], K.xn[:, :, :], AX.X, ALU.max, apply_absolute_value=True))
                then(dve.tensor_scalar(vec[:, 1, :], vec[:, 0, :], 1e-5, None, ALU.max))
                then(dve.reciprocal(vec[:, 2, :], vec[:, 1, :]))
                then(dve.tensor_scalar(vec[:, 3, :], vec[:, 2, :], 127.0, None, ALU.mult))
                assert s.last() == SCALED
                dve.wait_ge(norm.loaded, norm.all_loaded)
                sum_magnitudes(dve, s_part, (w1, w2), part, wv[:, 0, :], s)
                assert s.last() == SUMS
                dve.wait_ge(s_sum, 1)
                then(dve.tensor_scalar(wv[:, 1, :], ps[:, 7, 0:2], 1.0 / (F * D), 1e-5, ALU.mult, ALU.max))
                then(dve.reciprocal(wv[:, 2, :], wv[:, 1, :]))
                assert s.last() == MEANS
                then(dve.tensor_scalar(vec[:, 4, :], vec[:, 1, :], wv[:, 1, 0:1], 1.0 / 127, ALU.mult, ALU.mult))
                then(dve.tensor_scalar(wv[:, 3, 1:2], wv[:, 1, 1:2], gate, 1.0 / 127, ALU.mult, ALU.mult))
                assert s.last() == UNITS
                dve.wait_ge(s_xm, NT)
                dve.tensor_scalar(xq[:, :, :], scaled_xn, MAGIC, None, ALU.subtract).then_inc(s_xq, 1)
                for n, q in enumerate((q1, q2)):
                    dve.wait_ge(s_wm, n + 1)
                    then(dve.tensor_scalar(wt[:, n, :], wt[:, n, :], MAGIC, 1.0, ALU.subtract, ALU.min))
                    then(dve.tensor_scalar(q[:, :, :].rearrange("p k f -> p (k f)"), wt[:, n, :], -1.0, None, ALU.max))
                dve.wait_ge(s_de, 4)
                dve.sem_inc(x_done, 1)
                TS = 4
                with dve.Fori(0, B) as b:
                    def dequant(f):
                        dve.wait_ge(h_ps, b * FT + f + 1)
                        if f >= 2:
                            dve.wait_ge(y_sb, b * FT + f - 1)
                        dve.tensor_tensor(hb[:, f % 2, 1:S + 1], ps[:, 2 * (f % 2):2 * (f % 2) + 2, :].rearrange("p a c -> p (a c)"),
                                          dqb[:, bass.ds(b * S, S)], ALU.mult).then_inc(h_sb, 1)

                    dequant(0)
                    for f in range(FT):
                        if f + 1 < FT:
                            dequant(f + 1)
                        dve.wait_ge(y0, b * FT + f + 1)
                        y = yb[:, f % 2, :]
                        dve.scalar_tensor_tensor(y, hb[:, f % 2, 0:S], cw[:, f, 0:1], y, ALU.mult, ALU.add).then_inc(tap, 1)
                        dve.wait_ge(tap, b * FT + f + 3)
                        dve.scalar_tensor_tensor(y, hb[:, f % 2, 2:S + 2], cw[:, f, 2:3], y, ALU.mult,
                                                 ALU.add).then_inc(y_sb, 1)

                    def scale(i):
                        dve.wait_ge(t_ps, b * TB + i + 1)
                        t = Steps(t_step, b * TS * TB + TS * i)
                        t.did(dve.tensor_reduce(tv[:, 0, i:i + 1], turned(i), AX.X, ALU.max,
                                                apply_absolute_value=True))
                        dve.wait_ge(t_step, t.last())
                        t.did(dve.tensor_scalar(tv[:, 1, i:i + 1], tv[:, 0, i:i + 1], 1e-5, None, ALU.max))
                        dve.wait_ge(t_step, t.last())
                        t.did(dve.reciprocal(tv[:, 2, i:i + 1], tv[:, 1, i:i + 1]))
                        t.did(dve.tensor_scalar(tv[:, 4, i:i + 1], tv[:, 1, i:i + 1], wv[:, 3, 1:2], None, ALU.mult))
                        dve.wait_ge(t_step, t.last())
                        dve.tensor_scalar(tv[:, 3, i:i + 1], tv[:, 2, i:i + 1], 127.0, None, ALU.mult).then_inc(sc_ready, 1)

                    def residual(i):
                        dve.wait_ge(y_ps, b * TB + i + 1)
                        xt = K.x[:, b * TB + i, :]
                        dve.scalar_tensor_tensor(xt, ps[:, 7, 0:D], tv[:, 4, i:i + 1], xt, ALU.mult,
                                                 ALU.add).then_inc(x_done, 1)
                        dve.wait_ge(x_done, b * TB + i + 2)
                        dve.bn_stats(K.st[:, b * TB + i, :], xt)

                    def whole(i):
                        dve.wait_ge(qf_sb, b * TB + i + 1)
                        if i >= 2:
                            dve.wait_ge(u_ps, b * TB + i - 1)
                        dve.tensor_scalar(qb[:, i % 2, :], qf[:, i % 2, :], MAGIC, None, ALU.subtract).then_inc(qb_sb, 1)

                    scale(0)
                    scale(1)
                    whole(0)
                    for i in range(TB):
                        if i + 1 < TB:
                            whole(i + 1)
                        if i + 2 < TB:
                            scale(i + 2)
                        residual(i)


def ternary_ffn(nc, ctx, K, tag, norm, layer, wu, wd):
    F = 1024
    FT = F // P
    W = 512
    NH = S // W
    ps = K.ps
    with ExitStack() as c:
        tu = sbuf(nc, c, tag + "tu", [P, KT, F], F32R)
        td = sbuf(nc, c, tag + "td", [P, FT, D], F32R)
        wneg = sbuf(nc, c, tag + "wneg", [P, 2048])
        wv = sbuf(nc, c, tag + "wv", [P, 4, 2])
        xh = sbuf(nc, c, tag + "xh", [P, 2, KT, W], F32R)
        xl = sbuf(nc, c, tag + "xl", [P, 2, KT, W], F32R)
        h = sbuf(nc, c, tag + "h", [P, 4, W])
        hh = [sbuf(nc, c, tag + "hh", [P, FT, W], F32R),
              K.xn[:, :, :].bitcast(F32R).rearrange("p t d -> p (t d)").rearrange("p (f w) -> p f w", f=FT)]
        hl = [sbuf(nc, c, tag + f"hl{i}", [P, FT, W], F32R) for i in range(NH)]
        sq = sbuf(nc, c, tag + "sq", [P, 4, W])
        vec = sbuf(nc, c, tag + "vec", [P, 5, 4])
        part = sbuf(nc, c, tag + "part", [P, 2, 32])
        (s_part,) = semaphores(nc, c, tag, "part")
        s_set, s_sum, x_hi, x_lo, u_ps, h_sb, h_hi, h_lo, h_sq, q_step, q_ps, vstep, rms, y_ps, x_done = semaphores(
            nc, c, tag, "set sum x_hi x_lo u_ps h_sb h_hi h_lo h_sq q_step q_ps vstep rms y_ps xd")
        gate = K.gate[:, 1, layer:layer + 1]
        with nc.Block() as block:
            @block.sync
            def _(sp):
                norm.sync(sp)

            @block.tensor
            def _(pe):
                norm.tensor(pe)
                pe.wait_ge(s_set, 2)
                pe.matmul(ps[:, 7, 0:2], K.ones[:, :], wv[:, 0, :], start=True, stop=True).then_inc(s_sum, 1)
                pe.wait_ge(s_set, 8)
                pe.wait_ge(norm.turned, NT // 2)

                with pe.Fori(0, B) as b:
                    def squares(g, f):
                        pe.wait_ge(h_sq, (b * NH + g) * FT + f + 1)
                        for j in range(4):
                            m = pe.matmul(ps[:, 6 + g, j:j + 1], sq[:, f % 4, j * P:(j + 1) * P], K.ones[:, 0:1],
                                          start=(f == 0 and j == 0), stop=(f == FT - 1), skip_group_check=True)
                        m.then_inc(q_step, 1)
                        if f == FT - 1:
                            pe.sem_inc(q_ps, 1)

                    pe.wait_ge(x_done, b * TB + 1)
                    todo = [(g, f) for g in range(NH) for f in range(FT)]
                    for n, (g, f) in enumerate(todo):
                        if f == 0:
                            pe.wait_ge(x_lo, b * NH + g + 1)
                        if n >= 4:
                            pe.wait_ge(h_sb, b * NH * FT + n - 3)
                        for k in range(KT):
                            for part_n, xs in enumerate((xh, xl)):
                                m = pe.matmul(ps[:, f % 4, :], tu[:, k, f * P:(f + 1) * P], xs[:, g, k, :],
                                              start=(k == 0 and part_n == 0), stop=(k == KT - 1 and part_n == 1))
                        m.then_inc(u_ps, 1)
                        if n >= 2:
                            squares(*todo[n - 2])
                    squares(*todo[-2])
                    squares(*todo[-1])
                    for g in range(NH):
                        pe.wait_ge(h_lo, (b * NH + g) * FT + FT)
                        for i in range(4):
                            if i >= 2 or g:
                                pe.wait_ge(x_done, (b * NH + g) * 4 + i)
                            for f in range(FT):
                                for n, hs in enumerate((hh[g], hl[g])):
                                    m = pe.matmul(ps[:, 4 + i % 2, 0:D], hs[:, f, i * P:(i + 1) * P], td[:, f, :],
                                                  start=(f == 0 and n == 0), stop=(f == FT - 1 and n == 1))
                            m.then_inc(y_ps, 1)

            @block.scalar
            def _(act):
                norm.scalar(act)
                with act.Fori(0, B) as b:
                    for n in range(NH * FT):
                        act.wait_ge(u_ps, b * NH * FT + n + 1)
                        if n >= 4:
                            act.wait_ge(h_lo, b * NH * FT + n - 3)
                            act.wait_ge(h_sq, b * NH * FT + n - 3)
                        act.activation(h[:, n % 4, :], ps[:, n % 4, :], ACT.Gelu).then_inc(h_sb, 1)

            @block.gpsimd
            def _(pool):
                norm.gpsimd(pool)
                with pool.Fori(0, B) as b:
                    for n in range(NH * FT):
                        pool.wait_ge(h_sb, b * NH * FT + n + 1)
                        if n >= 4:
                            pool.wait_ge(q_step, b * NH * FT + n - 3)
                        pool.tensor_tensor(sq[:, n % 4, :], h[:, n % 4, :], h[:, n % 4, :], ALU.mult).then_inc(h_sq, 1)
                    for g in range(NH):
                        pool.wait_ge(vstep, (b * NH + g) * 3 + 1)
                        pool.tensor_tensor(vec[:, 1, :], vec[:, 0, :], K.hpow[:, 0:4], ALU.pow).then_inc(rms, 1)

            @block.vector
            def _(dve):
                norm.vector(dve)
                dve.wait_ge(norm.rows, NT)
                dve.wait_ge(norm.loaded, norm.all_loaded)
                s = Steps(s_set)

                def then(ins):
                    s.did(ins)
                    dve.wait_ge(s_set, s.last())

                flats = [z[:, :, :].rearrange("p k f -> p (k f)") for z in (wu, wd)]
                sum_magnitudes(dve, s_part, (wu, wd), part, wv[:, 0, :], s)
                dve.wait_ge(s_sum, 1)
                s.did(dve.tensor_scalar(wv[:, 1, :], ps[:, 7, 0:2], 0.5 / (F * D), None, ALU.mult))
                then(dve.tensor_scalar(wv[:, 2, :], ps[:, 7, 0:2], -0.5 / (F * D), None, ALU.mult))
                for n, q in enumerate((tu, td)):
                    then(dve.tensor_scalar(wneg[:, :], flats[n], wv[:, 2, n:n + 1], None, ALU.is_lt))
                    then(dve.scalar_tensor_tensor(q[:, :, :].rearrange("p k f -> p (k f)"), flats[n],
                                                  wv[:, 1, n:n + 1], wneg[:, :], ALU.is_gt, ALU.subtract))
                dve.wait_ge(norm.turned, NT // 2)
                dve.sem_inc(x_done, 1)
                with dve.Fori(0, B) as b:
                    for g in range(NH):
                        xs = K.xnT[:, :, bass.ds(b * S + g * W, W)]
                        dve.tensor_copy(xh[:, g, :, :], xs).then_inc(x_hi, 1)
                        dve.wait_ge(x_hi, b * NH + g + 1)
                        dve.tensor_tensor(xl[:, g, :, :], xs, xh[:, g, :, :].bitcast(F32), ALU.subtract).then_inc(x_lo, 1)
                    for g in range(NH):
                        for f in range(FT):
                            n = (b * NH + g) * FT + f + 1
                            dve.wait_ge(h_sb, n)
                            dve.tensor_copy(hh[g][:, f, :], h[:, f % 4, :]).then_inc(h_hi, 1)
                            dve.wait_ge(h_hi, n)
                            dve.tensor_tensor(hl[g][:, f, :], h[:, f % 4, :], hh[g][:, f, :].bitcast(F32),
                                              ALU.subtract).then_inc(h_lo, 1)
                    for g in range(NH):
                        dve.wait_ge(q_ps, b * NH + g + 1)
                        v = (b * NH + g) * 3
                        dve.tensor_scalar(vec[:, 0, :], ps[:, 6 + g, 0:4], 1.0 / F, None, ALU.mult).then_inc(vstep, 1)
                        dve.wait_ge(rms, b * NH + g + 1)
                        dve.tensor_scalar(vec[:, 2, :], vec[:, 1, :], 1e-8, None, ALU.add).then_inc(vstep, 1)
                        dve.wait_ge(vstep, v + 2)
                        dve.reciprocal(vec[:, 3, :], vec[:, 2, :]).then_inc(vstep, 1)
                        dve.wait_ge(vstep, v + 3)
                        dve.tensor_scalar(vec[:, 4, :], vec[:, 3, :], gate, None, ALU.mult).then_inc(s_sum, 1)
                        dve.wait_ge(s_sum, b * NH + g + 2)
                        for i in range(4):
                            dve.wait_ge(y_ps, (b * NH + g) * 4 + i + 1)
                            xt = K.x[:, b * TB + 4 * g + i, :]
                            dve.scalar_tensor_tensor(xt, ps[:, 4 + i % 2, 0:D], vec[:, 4, i:i + 1], xt, ALU.mult,
                                                     ALU.add).then_inc(x_done, 1)
                            dve.wait_ge(x_done, (b * NH + g) * 4 + i + 2)
                            dve.bn_stats(K.st[:, b * TB + 4 * g + i, :], xt)


def expert_choice_ffn(nc, ctx, K, tag, norm, layer, gw, sg, su, sd, wg_d, wu_d, wd_d, xn_dram, acc_dram):
    E, F = 16, 512
    CAP = S * 2 // E
    FT = F // P
    NS = B * S // 256
    W = 2 * P
    ps = K.ps
    ROUNDS = CAP // 8
    per_unit = [3, 3, 3, 3, 2, 2]
    assert sum(per_unit) == ROUNDS
    with ExitStack() as c:
        lg = sbuf(nc, c, tag + "lg", [P, NT, E])
        sc = sbuf(nc, c, tag + "sc", [P, TB, B, E])
        vec = sbuf(nc, c, tag + "vec", [P, 3, NT])
        va = [sbuf(nc, c, tag + f"va{i}", [B * E, S]) for i in range(2)]
        tw = sbuf(nc, c, tag + "tw", [B * E, CAP])
        ti = sbuf(nc, c, tag + "ti", [B * E, CAP], U32)
        tf = sbuf(nc, c, tag + "tf", [B * E, CAP])
        boff = sbuf(nc, c, tag + "boff", [B * E, 1])
        wcol = sbuf(nc, c, tag + "wcol", [P, B * E])
        idx = sbuf(nc, c, tag + "idx", [P, B * E], U32)
        wg = [sbuf(nc, c, tag + f"wg{i}", [P, KT, F]) for i in range(2)]
        wu = [sbuf(nc, c, tag + f"wu{i}", [P, KT, F]) for i in range(2)]
        wd = [sbuf(nc, c, tag + f"wd{i}", [P, FT, D]) for i in range(2)]
        xg = [sbuf(nc, c, tag + f"xg{i}", [P, B, D]) for i in range(2)]
        xgT = [sbuf(nc, c, tag + f"xgT{i}", [P, KT, W]) for i in range(2)]
        ge = [sbuf(nc, c, tag + f"ge{i}", [P, FT * W]) for i in range(2)]
        hT = [sbuf(nc, c, tag + f"hT{i}", [P, FT, W]) for i in range(2)]
        eo = [sbuf(nc, c, tag + f"eo{i}", [P, B, D]) for i in range(2)]
        acc = [sbuf(nc, c, tag + f"acc{i}", [P, 4, D]) for i in range(2)]
        (l_ps, smx, exp_in, exp_done, sc_rdy, v_ps, rnd, off, t_rdy, t_ps, i_rdy, xt_ps, xt_sb,
         g_ps, u_ps, ge_sb, h_sb, y_ps, y_sb, x_done, added) = semaphores(
            nc, c, tag, "l_ps smx exp_in exp_done sc_rdy v_ps rnd off t_rdy t_ps i_rdy xt_ps xt_sb "
            "g_ps u_ps ge_sb h_sb y_ps y_sb x_done added")
        w_in, d_in, out_dma, acc_in = (semaphores(nc, c, tag, f"{n}0 {n}1") for n in
                                       ("w_in", "d_in", "out_dma", "acc_in"))
        gat, scat = K.row_gathered, K.row_scattered
        gate = K.gate[:, 1, layer:layer + 1]
        with nc.Block() as block:
            @block.sync
            def _(sp):
                norm.sync(sp)

                def store_shared(u, p):
                    sp.wait_ge(y_sb, u + 3)
                    for j in range(2):
                        sp.dma_start(acc_dram[bass.ds(u * W + j * P, P), :], eo[p][:, j, :]).then_inc(out_dma[p], 16)

                with sp.Fori(0, NS // 2) as pair:
                    u = 2 * pair
                    for p in range(2):
                        store_shared(u + p, p)
                with sp.Fori(0, E // 2) as pair:
                    e = 2 * pair
                    for p in range(2):
                        sp.wait_ge(u_ps, e + p + NS - 1)
                        sp.dma_start(wg[p][:, :, :], wg_d[e + p].rearrange("(k q) f -> q k f", q=P)).then_inc(w_in[p], 16)
                        sp.dma_start(wu[p][:, :, :], wu_d[e + p].rearrange("(k q) f -> q k f", q=P)).then_inc(w_in[p], 16)
                        sp.wait_ge(y_ps, e + p + NS + 1)
                        sp.dma_start(wd[p][:, :, :], wd_d[e + p].rearrange("(k q) f -> q k f", q=P)).then_inc(d_in[p], 16)
                sp.wait_ge(added, E + 2)
                for q in range(4):
                    if q >= 2:
                        sp.wait_ge(x_done, q - 1)
                    sp.dma_start(acc[q % 2][:, :, :],
                                 acc_dram[q * 512:(q + 1) * 512, :].rearrange("(t p) d -> p t d", p=P)).then_inc(acc_in[q % 2], 16)

            @block.gpsimd
            def _(pool):
                norm.gpsimd(pool)
                pool.memset(boff[:, :], float(S)).then_inc(off, 1)
                pool.wait_ge(off, 1)
                pool.affine_select(out=boff[:, :], in_=boff[:, :], compare_op=ALU.is_ge, fill=0.0, base=-E,
                                   pattern=[[0, 1]], channel_multiplier=1).then_inc(off, 1)

                def gather(e):
                    if e >= 2:
                        pool.wait_ge(xt_ps, e - 1)
                    for b in range(B):
                        n = b * E + e
                        pool.indirect_dma_start(xg[e % 2][:, b, :], None, xn_dram[:, :],
                                                bass.IndirectOffsetOnAxis(ap=idx[:, n:n + 1], axis=0)).then_inc(gat[e % 2], 16)

                pool.sem_inc(added, 2)
                pool.wait_ge(i_rdy, 2)
                pool.wait_ge(norm.s_out, 64)
                gather(0)
                gather(1)
                for e in range(E):
                    if e % 2 == 0 and e + 2 < E:
                        gather(e + 2)
                        gather(e + 3)
                    if e == 0:
                        for q in range(2):
                            pool.wait_ge(out_dma[q], 32 + 32 * NS // 2)
                    else:
                        pool.wait_ge(scat[(e - 1) % 2], 32 * ((e - 1) // 2 + 1))
                        pool.sem_inc(added, 1)
                    pool.wait_ge(y_sb, NS + e + 3)
                    for b in range(B):
                        n = b * E + e
                        pool.indirect_dma_start(acc_dram[:, :], bass.IndirectOffsetOnAxis(ap=idx[:, n:n + 1], axis=0),
                                                eo[e % 2][:, b, :], None, compute_op=ALU.add).then_inc(scat[e % 2], 16)
                pool.wait_ge(scat[(E - 1) % 2], 32 * (E // 2))
                pool.sem_inc(added, 1)

            def up(pe, n, p, g, u, rhs):
                pe.wait_ge(ge_sb, n + 1)
                for f in range(FT):
                    for k in range(KT):
                        m = pe.matmul(ps[:, f // 2, (f % 2) * W:(f % 2 + 1) * W], g[:, k, f * P:(f + 1) * P], rhs[k],
                                      start=(k == 0), stop=(k == KT - 1))
                m.then_inc(g_ps, 1)
                pe.wait_ge(h_sb, n + 2)
                for f in range(FT):
                    for k in range(KT):
                        m = pe.matmul(ps[:, 2 + f // 2, (f % 2) * W:(f % 2 + 1) * W], u[:, k, f * P:(f + 1) * P], rhs[k],
                                      start=(k == 0), stop=(k == KT - 1))
                m.then_inc(u_ps, 1)

            def down(pe, n, p, w):
                pe.wait_ge(h_sb, n + 3)
                pe.wait_ge(y_sb, n + 1)
                for j in range(2):
                    for f in range(FT):
                        m = pe.matmul(ps[:, 4 + p, j * D:(j + 1) * D], hT[p][:, f, j * P:(j + 1) * P], w[:, f, :],
                                      start=(f == 0), stop=(f == FT - 1))
                m.then_inc(y_ps, 1)

            @block.tensor
            def _(pe):
                norm.tensor(pe)
                pe.wait_ge(norm.turned, NT // 2)
                pe.wait_ge(norm.loaded, norm.all_loaded)
                for t in range(NT):
                    for k in range(KT):
                        m = pe.matmul(ps[:, 7, t * E:(t + 1) * E], K.xnT[:, k, t * P:(t + 1) * P], gw[:, k, :],
                                      start=(k == 0), stop=(k == KT - 1))
                m.then_inc(l_ps, 1)
                pe.sem_inc(y_ps, 2)
                pe.wait_ge(sc_rdy, 1)
                for i in range(TB):
                    m = pe.transpose(ps[0:B * E, 6 + i // 4, (i % 4) * P:(i % 4 + 1) * P],
                                     sc[:, i, :, :].rearrange("p b e -> p (b e)"), K.ident[:, :])
                m.then_inc(v_ps, 1)

                def shared_pair(u):
                    for p in range(2):
                        rhs = [K.xnT[:, k, bass.ds((u + p) * W, W)] for k in range(KT)]
                        up(pe, u + p, p, sg, su, rhs)
                    for p in range(2):
                        down(pe, u + p, p, sd)

                with pe.Fori(0, (NS - 2) // 2) as pair:
                    u = 2 * pair
                    shared_pair(u)
                pe.wait_ge(t_rdy, 1)
                pe.transpose(ps[:, 6, 0:B * E], tf[:, :], K.ident[0:B * E, 0:B * E])
                pe.transpose(ps[:, 6, 128:128 + B * E], tw[:, :], K.ident[0:B * E, 0:B * E]).then_inc(t_ps, 1)
                shared_pair(NS - 2)
                pe.wait_ge(i_rdy, 2)
                with pe.Fori(0, E // 2) as pair:
                    e = 2 * pair
                    for p in range(2):
                        pe.wait_ge(gat[p], 32 * pair + 32)
                        pe.wait_ge(xt_sb, e + p + 1)
                        for k in range(KT):
                            for b in range(B):
                                m = pe.transpose(ps[:, 6 + p, (k * B + b) * P:(k * B + b + 1) * P],
                                                 xg[p][:, b, k * P:(k + 1) * P], K.ident[:, :])
                        m.then_inc(xt_ps, 1)
                    for p in range(2):
                        pe.wait_ge(xt_sb, e + p + 3)
                        pe.wait_ge(w_in[p], 32 * pair + 32)
                        up(pe, e + p + NS, p, wg[p], wu[p], [xgT[p][:, k, :] for k in range(KT)])
                    for p in range(2):
                        pe.wait_ge(d_in[p], 16 * pair + 16)
                        down(pe, e + p + NS, p, wd[p])

            @block.scalar
            def _(act):
                def gelu(n, p):
                    act.wait_ge(g_ps, n + 1)
                    act.wait_ge(h_sb, n + 1)
                    act.activation(ge[p][:, :], ps[:, 0:2, :].rearrange("p a c -> p (a c)"), ACT.Gelu).then_inc(ge_sb, 1)

                norm.scalar(act)
                act.sem_inc(ge_sb, 1)
                act.sem_inc(y_sb, 2)
                act.sem_inc(xt_sb, 2)
                act.wait_ge(exp_in, 1)
                act.activation(lg[:, :, :], lg[:, :, :], ACT.Exp).then_inc(exp_done, 1)
                with act.Fori(0, NS // 2) as pair:
                    u = 2 * pair
                    for p in range(2):
                        gelu(u + p, p)
                    for p in range(2):
                        act.wait_ge(y_ps, u + p + 3)
                        act.wait_ge(out_dma[p], 32 * pair + 32)
                        act.activation(eo[p][:, :, :].rearrange("p a c -> p (a c)"), ps[:, 4 + p, :],
                                       ACT.Copy).then_inc(y_sb, 1)
                with act.Fori(0, E // 2) as pair:
                    e = 2 * pair
                    for p in range(2):
                        act.wait_ge(xt_ps, e + p + 1)
                        act.wait_ge(u_ps, e + p + NS - 1)
                        act.activation(xgT[p][:, :, :].rearrange("p a c -> p (a c)"), ps[:, 6 + p, :],
                                       ACT.Copy).then_inc(xt_sb, 1)
                    for p in range(2):
                        gelu(e + p + NS, p)

            @block.vector
            def _(dve):
                norm.vector(dve)
                dve.wait_ge(norm.rows, NT)
                dve.sem_inc(h_sb, 2)
                for p in range(2):
                    dve.sem_inc(out_dma[p], 32)
                s = Steps(smx)

                def then(ins):
                    s.did(ins)
                    dve.wait_ge(smx, s.last())

                dve.wait_ge(l_ps, 1)
                logits = ps[:, 7, 0:NT * E].rearrange("p (t e) -> p t e", t=NT)
                then(dve.tensor_reduce(vec[:, 0, :], logits, AX.X, ALU.max))
                dve.tensor_tensor(lg[:, :, :], logits, vec[:, 0, :].unsqueeze(2).broadcast_to([P, NT, E]),
                                  ALU.subtract).then_inc(exp_in, 1)
                dve.wait_ge(exp_done, 1)
                then(dve.tensor_reduce(vec[:, 1, :], lg[:, :, :], AX.X, ALU.add))
                then(dve.reciprocal(vec[:, 2, :], vec[:, 1, :]))
                dve.tensor_tensor(sc[:, :, :, :].rearrange("p i b e -> p b i e"),
                                  lg[:, :, :].rearrange("p (b i) e -> p b i e", b=B),
                                  vec[:, 2, :].rearrange("p (b i) -> p b i", b=B).unsqueeze(3).broadcast_to([P, B, TB, E]),
                                  ALU.mult).then_inc(sc_rdy, 1)
                dve.wait_ge(v_ps, 1)
                then(dve.tensor_copy(va[0][:, :], ps[0:B * E, 6:8, :].rearrange("p a c -> p (a c)")))

                def pick(r):
                    best = tw[:, 8 * r:8 * r + 8]
                    then(dve.max(best, va[r % 2][:, :]))
                    dve.max_index(ti[:, 8 * r:8 * r + 8], best, va[r % 2][:, :]).then_inc(rnd, 1)
                    then(dve.match_replace(va[1 - r % 2][:, :], best, va[r % 2][:, :], -1.0))

                def hidden(n, p):
                    dve.wait_ge(ge_sb, n + 2)
                    dve.wait_ge(u_ps, n + 1)
                    dve.wait_ge(y_ps, n + 1)
                    dve.tensor_tensor(hT[p][:, :, :].rearrange("p a c -> p (a c)"), ge[p][:, :],
                                      ps[:, 2:4, :].rearrange("p a c -> p (a c)"), ALU.mult).then_inc(h_sb, 1)

                r = 0
                for u in range(NS):
                    if u < len(per_unit):
                        for _ in range(per_unit[u]):
                            pick(r)
                            r += 1
                    hidden(u, u % 2)
                    if r == ROUNDS and u == len(per_unit) - 1:
                        dve.wait_ge(rnd, ROUNDS)
                        dve.wait_ge(off, 2)
                        dve.tensor_scalar(tf[:, :], ti[:, :], boff[:, 0:1], None, ALU.add).then_inc(t_rdy, 1)
                        dve.wait_ge(t_ps, 1)
                        dve.tensor_copy(idx[:, :], ps[:, 6, 0:B * E]).then_inc(i_rdy, 1)
                        dve.tensor_copy(wcol[:, :], ps[:, 6, 128:128 + B * E]).then_inc(i_rdy, 1)
                dve.wait_ge(i_rdy, 2)
                for p in range(2):
                    dve.wait_ge(out_dma[p], 32 + 32 * NS // 2)
                with dve.Fori(0, E // 2) as pair:
                    e = 2 * pair
                    for p in range(2):
                        hidden(e + p + NS, p)
                    for p in range(2):
                        dve.wait_ge(y_ps, e + p + NS + 3)
                        dve.wait_ge(added, e + p + 1)
                        for b in range(B):
                            m = dve.tensor_scalar(eo[p][:, b, :], ps[:, 4 + p, b * D:(b + 1) * D],
                                                  wcol[:, bass.ds(e + p + b * E, 1)], None, ALU.mult)
                        m.then_inc(y_sb, 1)
                for q in range(4):
                    dve.wait_ge(acc_in[q % 2], 16 * (q // 2 + 1))
                    xt = K.x[:, 4 * q:4 * q + 4, :]
                    dve.scalar_tensor_tensor(xt, acc[q % 2][:, :, :], gate, xt, ALU.mult, ALU.add).then_inc(x_done, 1)
                    dve.wait_ge(x_done, q + 1)
                    for t in range(4 * q, 4 * q + 4):
                        dve.bn_stats(K.st[:, t, :], K.x[:, t, :])


def top2_ffn(nc, ctx, K, tag, norm, layer, gw, w1, w3, w2, n_weights, xn_dram, acc_dram, out):
    E, F, TOP = 8, 512, 2
    FT = F // P
    ps = K.ps
    NTILE = (TOP * B * S + E * (P - 1)) // P
    NTILE += NTILE % 2
    NPAIR = NTILE // 2
    gate = K.gate[:, 1, layer:layer + 1]
    with ExitStack() as c:
        take = sbuf(nc, c, tag + "take", [P, NTILE], U32)
        give = sbuf(nc, c, tag + "give", [P, NTILE], U32)
        weight = sbuf(nc, c, tag + "weight", [P, NTILE])
        te = sbuf(nc, c, tag + "te", [1, NTILE], I32)

        with ExitStack() as r:
            pr = sbuf(nc, r, tag + "pr", [P, NT, E])
            oh = sbuf(nc, r, tag + "oh", [P, TOP, NT, E])
            both = sbuf(nc, r, tag + "both", [P, NT, E])
            tmp = sbuf(nc, r, tag + "tmp", [P, 3, NT, E])
            vec = sbuf(nc, r, tag + "vec", [P, 8, NT])
            ev = sbuf(nc, r, tag + "ev", [P, 6, E])
            gwt = sbuf(nc, r, tag + "gwt", [P, TOP, NT])
            slf = sbuf(nc, r, tag + "slf", [P, TOP, NT])
            hi = sbuf(nc, r, tag + "hi", [P, TOP, NT])
            lo = sbuf(nc, r, tag + "lo", [P, TOP, NT])
            in_lane = sbuf(nc, r, tag + "in_lane", [P, TOP, NT, P])
            in_tile = sbuf(nc, r, tag + "in_tile", [P, TOP, NT, 2, NTILE])
            empty = sbuf(nc, r, tag + "empty", [P, NTILE])
            tri = sbuf(nc, r, tag + "tri", [P, P])
            rev_i = sbuf(nc, r, tag + "rev_i", [P, E], I32)
            rev = sbuf(nc, r, tag + "rev", [P, E])
            jrow_i = sbuf(nc, r, tag + "jrow_i", [P, NTILE], I32)
            jrow = sbuf(nc, r, tag + "jrow", [P, NTILE])
            lane_i = sbuf(nc, r, tag + "lane_i", [P, P], I32)
            lane = sbuf(nc, r, tag + "lane", [P, P])
            tok_i = sbuf(nc, r, tag + "tok_i", [P, NT], I32)
            tok = sbuf(nc, r, tag + "tok", [P, NT])
            dump_i = sbuf(nc, r, tag + "dump_i", [P, 1], I32)
            dump = sbuf(nc, r, tag + "dump", [P, 1])
            cmp = sbuf(nc, r, tag + "cmp", [1, NTILE, E])
            cnt = sbuf(nc, r, tag + "cnt", [1, 2, NTILE])
            l_ps, step, exp_in, exp_done, const, oh_rdy, rank_ps, lo_rdy, lane_rdy, tile_rdy, slot_ps, rows_out = semaphores(
                nc, r, tag, "l_ps step exp_in exp_done const oh_rdy rank_ps lo_rdy lane_rdy tile_rdy slot_ps rows_out")
            with nc.Block() as block:
                @block.sync
                def _(sp):
                    norm.sync(sp)
                    sp.wait_ge(norm.rows, NT)
                    for dst, src in ((xn_dram, K.xn), (acc_dram, K.x)):
                        for q in range(2):
                            sp.dma_start(dst[q * S:(q + 1) * S, :].rearrange("(t p) d -> p t d", p=P),
                                         src[:, TB * q:TB * (q + 1), :]).then_inc(rows_out, 16)
                    sp.dma_start(acc_dram[B * S:B * S + P, :], K.zeros[:, :]).then_inc(rows_out, 16)
                    sp.wait_ge(rows_out, 5 * 16)

                @block.tensor
                def _(pe):
                    norm.tensor(pe)
                    pe.wait_ge(norm.turned, NT // 2)
                    pe.wait_ge(norm.loaded, norm.all_loaded)
                    for t in range(NT):
                        for k in range(KT):
                            m = pe.matmul(ps[:, 0, t * E:(t + 1) * E], K.xnT[:, k, t * P:(t + 1) * P], gw[:, k, :],
                                          start=(k == 0), stop=(k == KT - 1))
                    m.then_inc(l_ps, 1)
                    pe.wait_ge(oh_rdy, 1)
                    pe.wait_ge(const, 6)
                    flat = both[:, :, :].rearrange("p t e -> p (t e)")
                    pe.matmul(ps[:, 2, 0:NT * E], K.ones[:, :], flat, start=True, stop=True)
                    pe.matmul(ps[:, 1, 0:NT * E], tri[:, :], flat, start=True, stop=False, skip_group_check=True)
                    for n in range(1, NT):
                        m = pe.matmul(ps[:, 1, n * E:NT * E], K.ones[:, :], flat[:, 0:(NT - n) * E], start=False,
                                      stop=(n == NT - 1), skip_group_check=True)
                    m.then_inc(rank_ps, 1)
                    pe.wait_ge(tile_rdy, 1)
                    for n in range(TOP):
                        pe.wait_ge(lane_rdy, n + 1)
                        for t in range(NT):
                            m = pe.matmul(ps[:, 3, 0:2 * NTILE], in_lane[:, n, t, :],
                                          in_tile[:, n, t, :, :].rearrange("p a j -> p (a j)"),
                                          start=(n == 0 and t == 0), stop=(n == TOP - 1 and t == NT - 1))
                    m.then_inc(slot_ps, 1)

                @block.scalar
                def _(act):
                    norm.scalar(act)
                    act.wait_ge(exp_in, 1)
                    act.activation(pr[:, :, :], pr[:, :, :], ACT.Exp).then_inc(exp_done, 1)

                @block.gpsimd
                def _(pool):
                    norm.gpsimd(pool)
                    pool.iota(rev_i[:, :], [[-1, E]], base=E, channel_multiplier=0).then_inc(const, 1)
                    pool.iota(jrow_i[:, :], [[1, NTILE]], base=0, channel_multiplier=0).then_inc(const, 1)
                    pool.iota(lane_i[:, :], [[1, P]], base=0, channel_multiplier=0).then_inc(const, 1)
                    pool.iota(tok_i[:, :], [[P, NT]], base=1, channel_multiplier=1).then_inc(const, 1)
                    pool.iota(dump_i[:, :], [[1, 1]], base=B * S + 1, channel_multiplier=1).then_inc(const, 1)
                    pool.affine_select(out=tri[:, :], in_=K.ones[:, :], compare_op=ALU.is_ge, fill=0.0, base=-1,
                                       pattern=[[1, P]], channel_multiplier=-1).then_inc(const, 1)

                @block.vector
                def _(dve):
                    norm.vector(dve)
                    dve.wait_ge(norm.rows, NT)
                    s = Steps(step)

                    def then(ins):
                        s.did(ins)
                        dve.wait_ge(step, s.last())

                    def wide(v):
                        return v.unsqueeze(2).broadcast_to([P, NT, E])

                    def per_expert(v):
                        return v.unsqueeze(1).broadcast_to([P, NT, E])

                    dve.wait_ge(const, 5)
                    for f, i in ((rev, rev_i), (jrow, jrow_i), (lane, lane_i), (tok, tok_i), (dump, dump_i)):
                        s.did(dve.tensor_copy(f[:, :], i[:, :]))
                    dve.wait_ge(step, s.last())
                    dve.wait_ge(l_ps, 1)
                    logits = ps[:, 0, 0:NT * E].rearrange("p (t e) -> p t e", t=NT)
                    then(dve.tensor_reduce(vec[:, 0, :], logits, AX.X, ALU.max))
                    dve.tensor_tensor(pr[:, :, :], logits, wide(vec[:, 0, :]), ALU.subtract).then_inc(exp_in, 1)
                    dve.wait_ge(exp_done, 1)
                    then(dve.tensor_reduce(vec[:, 1, :], pr[:, :, :], AX.X, ALU.add))
                    then(dve.reciprocal(vec[:, 2, :], vec[:, 1, :]))
                    then(dve.tensor_tensor(pr[:, :, :], pr[:, :, :], wide(vec[:, 2, :]), ALU.mult))
                    src = pr
                    for n in range(TOP):
                        best = vec[:, 3 + n, :]
                        then(dve.tensor_reduce(best, src[:, :, :], AX.X, ALU.max))
                        then(dve.tensor_tensor(tmp[:, 0, :, :], src[:, :, :], wide(best), ALU.is_equal))
                        then(dve.tensor_tensor(tmp[:, 1, :, :], tmp[:, 0, :, :], per_expert(rev[:, :]), ALU.mult))
                        then(dve.tensor_reduce(vec[:, 5, :], tmp[:, 1, :, :], AX.X, ALU.max))
                        then(dve.tensor_tensor(oh[:, n, :, :], tmp[:, 1, :, :], wide(vec[:, 5, :]), ALU.is_equal))
                        if n == 0:
                            then(dve.scalar_tensor_tensor(tmp[:, 2, :, :], oh[:, 0, :, :], -2.0, pr[:, :, :],
                                                          ALU.mult, ALU.add))
                            src = tmp[:, 2, :, :]
                    dve.tensor_tensor(both[:, :, :], oh[:, 0, :, :], oh[:, 1, :, :], ALU.add).then_inc(oh_rdy, 1)
                    then(dve.tensor_tensor(vec[:, 6, :], vec[:, 3, :], vec[:, 4, :], ALU.add))
                    then(dve.reciprocal(vec[:, 7, :], vec[:, 6, :]))
                    then(dve.tensor_scalar(vec[:, 7, :], vec[:, 7, :], gate, None, ALU.mult))
                    for n in range(TOP):
                        s.did(dve.tensor_tensor(gwt[:, n, :], vec[:, 3 + n, :], vec[:, 7, :], ALU.mult))
                    dve.wait_ge(rank_ps, 1)
                    then(dve.tensor_reduce(ev[:, 0, :], ps[:, 2, 0:NT * E].rearrange("p (t e) -> p e t", t=NT), AX.X, ALU.add))
                    then(dve.tensor_scalar(ev[:, 1, :], ev[:, 0, :], 1.0 / P, (P - 1.0) / (2 * P), ALU.mult, ALU.add))
                    then(dve.tensor_scalar(ev[:, 2, :], ev[:, 1, :], MAGIC, MAGIC, ALU.add, ALU.subtract))
                    then(dve.tensor_tensor_scan(ev[:, 3, :], K.ones[:, 0:E], ev[:, 2, :], 0.0, ALU.mult, ALU.add))
                    then(dve.tensor_tensor(ev[:, 4, :], ev[:, 3, :], ev[:, 2, :], ALU.subtract))
                    then(dve.scalar_tensor_tensor(tmp[:, 0, :, :], per_expert(ev[:, 4, :]), float(P),
                                                  ps[:, 1, 0:NT * E].rearrange("p (t e) -> p t e", t=NT),
                                                  ALU.mult, ALU.add))
                    for n in range(TOP):
                        then(dve.tensor_tensor(tmp[:, 1, :, :], oh[:, n, :, :], tmp[:, 0, :, :], ALU.mult))
                        then(dve.tensor_reduce(slf[:, n, :], tmp[:, 1, :, :], AX.X, ALU.add))
                    then(dve.tensor_scalar(hi[:, :, :], slf[:, :, :], 1.0 / P, (P - 1.0) / (2 * P), ALU.mult, ALU.subtract))
                    then(dve.tensor_scalar(hi[:, :, :], hi[:, :, :], MAGIC, MAGIC, ALU.add, ALU.subtract))
                    then(dve.scalar_tensor_tensor(lo[:, :, :], hi[:, :, :], -float(P), slf[:, :, :], ALU.mult, ALU.add))
                    for n in range(TOP):
                        def tiles(v):
                            return v.unsqueeze(2).broadcast_to([P, NT, NTILE])
                        then(dve.tensor_tensor(in_tile[:, n, :, 0, :], tiles(hi[:, n, :]),
                                               jrow[:, :].unsqueeze(1).broadcast_to([P, NT, NTILE]), ALU.is_equal))
                        then(dve.tensor_tensor(in_tile[:, n, :, 1, :], in_tile[:, n, :, 0, :], tiles(gwt[:, n, :]), ALU.mult))
                        m = dve.tensor_tensor(in_tile[:, n, :, 0, :], in_tile[:, n, :, 0, :], tiles(tok[:, :]), ALU.mult)
                    m.then_inc(tile_rdy, 1)
                    for n in range(TOP):
                        dve.tensor_tensor(in_lane[:, n, :, :], lo[:, n, :].unsqueeze(2).broadcast_to([P, NT, P]),
                                          lane[:, :].unsqueeze(1).broadcast_to([P, NT, P]), ALU.is_equal).then_inc(lane_rdy, 1)
                    then(dve.tensor_tensor(cmp[:, :, :], ev[0:1, 3, :].unsqueeze(1).broadcast_to([1, NTILE, E]),
                                           jrow[0:1, :].unsqueeze(2).broadcast_to([1, NTILE, E]), ALU.is_le))
                    then(dve.tensor_reduce(cnt[:, 0, :], cmp[:, :, :], AX.X, ALU.add))
                    then(dve.tensor_scalar(te[:, :], cnt[:, 0, :], E - 1.0, None, ALU.min))
                    dve.wait_ge(slot_ps, 1)
                    of_slot = ps[:, 3, 0:NTILE]
                    s.did(dve.tensor_scalar(take[:, :], of_slot, -1.0, 0.0, ALU.add, ALU.max))
                    then(dve.tensor_scalar(empty[:, :], of_slot, 0.0, dump[:, 0:1], ALU.is_equal, ALU.mult))
                    s.did(dve.scalar_tensor_tensor(give[:, :], of_slot, -1.0, empty[:, :], ALU.add, ALU.add))
                    s.did(dve.tensor_copy(weight[:, :], ps[:, 3, NTILE:2 * NTILE]))

        with ExitStack() as r:
            xs = [sbuf(nc, r, tag + f"xs{i}", [P, D]) for i in range(2)]
            xsT = sbuf(nc, r, tag + "xsT", [P, 2 * KT * P])
            s1 = [sbuf(nc, r, tag + f"s1{i}", [P, F]) for i in range(2)]
            hid = [sbuf(nc, r, tag + f"hid{i}", [P, F]) for i in range(2)]
            hT = [sbuf(nc, r, tag + f"hT{i}", [P, F]) for i in range(2)]
            yo = [sbuf(nc, r, tag + f"yo{i}", [P, D]) for i in range(2)]
            X_BANK, HT_BANK, Y_BANK = 6, (4, 7), (5, 4)
            xt_ps, xt_sb, h1_ps, up_ps, silu, h_sb, ht_ps, ht_sb, y_ps, y_sb, yo_free, all_in, stored = semaphores(
                nc, r, tag, "xt_ps xt_sb h1_ps up_ps silu h_sb ht_ps ht_sb y_ps y_sb yo_free all_in stored")
            x_in, y_out = K.rows_taken, K.rows_given
            with nc.Block() as block:
                @block.gpsimd
                def _(pool):
                    def gather(j):
                        pool.indirect_dma_start(xs[j % 2][:, :], None, xn_dram[:, :],
                                                bass.IndirectOffsetOnAxis(ap=take[:, j:j + 1], axis=0)).then_inc(x_in[j % 2], 16)

                    for p in range(2):
                        gather(p)
                    pool.sem_inc(yo_free, 2)
                    pool.wait_ge(xt_ps, 1)
                    for p in range(2):
                        gather(2 + p)
                    for j in range(NTILE):
                        if j % 2 == 0 and j + 4 < NTILE:
                            pool.wait_ge(xt_ps, j // 2 + 2)
                            for p in range(2):
                                gather(j + 4 + p)
                        if j:
                            pool.wait_ge(y_out[(j - 1) % 2], 16 * ((j - 1) // 2 + 1))
                            pool.sem_inc(yo_free, 1)
                        pool.wait_ge(y_sb, j + 3)
                        pool.indirect_dma_start(acc_dram[:, :], bass.IndirectOffsetOnAxis(ap=give[:, j:j + 1], axis=0),
                                                yo[j % 2][:, :], None, compute_op=ALU.add).then_inc(y_out[j % 2], 16)
                    for p in range(2):
                        pool.wait_ge(y_out[p], 16 * NPAIR)
                    pool.sem_inc(all_in, 1)

                @block.sync
                def _(sp):
                    flat = out.rearrange("b s d -> (b s) d")
                    sp.wait_ge(all_in, 1)
                    for q in range(4):
                        rows = slice(q * B * S // 4, (q + 1) * B * S // 4)
                        sp.dma_start(flat[rows, :], acc_dram[rows, :]).then_inc(stored, 16)
                    sp.wait_ge(stored, 64)

                @block.tensor
                def _(pe):
                    def turn(k):
                        pe.wait_ge(xt_sb, k + 1)
                        for p in range(2):
                            pe.wait_ge(x_in[p], 16 * k + 16)
                            for n in range(KT):
                                m = pe.transpose(ps[:, X_BANK, (p * KT + n) * P:(p * KT + n + 1) * P],
                                                 xs[p][:, n * P:(n + 1) * P], K.ident[:, :])
                        m.then_inc(xt_ps, 1)

                    def pair(k, last):
                        expert = []
                        pe.wait_ge(xt_sb, k + 2)
                        for p in range(2):
                            j = 2 * k + p
                            where = te[0:1, j:j + 1] if last else te[0:1, bass.ds(j, 1)]
                            e = pe.value_load(where, min_val=0, max_val=E - 1)
                            expert.append(e)
                            pe.wait_ge(h_sb, j + 1)
                            for n, w in enumerate((w1, w3)):
                                for i in range(KT):
                                    m = pe.matmul(ps[:, 2 * p + n, :], xsT[:, (p * KT + i) * P:(p * KT + i + 1) * P],
                                                  w[:, e, i, :], start=(i == 0), stop=(i == KT - 1))
                                m.then_inc((h1_ps, up_ps)[n], 1)
                        if not last:
                            turn(k + 1)
                        pe.wait_ge(y_sb, 2 * k + 2)
                        for p in range(2):
                            j = 2 * k + p
                            pe.wait_ge(h_sb, j + 3)
                            pe.wait_ge(ht_sb, j + 1)
                            for f in range(FT):
                                m = pe.transpose(ps[:, HT_BANK[p], f * P:(f + 1) * P], hid[p][:, f * P:(f + 1) * P],
                                                 K.ident[:, :])
                            m.then_inc(ht_ps, 1)
                        for p in range(2):
                            j = 2 * k + p
                            pe.wait_ge(ht_sb, j + 3)
                            pe.wait_ge(y_sb, j + 1)
                            for f in range(FT):
                                m = pe.matmul(ps[:, Y_BANK[p], 0:D], hT[p][:, f * P:(f + 1) * P], w2[:, expert[p], f, :],
                                              start=(f == 0), stop=(f == FT - 1))
                            m.then_inc(y_ps, 1)

                    for sem in (ht_ps, y_ps):
                        pe.sem_inc(sem, 2)
                    pe.wait_ge(K.experts_in, 16 * n_weights)
                    turn(0)
                    with pe.Fori(0, NPAIR - 1) as k:
                        pair(k, False)
                    pair(NPAIR - 1, True)

                @block.scalar
                def _(act):
                    with act.Fori(0, NPAIR) as k:
                        for p in range(2):
                            j = 2 * k + p
                            act.wait_ge(h1_ps, j + 1)
                            act.wait_ge(h_sb, j + 1)
                            act.activation(s1[p][:, :], ps[:, 2 * p, :], ACT.Silu).then_inc(silu, 1)

                @block.vector
                def _(dve):
                    def copy_turned(k):
                        dve.wait_ge(xt_ps, k + 1)
                        dve.tensor_copy(xsT[:, :], ps[:, X_BANK, :]).then_inc(xt_sb, 1)

                    def pair(k, last):
                        for p in range(2):
                            j = 2 * k + p
                            dve.wait_ge(silu, j + 1)
                            dve.wait_ge(up_ps, j + 1)
                            dve.wait_ge(ht_ps, j + 1)
                            dve.tensor_tensor(hid[p][:, :], s1[p][:, :], ps[:, 2 * p + 1, :], ALU.mult).then_inc(h_sb, 1)
                        if not last:
                            copy_turned(k + 1)
                        for p in range(2):
                            j = 2 * k + p
                            dve.wait_ge(ht_ps, j + 3)
                            dve.wait_ge(y_ps, j + 1)
                            dve.tensor_copy(hT[p][:, :], ps[:, HT_BANK[p], :]).then_inc(ht_sb, 1)
                        for p in range(2):
                            j = 2 * k + p
                            dve.wait_ge(y_ps, j + 3)
                            dve.wait_ge(yo_free, j + 1)
                            of_tile = weight[:, j:j + 1] if last else weight[:, bass.ds(j, 1)]
                            dve.tensor_scalar(yo[p][:, :], ps[:, Y_BANK[p], 0:D], of_tile, None, ALU.mult).then_inc(y_sb, 1)

                    dve.sem_inc(h_sb, 2)
                    dve.sem_inc(ht_sb, 2)
                    dve.sem_inc(y_sb, 2)
                    dve.sem_inc(xt_sb, 1)
                    copy_turned(0)
                    with dve.Fori(0, NPAIR - 1) as k:
                        pair(k, False)
                    pair(NPAIR - 1, True)


def flamingo(nc, ins, out):
    K = Core()
    with ExitStack() as ctx:
        load_and_constants(nc, ctx, K, ins)
        K.row_gathered = lasting_semaphores(nc, ctx, "row_gathered", "0 1")
        K.row_scattered = lasting_semaphores(nc, ctx, "row_scattered", "0 1")
        K.rows_taken = lasting_semaphores(nc, ctx, "rows_taken", "0 1")
        K.rows_given = lasting_semaphores(nc, ctx, "rows_given", "0 1")

        early = Weights(nc, ctx, ins)
        wq2, wk2, wv2 = early.same("L1_xattn_Wq"), early.rows("L1_xattn_Wk"), early.rows("L1_xattn_Wv")
        bq2, bk2, bv2 = early.same("L1_xattn_bq"), early.same("L1_xattn_bk"), early.repeated("L1_xattn_bv", 1)
        wT4, wn4, bc4 = early.rows("L2_xattn_W"), early.rows("L2_xattn_Wn"), early.same("L2_xattn_b")
        w6 = [early.rows("L3_xattn_w_" + n) for n in "qkvo"]
        (early_in,) = lasting_semaphores(nc, ctx, "early_", "in")
        all_early = (early_in, 16 * len(early.loads))

        def transposed_rows(sub):
            K.xnT = sbuf(nc, sub, "xnT_sb", [P, KT, B * S])

        with ExitStack() as sub:
            w = Weights(nc, sub, ins)
            transposed_rows(sub)
            wq, wk, wv, wo = (w.rows("L0_xattn_W" + n) for n in "qkvo")
            bq, bk = w.same("L0_xattn_bq"), w.same("L0_xattn_bk")
            bv, bo = w.repeated("L0_xattn_bv", 1), w.repeated("L0_xattn_bo")
            norm = Norm(nc, sub, K, "n0_", w.loads, banks=range(4),
                        prefetch=[(dst, src, early_in) for dst, src in early.loads])
            multihead(nc, sub, K, "a0_", norm, 0, wq, wk, wv, wo, bq, bk, bv, bo, mask=ins["mask_1x1xSxS2_ik0"])
        with ExitStack() as sub:
            w = Weights(nc, sub, ins)
            transposed_rows(sub)
            gw, sg, su, sd = (w.rows("L0_ffn_" + n) for n in ("gate_w", "Ws_g", "Ws_u", "Ws_d"))
            xn_dram = nc.dram_tensor("xn_rows_1", (B * S, D), F32, kind="Internal").ap()
            acc_dram = nc.dram_tensor("acc_rows_1", (B * S, D), F32, kind="Internal").ap()
            norm = Norm(nc, sub, K, "n1_", w.loads, to_dram=xn_dram, banks=range(6))
            expert_choice_ffn(nc, sub, K, "f1_", norm, 0, gw, sg, su, sd, ins["L0_ffn_Wg"], ins["L0_ffn_Wu"],
                              ins["L0_ffn_Wd"], xn_dram, acc_dram)

        with ExitStack() as sub:
            transposed_rows(sub)
            norm = Norm(nc, sub, K, "n2_", [], banks=range(4, 8), loaded=all_early)
            sigmoid_attention(nc, sub, K, "a2_", norm, 1, wq2, wk2, wv2, bq2, bk2, bv2)
        with ExitStack() as sub:
            w = Weights(nc, sub, ins)
            w1, w2 = w.rows("L1_ffn_w1"), w.rows("L1_ffn_w2")
            cw, cb = w.same("L1_ffn_conv_w"), w.same("L1_ffn_conv_b")
            norm = Norm(nc, sub, K, "n3_", w.loads)
            bitnet_ffn(nc, sub, K, "f3_", norm, 1, w1, w2, cw, cb)
        clear_semaphores(nc)

        with ExitStack() as sub:
            transposed_rows(sub)
            norm = Norm(nc, sub, K, "n4_", [], banks=range(4, 8), loaded=all_early)
            align_attention(nc, sub, K, "a4_", norm, 2, wT4, wn4, bc4)
        with ExitStack() as sub:
            w = Weights(nc, sub, ins)
            transposed_rows(sub)
            wu, wd = w.rows("L2_ffn_w_up"), w.rows("L2_ffn_w_down")
            norm = Norm(nc, sub, K, "n5_", w.loads, ternary=True, banks=range(4))
            ternary_ffn(nc, sub, K, "f5_", norm, 2, wu, wd)

        late = Weights(nc, ctx, ins)
        w1, w3 = (late.experts("L3_ffn_" + n) for n in ("w1", "w3"))
        (K.experts_in,) = semaphores(nc, ctx, "experts_", "in")
        with ExitStack() as sub:
            transposed_rows(sub)
            norm = Norm(nc, sub, K, "n6_", [], banks=range(4), loaded=all_early,
                        prefetch=[(dst, src, K.experts_in) for dst, src in late.loads])
            multihead(nc, sub, K, "a6_", norm, 3, *w6)
        with ExitStack() as sub:
            w, down = Weights(nc, sub, ins), Weights(nc, sub, ins)
            transposed_rows(sub)
            gw = w.rows("L3_ffn_wg")
            w2 = down.experts("L3_ffn_w2")
            xn_dram = nc.dram_tensor("xn_rows_7", (B * S, D), F32, kind="Internal").ap()
            acc_dram = nc.dram_tensor("acc_rows_7", (B * S + P, D), F32, kind="Internal").ap()
            norm = Norm(nc, sub, K, "n7_", w.loads, banks=range(4, 8),
                        prefetch=[(dst, src, K.experts_in) for dst, src in down.loads])
            top2_ffn(nc, sub, K, "f7_", norm, 3, gw, w1, w3, w2, len(late.loads + down.loads), xn_dram, acc_dram, out)


def kernel(**inputs):
    import concourse.bacc as _bacc
    from concourse.bass_utils import run_bass_kernel_spmd as _run

    nc = _bacc.Bacc("TRN2", target_bir_lowering=False, num_devices=1)

    def laid(name):
        a = np.asarray(inputs[name])
        if name in _FLIP:
            a = np.swapaxes(a, -1, -2)
        if name == "L1_ffn_conv_w":
            a = a.reshape(8, P, 3).transpose(1, 0, 2)
        if name in ("L1_xattn_bq", "L1_xattn_bk"):
            a = a.reshape(64, 1)
        if name in _COLUMNS:
            a = a.reshape(-1, P).T
        if name == "mask_1x1xSxS2_ik0":
            a = a.reshape(S, L)
        return np.ascontiguousarray(a)

    arrays = {n: laid(n) for n in _NAMES}
    arrays["L2_xattn_Wn"] = np.ascontiguousarray(np.asarray(inputs["L2_xattn_W"]))
    arrays["gates"] = np.stack([np.asarray(inputs["g_xattn"]), np.asarray(inputs["g_ffn"])])
    aps = {n: nc.dram_tensor("in_" + n, a.shape, mybir.dt.from_np(a.dtype), kind="ExternalInput").ap()
           for n, a in arrays.items()}
    out = nc.dram_tensor("out_x", (B, S, D), F32, kind="ExternalOutput").ap()
    flamingo(nc, aps, out)
    r = _run(nc, [{"in_" + n: a for n, a in arrays.items()}], core_ids=[0])
    return r.results[0]["out_x"]


_COLUMNS = ("L0_xattn_bq", "L0_xattn_bk", "L1_ffn_conv_b", "L2_xattn_b")
_FLIP = ("L3_ffn_wg", "L3_ffn_w1", "L3_ffn_w3", "L3_ffn_w2", "L0_ffn_gate_w", "L0_ffn_Ws_g", "L0_ffn_Ws_u", "L0_ffn_Ws_d", "L0_ffn_Wg", "L0_ffn_Wu", "L0_ffn_Wd",
         "L0_xattn_Wq", "L0_xattn_Wk", "L0_xattn_Wv", "L0_xattn_Wo", "L1_xattn_Wk", "L1_xattn_Wv",
         "L1_ffn_w1", "L1_ffn_w2", "L2_xattn_W", "L2_ffn_w_up", "L2_ffn_w_down",
         "L3_xattn_w_q", "L3_xattn_w_k", "L3_xattn_w_v", "L3_xattn_w_o")
_NAMES = ("x", "ctx_1024", "mask_1x1xSxS2_ik0", "L0_xattn_bv", "L0_xattn_bo", "L1_xattn_Wq",
          "L1_xattn_bq", "L1_xattn_bk", "L1_xattn_bv", "L1_ffn_conv_w") + _COLUMNS + _FLIP
```
